# Optimizing a Trainium2 kernel written in Bass

```python
import numpy as np
import jax
import jax.numpy as jnp

def _softmax(x, axis=-1):
    return jax.nn.softmax(x, axis=axis)

def _gelu(x):
    return jax.nn.gelu(x, approximate=True)

def _silu(x):
    return jax.nn.silu(x)

def _sigmoid(x):
    return jax.nn.sigmoid(x)

def _layernorm(x, axis=-1, eps=1e-05):
    m = jnp.mean(x, axis=axis, keepdims=True)
    v = jnp.var(x, axis=axis, keepdims=True)
    return (x - m) / jnp.sqrt(v + eps)

def _scatter_add(tgt, idx, src, axis=0):
    return tgt.at[idx].add(src)

def _segment_sum(src, seg, n):
    return jax.ops.segment_sum(src, seg, n)
kernel_name = 'mk_xattn_seq_d2_seqx_r8_2cfe41'

def setup_inputs(seed: int=0):
    np.random.seed(seed)
    _w = jnp.asarray

    def _rec_inputs():
        import jax
        import jax.numpy as jnp
        _rk = jax.random.key(seed)
        x = -0.0005207 + 1.001 * jax.random.normal(jax.random.fold_in(_rk, 1), (4, 512, 128), jnp.float32)
        _lenS = 512 - jax.random.randint(jax.random.fold_in(_rk, 7), (4,), 0, max(1, 512 // 4) + 1, jnp.int32)
        _lenS2 = 154 - jax.random.randint(jax.random.fold_in(_rk, 8), (4,), 0, max(1, 154 // 4) + 1, jnp.int32)
        _ctx_1024P = jax.random.normal(jax.random.fold_in(_rk, 11), (4, 16, 128), jnp.float32)
        _ctx_1024c = jax.random.dirichlet(jax.random.fold_in(_rk, 511), 0.3 * jnp.ones((16,), jnp.float32), (4, 154))
        _ctx_1024t = jnp.einsum('bsk,bkd->bsd', _ctx_1024c, _ctx_1024P)
        _ctx_1024t = _ctx_1024t * jax.lax.rsqrt(jnp.mean(jnp.square(_ctx_1024t)) + 1e-12) * 0.953939
        ctx_1024 = 4.13588e-05 + 0.999923 * (_ctx_1024t + 0.3 * jax.random.normal(jax.random.fold_in(_rk, 611), (4, 154, 128), jnp.float32))
        _validS = jnp.arange(512)[None, :] < _lenS[:, None]
        _validS2 = jnp.arange(154)[None, :] < _lenS2[:, None]
        _causal = jnp.tril(jnp.ones((512, 512), dtype=bool))
        mask_BxS2_ik0 = jnp.where(jnp.broadcast_to(_validS2[:, :], (4, 154)), 0, 1).astype(jnp.int32)
        return (x, ctx_1024, mask_BxS2_ik0)
    x, ctx_1024, mask_BxS2_ik0 = _rec_inputs()

    def _L0_xattn_setup():
        import jax, jax.numpy as jnp
        import numpy as np
        EMBED_DIM = 128
        NUM_HEADS = 16
        HEAD_DIM = EMBED_DIM // NUM_HEADS
        LN_EPS = 1e-05
        key = jax.random.key(seed)
        ks = jax.random.split(key, 12)
        B, SQ, SKV, E = (2, 128, 512, EMBED_DIM)
        s = 1.0 / np.sqrt(E)
        return {'query': jax.random.normal(ks[0], (B, SQ, E), jnp.float32), 'key_value': jax.random.normal(ks[1], (B, SKV, E), jnp.float32), 'key_value_mask': jax.random.randint(ks[2], (B, SKV), 0, 2, jnp.int32), 'Wq': jax.random.normal(ks[3], (E, E), jnp.float32) * s, 'bq': jnp.zeros((E,), jnp.float32), 'Wk': jax.random.normal(ks[4], (E, E), jnp.float32) * s, 'bk': jnp.zeros((E,), jnp.float32), 'Wv': jax.random.normal(ks[5], (E, E), jnp.float32) * s, 'bv': jnp.zeros((E,), jnp.float32), 'Wo': jax.random.normal(ks[6], (E, E), jnp.float32) * s, 'bo': jnp.zeros((E,), jnp.float32), 'ln_gamma': jnp.ones((E,), jnp.float32), 'ln_beta': jnp.zeros((E,), jnp.float32)}
    _L0_xattn_all = _L0_xattn_setup()
    _L0_xattn_in = {k: v for k, v in _L0_xattn_all.items() if k in ('Wq', 'bq', 'Wk', 'bk', 'Wv', 'bv', 'Wo', 'bo', 'ln_gamma', 'ln_beta')}
    del _L0_xattn_all

    def _L1_xattn_setup():
        import jax, jax.numpy as jnp
        import numpy as np
        B, S, SE, D, H, FF, E, K = (2, 256, 256, 128, 16, 512, 8, 2)
        HD = D // H

        def _layernorm(x, g, b):
            m = x.mean(-1, keepdims=True)
            v = ((x - m) ** 2).mean(-1, keepdims=True)
            return (x - m) / jnp.sqrt(v + 1e-05) * g + b

        def _attn(q_in, k_in, v_in, wq, bq, wk, bk, wv, bv, wo, bo, causal):
            Bq, Sq, Dm = q_in.shape
            Sk = k_in.shape[1]
            Q = (q_in @ wq + bq).reshape(Bq, Sq, H, HD)
            Kp = (k_in @ wk + bk).reshape(Bq, Sk, H, HD)
            V = (v_in @ wv + bv).reshape(Bq, Sk, H, HD)
            scores = jnp.einsum('bqhd,bkhd->bhqk', Q, Kp) / jnp.sqrt(jnp.float32(HD))
            if causal:
                mask = jnp.tril(jnp.ones((Sq, Sk), bool))
                scores = jnp.where(mask, scores, -jnp.inf)
            a = jax.nn.softmax(scores, axis=-1)
            o = jnp.einsum('bhqk,bkhd->bqhd', a, V).reshape(Bq, Sq, Dm)
            return o @ wo + bo

        def _moe(x, rw, rb, w1, b1, w2, b2):
            T = x.shape[0] * x.shape[1]
            xf = x.reshape(T, D)
            router_weights = jax.nn.softmax(xf @ rw + rb, axis=-1)
            topw, topi = jax.lax.top_k(router_weights, K)
            topw = jax.nn.softmax(topw, axis=-1)
            combine = jnp.zeros((T, E), xf.dtype).at[jnp.arange(T)[:, None], topi].add(topw)
            h = jax.nn.gelu(jnp.einsum('td,edf->etf', xf, w1) + b1[:, None, :], approximate=False)
            eo = jnp.einsum('etf,efd->etd', h, w2) + b2[:, None, :]
            out = jnp.einsum('etd,te->td', eo, combine)
            return out.reshape(x.shape)
        key = jax.random.key(seed)
        ks = jax.random.split(key, 32)
        w = lambda k, shape: jax.random.normal(k, shape, jnp.float32) * 0.02
        inp = {'x': jax.random.normal(ks[0], (B, S, D), jnp.float32), 'encoder_output': jax.random.normal(ks[1], (B, SE, D), jnp.float32), 'sa_wq': w(ks[2], (D, D)), 'sa_bq': jnp.zeros((D,), jnp.float32), 'sa_wk': w(ks[3], (D, D)), 'sa_bk': jnp.zeros((D,), jnp.float32), 'sa_wv': w(ks[4], (D, D)), 'sa_bv': jnp.zeros((D,), jnp.float32), 'sa_wo': w(ks[5], (D, D)), 'sa_bo': jnp.zeros((D,), jnp.float32), 'ca_wq': w(ks[6], (D, D)), 'ca_bq': jnp.zeros((D,), jnp.float32), 'ca_wk': w(ks[7], (D, D)), 'ca_bk': jnp.zeros((D,), jnp.float32), 'ca_wv': w(ks[8], (D, D)), 'ca_bv': jnp.zeros((D,), jnp.float32), 'ca_wo': w(ks[9], (D, D)), 'ca_bo': jnp.zeros((D,), jnp.float32), 'ln1_g': jnp.ones((D,), jnp.float32), 'ln1_b': jnp.zeros((D,), jnp.float32), 'ln2_g': jnp.ones((D,), jnp.float32), 'ln2_b': jnp.zeros((D,), jnp.float32), 'ln3_g': jnp.ones((D,), jnp.float32), 'ln3_b': jnp.zeros((D,), jnp.float32), 'router_w': w(ks[10], (D, E)), 'router_b': jnp.zeros((E,), jnp.float32), 'e_w1': w(ks[11], (E, D, FF)), 'e_b1': jnp.zeros((E, FF), jnp.float32), 'e_w2': w(ks[12], (E, FF, D)), 'e_b2': jnp.zeros((E, D), jnp.float32)}
        return inp
    _L1_xattn_all = _L1_xattn_setup()
    _L1_xattn_in = {k: v for k, v in _L1_xattn_all.items() if k in ('sa_wq', 'sa_bq', 'sa_wk', 'sa_bk', 'sa_wv', 'sa_bv', 'sa_wo', 'sa_bo', 'ca_wq', 'ca_bq', 'ca_wk', 'ca_bk', 'ca_wv', 'ca_bv', 'ca_wo', 'ca_bo', 'ln1_g', 'ln1_b', 'ln2_g', 'ln2_b', 'ln3_g', 'ln3_b', 'router_w', 'router_b', 'e_w1', 'e_b1', 'e_w2', 'e_b2')}
    del _L1_xattn_all
    return {'x': x, 'ctx_1024': ctx_1024, 'mask_BxS2_ik0': mask_BxS2_ik0, 'L0_xattn_Wq': _L0_xattn_in['Wq'], 'L0_xattn_bq': _L0_xattn_in['bq'], 'L0_xattn_Wk': _L0_xattn_in['Wk'], 'L0_xattn_bk': _L0_xattn_in['bk'], 'L0_xattn_Wv': _L0_xattn_in['Wv'], 'L0_xattn_bv': _L0_xattn_in['bv'], 'L0_xattn_Wo': _L0_xattn_in['Wo'], 'L0_xattn_bo': _L0_xattn_in['bo'], 'L0_xattn_ln_gamma': _L0_xattn_in['ln_gamma'], 'L0_xattn_ln_beta': _L0_xattn_in['ln_beta'], 'L1_xattn_sa_wq': _L1_xattn_in['sa_wq'], 'L1_xattn_sa_bq': _L1_xattn_in['sa_bq'], 'L1_xattn_sa_wk': _L1_xattn_in['sa_wk'], 'L1_xattn_sa_bk': _L1_xattn_in['sa_bk'], 'L1_xattn_sa_wv': _L1_xattn_in['sa_wv'], 'L1_xattn_sa_bv': _L1_xattn_in['sa_bv'], 'L1_xattn_sa_wo': _L1_xattn_in['sa_wo'], 'L1_xattn_sa_bo': _L1_xattn_in['sa_bo'], 'L1_xattn_ca_wq': _L1_xattn_in['ca_wq'], 'L1_xattn_ca_bq': _L1_xattn_in['ca_bq'], 'L1_xattn_ca_wk': _L1_xattn_in['ca_wk'], 'L1_xattn_ca_bk': _L1_xattn_in['ca_bk'], 'L1_xattn_ca_wv': _L1_xattn_in['ca_wv'], 'L1_xattn_ca_bv': _L1_xattn_in['ca_bv'], 'L1_xattn_ca_wo': _L1_xattn_in['ca_wo'], 'L1_xattn_ca_bo': _L1_xattn_in['ca_bo'], 'L1_xattn_ln1_g': _L1_xattn_in['ln1_g'], 'L1_xattn_ln1_b': _L1_xattn_in['ln1_b'], 'L1_xattn_ln2_g': _L1_xattn_in['ln2_g'], 'L1_xattn_ln2_b': _L1_xattn_in['ln2_b'], 'L1_xattn_ln3_g': _L1_xattn_in['ln3_g'], 'L1_xattn_ln3_b': _L1_xattn_in['ln3_b'], 'L1_xattn_router_w': _L1_xattn_in['router_w'], 'L1_xattn_router_b': _L1_xattn_in['router_b'], 'L1_xattn_e_w1': _L1_xattn_in['e_w1'], 'L1_xattn_e_b1': _L1_xattn_in['e_b1'], 'L1_xattn_e_w2': _L1_xattn_in['e_w2'], 'L1_xattn_e_b2': _L1_xattn_in['e_b2']}

def reference(x, ctx_1024, mask_BxS2_ik0, L0_xattn_Wq, L0_xattn_bq, L0_xattn_Wk, L0_xattn_bk, L0_xattn_Wv, L0_xattn_bv, L0_xattn_Wo, L0_xattn_bo, L0_xattn_ln_gamma, L0_xattn_ln_beta, L1_xattn_sa_wq, L1_xattn_sa_bq, L1_xattn_sa_wk, L1_xattn_sa_bk, L1_xattn_sa_wv, L1_xattn_sa_bv, L1_xattn_sa_wo, L1_xattn_sa_bo, L1_xattn_ca_wq, L1_xattn_ca_bq, L1_xattn_ca_wk, L1_xattn_ca_bk, L1_xattn_ca_wv, L1_xattn_ca_bv, L1_xattn_ca_wo, L1_xattn_ca_bo, L1_xattn_ln1_g, L1_xattn_ln1_b, L1_xattn_ln2_g, L1_xattn_ln2_b, L1_xattn_ln3_g, L1_xattn_ln3_b, L1_xattn_router_w, L1_xattn_router_b, L1_xattn_e_w1, L1_xattn_e_b1, L1_xattn_e_w2, L1_xattn_e_b2):
    import jax
    import jax.numpy as jnp

    def _L0_xattn_ref(query, key_value, key_value_mask, Wq, bq, Wk, bk, Wv, bv, Wo, bo, ln_gamma, ln_beta):
        import jax, jax.numpy as jnp
        import numpy as np
        EMBED_DIM = 128
        NUM_HEADS = 16
        HEAD_DIM = EMBED_DIM // NUM_HEADS
        LN_EPS = 1e-05
        B, SQ, E = query.shape
        SKV = key_value.shape[1]
        H, D = (NUM_HEADS, HEAD_DIM)
        q = (query @ Wq.T + bq).reshape(B, SQ, H, D).transpose(0, 2, 1, 3)
        k = (key_value @ Wk.T + bk).reshape(B, SKV, H, D).transpose(0, 2, 1, 3)
        v = (key_value @ Wv.T + bv).reshape(B, SKV, H, D).transpose(0, 2, 1, 3)
        scale = jnp.sqrt(jnp.asarray(D, q.dtype))
        scores = jnp.einsum('bhqd,bhkd->bhqk', q, k) / scale
        mask = (key_value_mask != 0)[:, None, None, :]
        scores = jnp.where(mask, scores, jnp.asarray(-jnp.inf, scores.dtype))
        attn = jax.nn.softmax(scores, axis=-1)
        out = jnp.einsum('bhqk,bhkd->bhqd', attn, v)
        out = out.transpose(0, 2, 1, 3).reshape(B, SQ, E)
        out = out @ Wo.T + bo
        x = query + out
        mu = jnp.mean(x, axis=-1, keepdims=True)
        var = jnp.mean(jnp.square(x - mu), axis=-1, keepdims=True)
        return (x - mu) * jax.lax.rsqrt(var + LN_EPS) * ln_gamma + ln_beta

    def _L1_xattn_ref(x, encoder_output, sa_wq, sa_bq, sa_wk, sa_bk, sa_wv, sa_bv, sa_wo, sa_bo, ca_wq, ca_bq, ca_wk, ca_bk, ca_wv, ca_bv, ca_wo, ca_bo, ln1_g, ln1_b, ln2_g, ln2_b, ln3_g, ln3_b, router_w, router_b, e_w1, e_b1, e_w2, e_b2):
        import jax, jax.numpy as jnp
        import numpy as np
        B, S, SE, D, H, FF, E, K = (2, 256, 256, 128, 16, 512, 8, 2)
        HD = D // H

        def _layernorm(x, g, b):
            m = x.mean(-1, keepdims=True)
            v = ((x - m) ** 2).mean(-1, keepdims=True)
            return (x - m) / jnp.sqrt(v + 1e-05) * g + b

        def _attn(q_in, k_in, v_in, wq, bq, wk, bk, wv, bv, wo, bo, causal):
            Bq, Sq, Dm = q_in.shape
            Sk = k_in.shape[1]
            Q = (q_in @ wq + bq).reshape(Bq, Sq, H, HD)
            Kp = (k_in @ wk + bk).reshape(Bq, Sk, H, HD)
            V = (v_in @ wv + bv).reshape(Bq, Sk, H, HD)
            scores = jnp.einsum('bqhd,bkhd->bhqk', Q, Kp) / jnp.sqrt(jnp.float32(HD))
            if causal:
                mask = jnp.tril(jnp.ones((Sq, Sk), bool))
                scores = jnp.where(mask, scores, -jnp.inf)
            a = jax.nn.softmax(scores, axis=-1)
            o = jnp.einsum('bhqk,bkhd->bqhd', a, V).reshape(Bq, Sq, Dm)
            return o @ wo + bo

        def _moe(x, rw, rb, w1, b1, w2, b2):
            T = x.shape[0] * x.shape[1]
            xf = x.reshape(T, D)
            router_weights = jax.nn.softmax(xf @ rw + rb, axis=-1)
            topw, topi = jax.lax.top_k(router_weights, K)
            topw = jax.nn.softmax(topw, axis=-1)
            combine = jnp.zeros((T, E), xf.dtype).at[jnp.arange(T)[:, None], topi].add(topw)
            h = jax.nn.gelu(jnp.einsum('td,edf->etf', xf, w1) + b1[:, None, :], approximate=False)
            eo = jnp.einsum('etf,efd->etd', h, w2) + b2[:, None, :]
            out = jnp.einsum('etd,te->td', eo, combine)
            return out.reshape(x.shape)
        x = _layernorm(x + _attn(x, x, x, sa_wq, sa_bq, sa_wk, sa_bk, sa_wv, sa_bv, sa_wo, sa_bo, True), ln1_g, ln1_b)
        x = _layernorm(x + _attn(x, encoder_output, encoder_output, ca_wq, ca_bq, ca_wk, ca_bk, ca_wv, ca_bv, ca_wo, ca_bo, False), ln2_g, ln2_b)
        x = _layernorm(x + _moe(x, router_w, router_b, e_w1, e_b1, e_w2, e_b2), ln3_g, ln3_b)
        return x
    x = _L0_xattn_ref(x, ctx_1024, mask_BxS2_ik0, L0_xattn_Wq, L0_xattn_bq, L0_xattn_Wk, L0_xattn_bk, L0_xattn_Wv, L0_xattn_bv, L0_xattn_Wo, L0_xattn_bo, L0_xattn_ln_gamma, L0_xattn_ln_beta)
    x = _L1_xattn_ref(x, ctx_1024, L1_xattn_sa_wq, L1_xattn_sa_bq, L1_xattn_sa_wk, L1_xattn_sa_bk, L1_xattn_sa_wv, L1_xattn_sa_bv, L1_xattn_sa_wo, L1_xattn_sa_bo, L1_xattn_ca_wq, L1_xattn_ca_bq, L1_xattn_ca_wk, L1_xattn_ca_bk, L1_xattn_ca_wv, L1_xattn_ca_bv, L1_xattn_ca_wo, L1_xattn_ca_bo, L1_xattn_ln1_g, L1_xattn_ln1_b, L1_xattn_ln2_g, L1_xattn_ln2_b, L1_xattn_ln3_g, L1_xattn_ln3_b, L1_xattn_router_w, L1_xattn_router_b, L1_xattn_e_w1, L1_xattn_e_b1, L1_xattn_e_w2, L1_xattn_e_b2)
    return x

_drawn_inputs = setup_inputs


def setup_inputs(seed=0):
    import zlib

    import numpy as np

    out = dict(_drawn_inputs(seed))
    spreads = {'L0_xattn_bq': (0.0, 0.1),
     'L0_xattn_bk': (0.0, 2.0),
     'L0_xattn_bv': (0.0, 0.1),
     'L0_xattn_bo': (0.0, 0.1),
     'L0_xattn_ln_gamma': (1.0, 0.2),
     'L0_xattn_ln_beta': (0.0, 0.1),
     'L1_xattn_sa_bq': (0.0, 2.0),
     'L1_xattn_sa_bk': (0.0, 2.0),
     'L1_xattn_sa_bv': (0.0, 0.408),
     'L1_xattn_sa_bo': (0.0, 0.1),
     'L1_xattn_ca_bq': (0.0, 2.0),
     'L1_xattn_ca_bk': (0.0, 2.0),
     'L1_xattn_ca_bv': (0.0, 0.299),
     'L1_xattn_ca_bo': (0.0, 0.1),
     'L1_xattn_ln1_g': (1.0, 0.2),
     'L1_xattn_ln1_b': (0.0, 0.1),
     'L1_xattn_ln2_g': (1.0, 0.2),
     'L1_xattn_ln2_b': (0.0, 0.1),
     'L1_xattn_ln3_g': (1.0, 0.2),
     'L1_xattn_ln3_b': (0.0, 0.1),
     'L1_xattn_router_b': (0.0, 0.1),
     'L1_xattn_e_b1': (0.0, 0.497),
     'L1_xattn_e_b2': (0.0, 0.1)}
    factors = {'L1_xattn_sa_wq': 8.0, 'L1_xattn_sa_wk': 8.0, 'L1_xattn_ca_wq': 8.0, 'L1_xattn_ca_wk': 8.0}
    for name, (base, spread) in spreads.items():
        noise = np.random.default_rng([zlib.crc32(name.encode()), seed]).standard_normal(out[name].shape)
        drawn = base * np.exp(spread * noise) if base else spread * noise
        out[name] = jnp.asarray(drawn.astype(out[name].dtype))
    for name, factor in factors.items():
        out[name] = (out[name] * factor).astype(out[name].dtype)
    return out
```

```python
import numpy as np
from contextlib import ExitStack

import concourse.bass as bass
from concourse import mybir

F32 = mybir.dt.float32
F32R = mybir.dt.float32r
BF16 = mybir.dt.bfloat16
I32 = mybir.dt.int32
U32 = mybir.dt.uint32
ALU = mybir.AluOpType
ACT = mybir.ActivationFunctionType
AX = mybir.AxisListType

P = 128
B = 4
S = 512
QC = S // P
CTX = 154
H, HD = 16, 8
G = H // 4
E, FF = 8, 512
FC = FF // P
T = B * QC
TAIL = CTX - P
PAD = 32
KCTX = P + PAD
PIECES = 3
STACK = PIECES * PIECES * HD
MASK_ROW = STACK
MAX_ROW = STACK + 1
ROWS_A = STACK + 1
ROWS_B = STACK + 1 + PIECES
LOW = -1.0e38
EPS = 1e-5
SCALE = float(HD) ** -0.5

LAYERS = ("L0", "SELF", "CROSS")
NL = len(LAYERS)
CHAINS = 2
UNITS = NL * CHAINS
BESIDE = ((0, 5), (5, 10), (10, 15), (15, 16))


class Count:

    def __init__(self, sem, per_layer):
        self.sem = sem
        self.before = [0]
        for u in range(UNITS):
            self.before.append(self.before[-1] + per_layer[u // CHAINS])
        self.total = self.before[-1]

    def index(self, u, k):
        return self.before[u] + k

    def wait(self, eng, u, k):
        eng.wait_ge(self.sem, (self.before[u] + k))


def a_items(layer):
    if layer == 1:
        return [[(0, 0, P), (1, P, 2 * P)], [(2, 0, 3 * P)], [(3, 0, 4 * P)]]
    return [[(0, 0, KCTX), (1, 256, KCTX)], [(2, 0, KCTX), (3, 256, KCTX)]]


def b_items():
    return [([(0, 0)], 4 * P), ([(1, 0), (3, 3 * P)], 4 * P), ([(2, 0)], 2 * P)]


P_AT = {0: 0, 1: 4 * P, 3: 7 * P, 2: 8 * P}
P_WIDE = 10 * P


def attention(nc, ins, xmid):
    ctx = ExitStack()
    with ctx:
        def sb(name, shape, dt=F32):
            return ctx.enter_context(nc.sbuf_tensor(name, shape, dt))

        def sem(name):
            return ctx.enter_context(nc.semaphore(name))

        def two(name, shape, dt=F32):
            return [sb(f"{name}{c}", shape, dt) for c in range(CHAINS)]

        ident = sb("ident", [P, P])
        ident16 = sb("ident16", [P, P], BF16)
        causal_q = sb("causal_q", [P, P], BF16)
        causal_k = sb("causal_k", [P, P], BF16)

        w = sb("w", [P, 4 * NL, P])
        cols = sb("cols", [P, 4 * NL])
        bqs = sb("bqs", [P, NL])
        rows = sb("rows", [P, 4 * NL, P])
        mask_int = sb("mask_int", [1, B * CTX], I32)
        mask_rows = sb("mask_rows", [1, B + 1, KCTX], BF16)
        zero_row = sb("zero_row", [1, S], BF16)
        minus_half = sb("minus_half", [P, QC])

        x_tok = two("x_tok", [P, QC, P])
        x_bo = two("x_bo", [P, QC, P])
        x_t = two("x_t", [P, S])
        ctx_tok = two("ctx_tok", [P, 2, P])
        ctx_t = two("ctx_t", [P, P + 4 * PAD])
        qk = two("qk", [P, 2, S])
        rest = sb("rest", [P, 2, S])
        pieces = two("pieces", [P, 2, PIECES, S], BF16)
        q_stack = two("q_stack", [P, H, S], BF16)
        k_stack = two("k_stack", [P, H, S], BF16)
        v_aug = two("v_aug", [P, QC + 1, H, PAD])
        neg_max = two("neg_max", [P, QC, H])
        max_rest = sb("max_rest", [P, QC, H])
        max_pieces = two("max_pieces", [P, QC, PIECES, H], BF16)
        max_t = two("max_t", [PIECES * H, S], BF16)

        probs = sb("probs", [P, 8, P_WIDE])
        o_t = sb("o_t", [P, G, S])
        recip = sb("recip", [P, QC, 4, 1])
        o_tok = sb("o_tok", [P, QC, P])
        o_tt = sb("o_tt", [P, S])
        y = sb("y", [P, QC, P])
        w_raw = y
        z = sb("z", [P, QC, P])
        stats = sb("stats", [P, QC, 2, 3])
        sums = sb("sums", [P, QC, 2])
        gap = sb("gap", [P, QC])
        gap2 = sb("gap2", [P, QC])
        within = sb("within", [P, QC])
        mean = sb("mean", [P, QC])
        var = sb("var", [P, QC])
        rstd = sb("rstd", [P, QC])

        bank = [ctx.enter_context(nc.psum_tensor(f"bank{i}", [P, S], F32)) for i in range(8)]
        A_BANKS, B_BANKS, AV_BANK, MISC = (0, 1), (2, 3, 4), 5, (6, 7)
        misc = {"T0": 6, "T1": 7, "T2": 6, "max": 7, "T3": 6, "oT": 7, "Y": 6, "xT": 7,
                "x": 6, "ctx": 7, "q": 6, "k": 7, "v": 6}
        job = {n: bank[i] for n, i in misc.items()}

        q_dram = [nc.dram_tensor(f"q_pieces{c}", (H, PIECES, HD, S), BF16, kind="Internal").ap() for c in range(CHAINS)]
        k_dram = [nc.dram_tensor(f"k_pieces{c}", (H, PIECES, HD, S), BF16, kind="Internal").ap() for c in range(CHAINS)]

        s_const = sem("s_const")
        s_made = sem("s_made")
        s_low = sem("s_low")
        s_wt = sem("s_wt")
        s_w = sem("s_w")
        s_bq = sem("s_bq")
        first_loop_sem = sem("a_ready")
        one = (1, 1, 1)
        n_a = tuple(H * len(a_items(l)) for l in range(NL))
        n_b = tuple(H * len(b_items()) if l == 1 else H + G for l in range(NL))
        first = (1, 0, 0)
        a_ready = Count(first_loop_sem, n_a)
        a_taken = Count(sem("a_taken"), n_a)
        b_ready = Count(sem("b_ready"), n_b)
        p_ready = Count(sem("p_ready"), n_b)
        av_done = Count(sem("av_done"), (G,) * NL)
        o_kept = Count(sem("o_kept"), (G,) * NL)
        t_ready = Count(sem("t_ready"), (G,) * NL)
        t_recip = Count(sem("t_recip"), (G,) * NL)
        t_taken = Count(sem("t_taken"), (G,) * NL)
        m_step = Count(sem("m_step"), (4,) * NL)
        mt_ready = Count(sem("mt_ready"), one)
        mt_kept = Count(sem("mt_kept"), one)
        ot_ready = Count(sem("ot_ready"), one)
        ot_kept = Count(sem("ot_kept"), one)
        y_ready = Count(sem("y_ready"), one)
        y_step = Count(sem("y_step"), (1,) * NL)
        bn_step = Count(sem("bn_step"), (QC + 5,) * NL)
        var_eps = Count(sem("var_eps"), one)
        rstd_ready = Count(sem("rstd_ready"), one)
        z_ready = Count(sem("z_ready"), (QC,) * NL)
        xt_ready = Count(sem("xt_ready"), one)
        xt_kept = Count(sem("xt_kept"), one)
        x_scaled = Count(sem("x_scaled"), one)
        x_new = Count(sem("x_new"), one)
        xbo_ready = Count(sem("xbo_ready"), one)
        xl_ready = Count(sem("xl_ready"), (2, 0, 0))
        xl_kept = Count(sem("xl_kept"), (2, 0, 0))
        tail_kept = Count(sem("tail_kept"), (1, 0, 0))
        qkv_ready = Count(sem("qkv_ready"), (3,) * NL)
        qk_kept = Count(sem("qk_kept"), (4,) * NL)
        rest_step = Count(sem("rest_step"), (6,) * NL)
        v_kept = Count(sem("v_kept"), one)
        v_part = Count(sem("v_part"), (4, 0, 4))
        loaded = [sem(f"loaded{c}") for c in range(CHAINS)]
        written = [sem(f"written{c}") for c in range(CHAINS)]
        stacked = [sem(f"stacked{c}") for c in range(CHAINS)]
        max_in = [sem(f"max_in{c}") for c in range(CHAINS)]
        stored = [sem(f"stored{c}") for c in range(CHAINS)]
        mask_in = [sem(f"mask_in{c}") for c in range(CHAINS)]
        row_in = [sem(f"row_in{c}") for c in range(CHAINS)]
        last_loop_sem = row_in[-1]
        N_LOAD, N_WRITE, N_STACK = 3, 2 * PIECES, PIECES * PIECES + PIECES

        def chain(u):
            return u % CHAINS

        def layer(u):
            return u // CHAINS

        def dma_wait(eng, sems, u, n):
            eng.wait_ge(sems[chain(u)], 16 * n * (layer(u) + 1))

        n_const = 4 * NL + 4 * NL + 4 * NL + 1


        with nc.Block() as block:
            @block.sync
            def _(sp):
                names = [("L0_xattn_", ("Wq", "Wk", "Wv", "Wo")), ("L1_xattn_sa_", ("wq", "wk", "wv", "wo")),
                         ("L1_xattn_ca_", ("wq", "wk", "wv", "wo"))]
                norms = [("L0_xattn_ln_gamma", "L0_xattn_ln_beta"), ("L1_xattn_ln1_g", "L1_xattn_ln1_b"),
                         ("L1_xattn_ln2_g", "L1_xattn_ln2_b")]
                for l, (head, ws) in enumerate(names[:NL]):
                    for i, n in enumerate(ws):
                        dst = w_raw[:, i, :] if l == 0 else w[:, 4 * l + i, :]
                        sp.dma_start(dst, ins[head + n]).then_inc(s_const, 16)
                    vectors = [ins[head + "bq"], ins[head + "bk"], ins[norms[l][0]], ins[norms[l][1]]]
                    for i, v in enumerate(vectors):
                        sp.dma_start(cols[:, 4 * l + i:4 * l + i + 1], v.rearrange("(p o) -> p o", o=1)).then_inc(s_const, 16)
                    vectors = [ins[head + "bv"], ins[head + "bo"], ins[norms[l][0]], ins[norms[l][1]]]
                    for i, v in enumerate(vectors):
                        sp.dma_start(rows[:, 4 * l + i, :], v.rearrange("(o d) -> o d", o=1).to_broadcast([P, P])).then_inc(s_const, 16)
                sp.dma_start(mask_int[:, :], ins["mask_BxS2_ik0"].rearrange("(o b) s -> o (b s)", o=1)).then_inc(s_const, 16)


            @block.gpsimd
            def _(pool):
                pool.memset(ident[:, :], 0.0).then_inc(s_made, 1)
                pool.memset(minus_half[:, :], -0.5).then_inc(s_made, 1)
                pool.memset(causal_q[:, :], 0.0).then_inc(s_made, 1)
                pool.memset(causal_k[:, :], 0.0).then_inc(s_made, 1)
                for c in range(CHAINS):
                    pool.memset(k_stack[c][:, :, :], 0.0).then_inc(s_made, 1)
                    pool.memset(ctx_t[c][:, :], 0.0).then_inc(s_made, 1)
                    pool.memset(v_aug[c][:, :, :, :], 0.0).then_inc(s_made, 1)
                pool.wait_ge(s_made, 10)
                pool.affine_select(out=ident[:, :], in_=ident[:, :], compare_op=ALU.not_equal, fill=1.0, base=0,
                                   pattern=[[-1, P]], channel_multiplier=1).then_inc(s_made, 1)
                pool.wait_ge(s_made, 11)
                pool.affine_select(out=causal_q[:, :], in_=causal_q[:, :], compare_op=ALU.is_ge, fill=LOW, base=0,
                                   pattern=[[-1, P]], channel_multiplier=1).then_inc(s_made, 1)
                pool.affine_select(out=causal_k[:, :], in_=causal_k[:, :], compare_op=ALU.is_ge, fill=LOW, base=0,
                                   pattern=[[1, P]], channel_multiplier=-1).then_inc(s_made, 1)
                pool.wait_ge(s_made, 13)
                pool.memset(zero_row[:, :], 0.0).then_inc(s_made, 1)
                pool.wait_ge(s_made, 14)
                for c in range(CHAINS):
                    pool.memset(k_stack[c][64:96, :, :], 1.0).then_inc(s_made, 1)

            @block.scalar
            def _(act):
                act.wait_ge(s_const, 16 * n_const)
                for l in range(NL):
                    act.mul(bqs[:, l:l + 1], cols[:, 4 * l:4 * l + 1], SCALE).then_inc(s_bq, 1)
                act.wait_ge(s_wt, 1)
                act.copy(w[:, 0:4, :], bank[0][:, :].rearrange("p (i d) -> p i d", i=4)).then_inc(s_w, 1)
            @block.vector
            def _(dve):
                dve.wait_ge(s_made, 16)
                dve.tensor_copy(ident16[:, :], ident[:, :]).then_inc(s_low, 1)
                for c in range(CHAINS):
                    dve.memset(q_stack[c][64:96, :, :], 1.0).then_inc(s_low, 1)
                dve.memset(mask_rows[:, :, :], 0.0).then_inc(s_low, 1)
                dve.wait_ge(s_low, 4)
                dve.memset(mask_rows[:, :, CTX:KCTX], LOW)
                dve.wait_ge(s_const, 16 * n_const)
                dve.tensor_scalar(mask_rows[:, 0:B, 0:CTX], mask_int[:, :].rearrange("p (b s) -> p b s", b=B), 0.0, LOW,
                                  ALU.is_equal, ALU.mult).then_inc(s_low, 1)
                for c in range(CHAINS):
                    dve.memset(v_aug[c][:, 0:QC, :, HD:HD + 1], 1.0)
                    for j in range(4):
                        dve.memset(v_aug[c][PAD * j:PAD * (j + 1), QC, j:H:4, HD:HD + 1], 1.0)

            @block.tensor
            def _(pe):
                pe.wait_ge(s_made, 16)
                pe.wait_ge(s_low, 1)
                pe.wait_ge(s_const, 16 * n_const)
                for i in range(4):
                    last = pe.transpose(bank[0][:, i * P:(i + 1) * P], w_raw[:, i, :], ident[:, :])
                last.then_inc(s_wt, 1)
                pe.wait_ge(s_w, 1)

        with nc.Fori(0, B // CHAINS) as it:
            with nc.Block() as block:
                @block.sync
                def _(sp):
                    def load(u):
                        c = chain(u)
                        b = it * CHAINS + c
                        x_b = ins["x"][bass.ds(b, 1), :, :].rearrange("o (t p) d -> p (o t) d", p=P)
                        sp.dma_start(x_tok[c][:, :, :], x_b).then_inc(loaded[c], 16)
                        c_b = ins["ctx_1024"][bass.ds(b, 1), :, :].rearrange("o s d -> (o s) d")
                        sp.dma_start(ctx_tok[c][:, 0, :], c_b[0:P, :]).then_inc(loaded[c], 16)
                        sp.dma_start(ctx_tok[c][0:TAIL, 1, :], c_b[P:CTX, :]).then_inc(loaded[c], 16)

                    def mask_row(u):
                        c = chain(u)
                        src = mask_rows[:, bass.ds(it * CHAINS + c, 1), :].rearrange("p o n -> p (o n)")
                        src = src.rearrange("p (o n) -> p o n", o=1).to_broadcast([1, H, KCTX])
                        sp.dma_start(k_stack[c][MASK_ROW:MASK_ROW + 1, :, 0:KCTX], src).then_inc(mask_in[c], 16)

                    def store(u):
                        c = chain(u)
                        x_new.wait(sp, u, 1)
                        b = it * CHAINS + c
                        sp.dma_start(xmid[bass.ds(b, 1), :, :].rearrange("o (t p) d -> p (o t) d", p=P),
                                     x_tok[c][:, :, :]).then_inc(stored[c], 16)

                    def stack(u):
                        c, l = chain(u), layer(u)
                        n_k = S if l == 1 else KCTX
                        qk_kept.wait(sp, u, 4)
                        rest_step.wait(sp, u, 6)
                        for t, (dram, n) in enumerate(((q_dram[c], S), (k_dram[c], n_k))):
                            for i in range(PIECES):
                                sp.dma_start(dram[:, i, :, 0:n], pieces[c][:, t, i, 0:n]).then_inc(written[c], 16)
                        dma_wait(sp, written, u, N_WRITE)
                        for i in range(PIECES):
                            at = PIECES * HD * i
                            for j in range(PIECES):
                                sp.dma_start(q_stack[c][at + HD * j:at + HD * (j + 1), :, :],
                                             q_dram[c][:, i, :, :].rearrange("h e n -> e h n")).then_inc(stacked[c], 16)
                            sp.dma_start(k_stack[c][at:at + PIECES * HD, :, 0:n_k],
                                         k_dram[c][:, :, :, 0:n_k].rearrange("h j e n -> (j e) h n")).then_inc(stacked[c], 16)
                        if l == 0:
                            return
                        src = zero_row[:, :] if l == 1 else mask_rows[:, B, :]
                        n_m = S if l == 1 else KCTX
                        src = src.rearrange("p (o n) -> p o n", o=1).to_broadcast([1, H, n_m])
                        sp.dma_start(k_stack[c][MASK_ROW:MASK_ROW + 1, :, 0:n_m], src).then_inc(row_in[c], 16)

                    def max_rows(u):
                        c = chain(u)
                        mt_kept.wait(sp, u, 1)
                        for i in range(PIECES):
                            sp.dma_start(q_stack[c][MAX_ROW + i:MAX_ROW + i + 1, :, :],
                                         max_t[c][H * i:H * (i + 1), :]).then_inc(max_in[c], 16)

                    for u in range(CHAINS):
                        load(u)
                        mask_row(u)
                    stack(0)
                    for k in range(UNITS + 1):
                        if k < UNITS:
                            max_rows(k)
                        if k + 1 < UNITS:
                            stack(k + 1)
                    for u in range(UNITS - CHAINS, UNITS):
                        store(u)
                    for c in range(CHAINS):
                        sp.wait_ge(stored[c], 16)

                @block.gpsimd
                def _(pool):
                    def next_bo(u):
                        c, l = chain(u), layer(u)
                        if l == 0:
                            pool.wait_ge(loaded[c], 16 * N_LOAD)
                        else:
                            x_new.wait(pool, u - CHAINS, 1)
                        bo = rows[:, 4 * l + 1:4 * l + 2, :].to_broadcast([P, QC, P])
                        pool.tensor_tensor(x_bo[c][:, :, :], x_tok[c][:, :, :], bo, ALU.add).then_inc(xbo_ready.sem, 1)

                    def norm(u):
                        c, l = chain(u), layer(u)
                        var_eps.wait(pool, u, 1)
                        pool.tensor_tensor(rstd[:, :], var[:, :], minus_half[:, :], ALU.pow).then_inc(rstd_ready.sem, 1)
                        z_ready.wait(pool, u, QC)
                        gamma = rows[:, 4 * l + 2:4 * l + 3, :].to_broadcast([P, QC, P])
                        beta = rows[:, 4 * l + 3:4 * l + 4, :].to_broadcast([P, QC, P])
                        pool.tensor_tensor(x_tok[c][:, :, :], z[:, :, :], gamma, ALU.mult).then_inc(x_scaled.sem, 1)
                        x_scaled.wait(pool, u, 1)
                        pool.tensor_tensor(x_tok[c][:, :, :], x_tok[c][:, :, :], beta, ALU.add).then_inc(x_new.sem, 1)

                    next_bo(0)
                    next_bo(1)
                    for u in range(UNITS):
                        norm(u)
                        if u + CHAINS < UNITS:
                            next_bo(u + CHAINS)

                @block.scalar
                def _(act):
                    def inputs(u):
                        c = chain(u)
                        xl_ready.wait(act, u, 1)
                        act.copy(x_t[c][:, :], job["x"][:, :]).then_inc(xl_kept.sem, 1)
                        xl_ready.wait(act, u, 2)
                        act.copy(ctx_t[c][:, 0:P], job["ctx"][:, 0:P]).then_inc(xl_kept.sem, 1)
                        tail = job["ctx"][:, P:CTX].rearrange("p (o n) -> p o n", o=1).to_broadcast([P, 4, TAIL])
                        act.copy(ctx_t[c][:, P:P + 4 * PAD].rearrange("p (j n) -> p j n", j=4)[:, :, 0:TAIL], tail)\
                           .then_inc(tail_kept.sem, 1)

                    def project(u):
                        c, l = chain(u), layer(u)
                        n_k = S if l == 1 else KCTX
                        for t, (name, n, bias, scale) in enumerate((("q", S, bqs[:, l:l + 1], SCALE),
                                                                    ("k", n_k, cols[:, 4 * l + 1:4 * l + 2], 1.0))):
                            qkv_ready.wait(act, u, t + 1)
                            act.activation(qk[c][:, t, 0:n], job[name][:, 0:n], ACT.Identity, bias=bias,
                                           scale=scale).then_inc(qk_kept.sem, 1)
                            act.activation(pieces[c][:, t, 0, 0:n], job[name][:, 0:n], ACT.Identity, bias=bias,
                                           scale=scale).then_inc(qk_kept.sem, 1)

                    def exps(u, g, h, i, n, at):
                        idx = b_ready.index(u, i)
                        b_ready.wait(act, u, i + 1)
                        if u * G + g >= 2:
                            act.wait_ge(av_done.sem, (u * G + g - 1))
                        act.activation(probs[:, h % 8, at:at + n], bank[B_BANKS[idx % 3]][:, 0:n], ACT.Exp).then_inc(p_ready.sem, 1)

                    def group_exps(u, g):
                        i = g * n_b[layer(u)] // G
                        for h in range(4 * g, 4 * g + 4):
                            if layer(u) == 1:
                                for at, n in ((0, 4 * P), (4 * P, 4 * P), (8 * P, 2 * P)):
                                    exps(u, g, h, i, n, at)
                                    i += 1
                            else:
                                exps(u, g, h, i, S, 0)
                                i += 1
                        if layer(u) != 1:
                            exps(u, g, 4 * g, i, S, S)

                    def keep_o(u, g):
                        av_done.wait(act, u, g + 1)
                        if u * G + g >= G:
                            t_ready.wait(act, u - 1, g + 1)
                        act.copy(o_t[:, g, :], bank[AV_BANK][:, :]).then_inc(o_kept.sem, 1)

                    def tail(u):
                        c, l = chain(u), layer(u)
                        ot_ready.wait(act, u, 1)
                        act.copy(o_tt[:, :], job["oT"][:, :]).then_inc(ot_kept.sem, 1)
                        xt_ready.wait(act, u, 1)
                        act.activation(x_t[c][:, :], job["xT"][:, :], ACT.Identity, bias=cols[:, 4 * l + 3:4 * l + 4],
                                       scale=cols[:, 4 * l + 2:4 * l + 3]).then_inc(xt_kept.sem, 1)

                    inputs(0)
                    project(0)
                    for k in range(UNITS + 1):
                        if k >= 1:
                            for g in range(G):
                                group_exps(k - 1, g)
                                if g >= 1:
                                    keep_o(k - 1, g - 1)
                            keep_o(k - 1, G - 1)
                            tail(k - 1)
                        if k + 1 < UNITS:
                            if k + 1 < CHAINS:
                                inputs(k + 1)
                            project(k + 1)

                @block.vector
                def _(dve):
                    def cut(u):
                        c, l = chain(u), layer(u)
                        n_k = S if l == 1 else KCTX
                        for t, n in ((0, S), (1, n_k)):
                            qk_kept.wait(dve, u, 2 * t + 2)
                            dve.tensor_tensor(rest[:, t, 0:n], qk[c][:, t, 0:n], pieces[c][:, t, 0, 0:n], ALU.subtract)\
                               .then_inc(rest_step.sem, 1)
                            rest_step.wait(dve, u, 3 * t + 1)
                            dve.tensor_copy(pieces[c][:, t, 1, 0:n], rest[:, t, 0:n]).then_inc(rest_step.sem, 1)
                            rest_step.wait(dve, u, 3 * t + 2)
                            dve.tensor_tensor(pieces[c][:, t, 2, 0:n], rest[:, t, 0:n], pieces[c][:, t, 1, 0:n], ALU.subtract)\
                               .then_inc(rest_step.sem, 1)

                    def keep_v(u):
                        c, l = chain(u), layer(u)
                        qkv_ready.wait(dve, u, 3)
                        n = QC if l == 1 else 1
                        v = job["v"][:, :].rearrange("p (t h e) -> p t h e", t=QC, h=H)
                        bv = rows[:, 4 * l, :].rearrange("p (h e) -> p h e", h=H)
                        if l != 1:
                            for j in range(4):
                                r = slice(PAD * j, PAD * (j + 1))
                                dve.tensor_tensor(v_aug[c][r, QC, j:H:4, 0:HD], v[r, 1, j:H:4, :], bv[r, j:H:4, :], ALU.add)\
                                   .then_inc(v_part.sem, 1)
                        for t in range(n):
                            last = dve.tensor_tensor(v_aug[c][:, t, :, 0:HD], v[:, t, :, :], bv, ALU.add)
                        last.then_inc(v_kept.sem, 1)

                    def maxima(u, h):
                        c, l = chain(u), layer(u)
                        items = a_items(l)
                        for n, item in enumerate(items):
                            i = len(items) * h + n
                            src = bank[A_BANKS[a_ready.index(u, i) % 2]]
                            a_ready.wait(dve, u, i + 1)
                            if l == 1:
                                for q, at, n_k in item:
                                    last = dve.tensor_reduce(neg_max[c][:, q, h:h + 1], src[:, at:at + n_k], AX.X, ALU.max,
                                                             negate=True)
                            else:
                                q = item[0][0]
                                last = dve.tensor_reduce(neg_max[c][:, q:q + 2, h:h + 1],
                                                         src[:, :].rearrange("p (t n) -> p t n", t=2)[:, :, 0:KCTX],
                                                         AX.X, ALU.max, negate=True)
                            last.then_inc(a_taken.sem, 1)

                    def cut_max(u):
                        c = chain(u)
                        a_taken.wait(dve, u, n_a[layer(u)])
                        pc = max_pieces[c]
                        dve.tensor_copy(pc[:, :, 0, :], neg_max[c][:, :, :]).then_inc(m_step.sem, 1)
                        m_step.wait(dve, u, 1)
                        dve.tensor_tensor(max_rest[:, :, :], neg_max[c][:, :, :], pc[:, :, 0, :], ALU.subtract)\
                           .then_inc(m_step.sem, 1)
                        m_step.wait(dve, u, 2)
                        dve.tensor_copy(pc[:, :, 1, :], max_rest[:, :, :]).then_inc(m_step.sem, 1)
                        m_step.wait(dve, u, 3)
                        dve.tensor_tensor(pc[:, :, 2, :], max_rest[:, :, :], pc[:, :, 1, :], ALU.subtract)\
                           .then_inc(m_step.sem, 1)
                        mt_ready.wait(dve, u, 1)
                        dve.tensor_copy(max_t[c][:, :], job["max"][0:PIECES * H, :]).then_inc(mt_kept.sem, 1)

                    def normalise(u, g):
                        t = job[f"T{g}"][:, :].rearrange("p (t j e) -> p t j e", t=QC, j=4)
                        t_ready.wait(dve, u, g + 1)
                        if u * G + g >= 1:
                            dve.wait_ge(t_taken.sem, (u * G + g))
                        dve.reciprocal(recip[:, :, :, :], t[:, :, :, HD:HD + 1]).then_inc(t_recip.sem, 1)
                        t_recip.wait(dve, u, g + 1)
                        if g == 0 and u >= 1:
                            ot_ready.wait(dve, u - 1, 1)
                        out = o_tok[:, :, 4 * HD * g:4 * HD * (g + 1)].rearrange("p t (j e) -> p t j e", j=4)
                        dve.tensor_tensor(out, t[:, :, :, 0:HD], recip[:, :, :, :].to_broadcast([P, QC, 4, HD]), ALU.mult)\
                           .then_inc(t_taken.sem, 1)

                    def tail(u):
                        c = chain(u)
                        y_ready.wait(dve, u, 1)
                        xbo_ready.wait(dve, u, 1)
                        dve.tensor_tensor(y[:, :, :], job["Y"][:, :].rearrange("p (t d) -> p t d", t=QC), x_bo[c][:, :, :],
                                          ALU.add).then_inc(y_step.sem, 1)
                        y_step.wait(dve, u, 1)
                        for t in range(QC):
                            dve.bn_stats(stats[:, t, :, :].rearrange("p a b -> p (a b)"), y[:, t, :]).then_inc(bn_step.sem, 1)
                        bn_step.wait(dve, u, QC)
                        dve.tensor_tensor(sums[:, :, :], stats[:, :, 0, 1:3], stats[:, :, 1, 1:3], ALU.add).then_inc(bn_step.sem, 1)
                        dve.tensor_tensor(gap[:, :], stats[:, :, 0, 1], stats[:, :, 1, 1], ALU.subtract).then_inc(bn_step.sem, 1)
                        bn_step.wait(dve, u, QC + 2)
                        dve.tensor_tensor(gap2[:, :], gap[:, :], gap[:, :], ALU.mult).then_inc(bn_step.sem, 1)
                        dve.tensor_scalar(within[:, :], sums[:, :, 1], 1.0 / P, EPS, ALU.mult, ALU.add).then_inc(bn_step.sem, 1)
                        dve.tensor_scalar(mean[:, :], sums[:, :, 0], 0.5, None, ALU.mult).then_inc(bn_step.sem, 1)
                        bn_step.wait(dve, u, QC + 5)
                        dve.scalar_tensor_tensor(var[:, :], gap2[:, :], 0.25, within[:, :], ALU.mult, ALU.add).then_inc(var_eps.sem, 1)
                        rstd_ready.wait(dve, u, 1)
                        if u >= 1:
                            x_scaled.wait(dve, u - 1, 1)
                            xt_ready.wait(dve, u - 1, 1)
                        for t in range(QC):
                            dve.tensor_scalar(z[:, t, :], y[:, t, :], mean[:, t:t + 1], rstd[:, t:t + 1], ALU.subtract,
                                              ALU.mult).then_inc(z_ready.sem, 1)

                    cut(0)
                    keep_v(0)
                    for k in range(UNITS + 1):
                        for g in range(G):
                            if k < UNITS:
                                for h in range(*BESIDE[g]):
                                    maxima(k, h)
                            if k >= 1 and g >= 2:
                                normalise(k - 1, g - 2)
                        if k >= 1:
                            normalise(k - 1, 2)
                        if k < UNITS:
                            cut_max(k)
                        if k >= 1:
                            normalise(k - 1, 3)
                            tail(k - 1)
                        if k + 1 < UNITS:
                            cut(k + 1)
                            keep_v(k + 1)

                @block.tensor
                def _(pe):
                    def inputs(u):
                        c = chain(u)
                        pe.wait_ge(loaded[c], 16 * N_LOAD)
                        if u >= 1:
                            v_kept.wait(pe, u - 1, 1)
                        for t in range(QC):
                            last = pe.transpose(job["x"][:, t * P:(t + 1) * P], x_tok[c][:, t, :], ident[:, :])
                        last.then_inc(xl_ready.sem, 1)
                        if u >= 1:
                            mt_kept.wait(pe, u - 1, 1)
                        pe.transpose(job["ctx"][:, 0:P], ctx_tok[c][:, 0, :], ident[:, :])
                        pe.transpose(job["ctx"][:, P:CTX], ctx_tok[c][0:TAIL, 1, :], ident[0:TAIL, 0:TAIL]).then_inc(xl_ready.sem, 1)

                    def project(u):
                        c, l = chain(u), layer(u)
                        n_k = S if l == 1 else KCTX
                        if l == 0:
                            xl_kept.wait(pe, u, 2)
                            tail_kept.wait(pe, u, 1)
                        else:
                            xt_kept.wait(pe, u - CHAINS, 1)
                            y_step.wait(pe, u - CHAINS, 1)
                        src = x_t[c] if l == 1 else ctx_t[c]
                        pe.matmul(job["q"][:, :], w[:, 4 * l, :], x_t[c][:, :], start=True, stop=True).then_inc(qkv_ready.sem, 1)
                        pe.matmul(job["k"][:, 0:n_k], w[:, 4 * l + 1, :], src[:, 0:n_k], start=True, stop=True)\
                          .then_inc(qkv_ready.sem, 1)
                        qk_kept.wait(pe, u, 2)
                        for t in range(QC if l == 1 else 2):
                            last = pe.matmul(job["v"][:, t * P:(t + 1) * P], src[:, t * P:(t + 1) * P], w[:, 4 * l + 2, :],
                                             start=True, stop=True)
                        last.then_inc(qkv_ready.sem, 1)

                    def scores_a(u, h):
                        c, l = chain(u), layer(u)
                        if h == 0:
                            dma_wait(pe, stacked, u, N_STACK)
                            if l == 0:
                                pe.wait_ge(mask_in[c], 16)
                            else:
                                pe.wait_ge(row_in[c], 16 * l)
                        items = a_items(l)
                        for n, item in enumerate(items):
                            i = len(items) * h + n
                            idx = a_ready.index(u, i)
                            dst = bank[A_BANKS[idx % 2]]
                            if idx >= 2:
                                pe.wait_ge(a_taken.sem, (idx - 1))
                            for q, at, n_k in item:
                                last = pe.matmul(dst[:, at:at + n_k], q_stack[c][0:ROWS_A, h, q * P:(q + 1) * P],
                                                 k_stack[c][0:ROWS_A, h, 0:n_k], start=True, stop=l != 1,
                                                 skip_group_check=True)
                                if l == 1:
                                    last = pe.matmul(dst[:, at + n_k - P:at + n_k], ident16[:, :], causal_q[:, :],
                                                     start=False, stop=True, skip_group_check=True)
                            last.then_inc(a_ready.sem, 1)

                    def score_bank(u, i):
                        idx = b_ready.index(u, i)
                        if idx >= 3:
                            pe.wait_ge(p_ready.sem, (idx - 2))
                        return bank[B_BANKS[idx % 3]]

                    def scores_b(u, h):
                        c, l = chain(u), layer(u)
                        if h == 0:
                            dma_wait(pe, max_in, u, PIECES)
                        if l == 1:
                            for n, (parts, _) in enumerate(b_items()):
                                i = len(b_items()) * h + n
                                dst = score_bank(u, i)
                                for kc, at in parts:
                                    pe.matmul(dst[:, at:at + S - P * kc], k_stack[c][0:ROWS_B, h, kc * P:(kc + 1) * P],
                                              q_stack[c][0:ROWS_B, h, kc * P:S], start=True, stop=False,
                                              skip_group_check=True)
                                    last = pe.matmul(dst[:, at:at + P], ident16[:, :], causal_k[:, :], start=False, stop=True,
                                                     skip_group_check=True)
                                last.then_inc(b_ready.sem, 1)
                            return
                        i = (h // 4) * 5 + h % 4
                        dst = score_bank(u, i)
                        pe.matmul(dst[:, :], k_stack[c][0:ROWS_B, h, 0:P], q_stack[c][0:ROWS_B, h, :], start=True, stop=True)\
                          .then_inc(b_ready.sem, 1)
                        if h % 4 == 3:
                            dst = score_bank(u, i + 1)
                            for j in range(4):
                                last = pe.matmul(dst[PAD * j:PAD * (j + 1), :], k_stack[c][0:ROWS_B, h - 3 + j, P:KCTX],
                                                 q_stack[c][0:ROWS_B, h - 3 + j, :], start=True, stop=True)
                            last.then_inc(b_ready.sem, 1)

                    def times_v(u, g):
                        c, l = chain(u), layer(u)
                        if g == 0:
                            v_kept.wait(pe, u, 1)
                        p_ready.wait(pe, u, (g + 1) * n_b[l] // G)
                        if u * G + g >= 1:
                            pe.wait_ge(o_kept.sem, (u * G + g))
                        for kc in (range(QC) if l == 1 else (0, QC)):
                            for j in range(4):
                                h = 4 * g + j
                                if kc == QC:
                                    rhs, q0 = probs[:, (4 * g) % 8, S:2 * S], 0
                                else:
                                    q0 = P * kc if l == 1 else 0
                                    rhs = probs[:, h % 8, P_AT[kc]:P_AT[kc] + S - q0]
                                last = pe.matmul(bank[AV_BANK][PAD * j:PAD * (j + 1), q0:S], v_aug[c][:, kc, h, :], rhs,
                                                 start=kc == 0, stop=kc == (QC - 1 if l == 1 else QC),
                                                 skip_group_check=True)
                        last.then_inc(av_done.sem, 1)

                    def turn(u, g):
                        o_kept.wait(pe, u, g + 1)
                        if g == 0:
                            v_kept.wait(pe, min(u + 1, UNITS - 1), 1)
                        elif g == 1:
                            qk_kept.wait(pe, min(u + 1, UNITS - 1), 4)
                        else:
                            t_taken.wait(pe, u, g - 1 if g == 2 else 3)
                        for t in range(QC):
                            last = pe.transpose(job[f"T{g}"][:, t * P:(t + 1) * P], o_t[:, g, t * P:(t + 1) * P], ident[:, :])
                        last.then_inc(t_ready.sem, 1)

                    def turn_max(u):
                        m_step.wait(pe, u, 4)
                        if u >= 1:
                            t_taken.wait(pe, u - 1, 2)
                        else:
                            qk_kept.wait(pe, u, 4)
                        for t in range(QC):
                            last = pe.matmul(job["max"][0:PIECES * H, t * P:(t + 1) * P],
                                             max_pieces[chain(u)][:, t, :, :].rearrange("p i h -> p (i h)"), ident16[:, :],
                                             start=True, stop=True)
                        last.then_inc(mt_ready.sem, 1)

                    def tail(u):
                        c, l = chain(u), layer(u)
                        t_taken.wait(pe, u, G)
                        if u + 1 < UNITS:
                            mt_kept.wait(pe, u + 1, 1)
                        for t in range(QC):
                            last = pe.transpose(job["oT"][:, t * P:(t + 1) * P], o_tok[:, t, :], ident[:, :])
                        last.then_inc(ot_ready.sem, 1)
                        ot_kept.wait(pe, u, 1)
                        for t in range(QC):
                            last = pe.matmul(job["Y"][:, t * P:(t + 1) * P], o_tt[:, t * P:(t + 1) * P], w[:, 4 * l + 3, :],
                                             start=True, stop=True)
                        last.then_inc(y_ready.sem, 1)
                        for t in range(QC):
                            z_ready.wait(pe, u, t + 1)
                            last = pe.transpose(job["xT"][:, t * P:(t + 1) * P], z[:, t, :], ident[:, :])
                        last.then_inc(xt_ready.sem, 1)

                    inputs(0)
                    project(0)
                    for k in range(UNITS + 1):
                        for g in range(G):
                            a = list(range(*BESIDE[g])) if k < UNITS else []
                            b = list(range(4 * g, 4 * g + 4)) if k >= 1 else []
                            for n in range(max(len(a), len(b))):
                                if n < len(b):
                                    scores_b(k - 1, b[n])
                                if n < len(a):
                                    scores_a(k, a[n])
                            if k >= 1 and g >= 1:
                                times_v(k - 1, g - 1)
                            if k >= 1 and g >= 2:
                                turn(k - 1, g - 2)
                        if k >= 1:
                            times_v(k - 1, G - 1)
                            turn(k - 1, 2)
                        if k < UNITS:
                            turn_max(k)
                        if k >= 1:
                            turn(k - 1, 3)
                            tail(k - 1)
                        if k + 1 < UNITS:
                            if k + 1 < CHAINS:
                                inputs(k + 1)
                            project(k + 1)


            nc.all_engine_barrier(sems_to_clear=range(first_loop_sem.num, last_loop_sem.num + 1))

E_PAR = 2
RING = 3
LEAD = 2
STEPS = E_PAR * QC * FC
BLOCKS = E_PAR * QC


def experts(nc, ins, xmid, out):
    ctx = ExitStack()
    with ctx:
        def sb(name, shape, dt=F32):
            return ctx.enter_context(nc.sbuf_tensor(name, shape, dt))

        def sem(name):
            return ctx.enter_context(nc.semaphore(name))

        pre = "L1_xattn_"
        ident = sb("ident_e", [P, P])
        acc = sb("acc", [P, T, P])
        x_t = sb("xe_t", [P, T, P])
        x_hi = sb("x_hi", [P, T * P], F32R)
        x_lo = sb("x_lo", [P, T * P], F32R)
        w1 = sb("w1", [P, E, FF])
        w2 = sb("w2", [P, E, FC, P])
        b1 = sb("b1", [P, E, FC])
        b2 = sb("b2", [P, E])
        router_w = sb("router_w", [P, E])
        router_b = sb("router_b", [P, E])
        gamma = sb("gamma", [P, P])
        beta = sb("beta", [P, P])
        w1_hi, w1_lo, w2_hi, w2_lo = ([sb(f"{n}{e}", [P, FF], F32R) for e in range(E_PAR)]
                                      for n in ("w1_hi", "w1_lo", "w2_hi", "w2_lo"))
        b1_e = [sb(f"b1_e{e}", [P, FC]) for e in range(E_PAR)]
        b2_e = [sb(f"b2_e{e}", [P, 1]) for e in range(E_PAR)]
        share_e = [sb(f"share_e{e}", [P, T]) for e in range(E_PAR)]
        hidden = sb("hidden", [P, RING, S])
        h_hi = sb("h_hi", [P, RING, S], F32R)
        h_lo = sb("h_lo", [P, RING, S], F32R)
        e_out = sb("e_out", [P, 2, S])
        logits = sb("logits", [P, T, E])
        top = sb("top", [P, T, 8])
        top_at = sb("top_at", [P, T, 8], U32)
        top_atf = sb("top_atf", [P, 2, T])
        row1 = sb("row1", [P, T])
        row2 = sb("row2", [P, T])
        weight = sb("weight", [P, 2, T])
        chosen = sb("chosen", [P, 2, E, T])
        share = sb("share", [P, E, T])
        minus_half = sb("minus_half_e", [P, T])
        stats = sb("stats_e", [P, T, 2, 3])
        sums = sb("sums_e", [P, T, 2])
        gap = sb("gap_e", [P, T])
        gap2 = sb("gap2_e", [P, T])
        within = sb("within_e", [P, T])
        mean = sb("mean_e", [P, T])
        var = sb("var_e", [P, T])
        rstd = sb("rstd_e", [P, T])
        z = x_t
        result = sb("result", [P, T, P])

        bank = [ctx.enter_context(nc.psum_tensor(f"e_bank{i}", [P, S], F32)) for i in range(8)]
        H_BANKS, O_BANKS, T_BANKS = (0, 1, 2, 3), (4, 5), (6, 7)

        s_x = sem("s_x")
        s_in = sem("s_in")
        s_id = sem("s_id")
        s_xt = sem("s_xt")
        s_xk = sem("s_xk")
        s_hi = sem("s_hi")
        s_log = sem("s_log")
        s_r = sem("s_r")
        s_exp = sem("s_exp")
        s_n = sem("s_n")
        s_rstd = sem("s_rstd")
        s_scaled = sem("s_scaled")
        s_result = sem("s_result")
        s_out = sem("s_out")
        split = sem("split")
        h_ready = sem("h_ready")
        h_kept = sem("h_kept")
        hi_ready = sem("hi_ready")
        lo_ready = sem("lo_ready")
        h_used = sem("h_used")
        o_kept = sem("o_kept_e")
        o_turned = sem("o_turned")
        o_added = sem("o_added")
        INPUTS = 8

        with nc.Block() as block:
            @block.sync
            def _(sp):
                for b in range(B):
                    sp.dma_start(acc[:, b * QC:(b + 1) * QC, :], xmid[b].rearrange("(t p) d -> p t d", p=P)).then_inc(s_x, 16)
                sp.dma_start(router_w[:, :], ins[pre + "router_w"]).then_inc(s_in, 16)
                for dst, n in ((router_b, "router_b"), (gamma, "ln3_g"), (beta, "ln3_b")):
                    v = ins[pre + n]
                    sp.dma_start(dst[:, :], v.rearrange("(o d) -> o d", o=1).to_broadcast([P, v.shape[0]])).then_inc(s_in, 16)
                sp.dma_start(w1[:, :, :], ins[pre + "e_w1"].rearrange("e d f -> d e f")).then_inc(s_in, 16)
                sp.dma_start(w2[:, :, :, :], ins[pre + "e_w2"].rearrange("e (c p) d -> p (e c) d", p=P)).then_inc(s_in, 16)
                with nc.allow_non_contiguous_dma(reason="biases, one per partition: small"):
                    sp.dma_start(b1[:, :, :], ins[pre + "e_b1"].rearrange("e (c p) -> p (e c)", p=P)).then_inc(s_in, 16)
                    sp.dma_start(b2[:, :], ins[pre + "e_b2"].rearrange("e d -> d e")).then_inc(s_in, 16)

            @block.gpsimd
            def _(pool):
                pool.memset(ident[:, :], 0.0).then_inc(s_id, 1)
                pool.memset(minus_half[:, :], -0.5).then_inc(s_id, 1)
                pool.wait_ge(s_id, 2)
                pool.affine_select(out=ident[:, :], in_=ident[:, :], compare_op=ALU.not_equal, fill=1.0, base=0,
                                   pattern=[[-1, P]], channel_multiplier=1).then_inc(s_id, 1)

            @block.tensor
            def _(pe):
                pe.wait_ge(s_id, 3)
                pe.wait_ge(s_x, 16 * B)
                for b in range(B):
                    for t in range(QC):
                        last = pe.transpose(bank[b][:, t * P:(t + 1) * P], acc[:, b * QC + t, :], ident[:, :])
                    last.then_inc(s_xt, 1)
                pe.wait_ge(s_in, 16 * INPUTS)
                pe.wait_ge(s_xk, B)
                for t in range(T):
                    last = pe.matmul(bank[4][:, t * E:(t + 1) * E], x_t[:, t, :], router_w[:, :], start=True, stop=True)
                last.then_inc(s_log, 1)

            @block.scalar
            def _(act):
                for b in range(B):
                    act.wait_ge(s_xt, b + 1)
                    act.copy(x_t[:, b * QC:(b + 1) * QC, :], bank[b][:, :].rearrange("p (t d) -> p t d", t=QC)).then_inc(s_xk, 1)
                act.wait_ge(s_r, 3)
                act.activation(logits[:, :, :], logits[:, :, :], ACT.Exp).then_inc(s_exp, 1)
                act.wait_ge(s_r, 6 + 2 * T + 3)
                act.activation(row2[:, :], row1[:, :], ACT.Exp).then_inc(s_exp, 1)

            @block.vector
            def _(dve):
                steps = [0]

                def done(ins_):
                    steps[0] += 1
                    ins_.then_inc(s_r, 1)
                    dve.wait_ge(s_r, steps[0])

                dve.wait_ge(s_xk, B)
                flat = x_t[:, :, :].rearrange("p t d -> p (t d)")
                dve.tensor_copy(x_hi[:, :], flat).then_inc(s_hi, 1)
                dve.wait_ge(s_hi, 1)
                dve.tensor_tensor(x_lo[:, :], flat, x_hi[:, :].bitcast(F32), ALU.subtract).then_inc(s_hi, 1)
                dve.wait_ge(s_log, 1)
                dve.wait_ge(s_in, 16 * INPUTS)
                done(dve.tensor_tensor(logits[:, :, :], bank[4][:, 0:T * E].rearrange("p (t e) -> p t e", e=E),
                                       router_b[:, :].rearrange("p (o e) -> p o e", o=1).to_broadcast([P, T, E]), ALU.add))
                done(dve.tensor_reduce(row1[:, :], logits[:, :, :], AX.X, ALU.max))
                r1 = row1[:, :].rearrange("p (t o) -> p t o", o=1).to_broadcast([P, T, E])
                done(dve.tensor_tensor(logits[:, :, :], logits[:, :, :], r1, ALU.subtract))
                dve.wait_ge(s_exp, 1)
                done(dve.tensor_reduce(row1[:, :], logits[:, :, :], AX.X, ALU.add))
                done(dve.reciprocal(row1[:, :], row1[:, :]))
                done(dve.tensor_tensor(logits[:, :, :], logits[:, :, :], r1, ALU.mult))
                for t in range(T):
                    dve.max(top[:, t, :], logits[:, t, :]).then_inc(s_r, 1)
                dve.wait_ge(s_r, 6 + T)
                for t in range(T):
                    dve.max_index(top_at[:, t, :], top[:, t, :], logits[:, t, :]).then_inc(s_r, 1)
                dve.wait_ge(s_r, 6 + 2 * T)
                steps[0] = 6 + 2 * T
                for i in range(2):
                    dve.tensor_copy(top_atf[:, i, :], top_at[:, :, i]).then_inc(s_r, 1)
                dve.tensor_tensor(row1[:, :], top[:, :, 1], top[:, :, 0], ALU.subtract).then_inc(s_r, 1)
                steps[0] += 3
                dve.wait_ge(s_exp, 2)
                done(dve.tensor_scalar(row1[:, :], row2[:, :], 1.0, None, ALU.add))
                done(dve.reciprocal(weight[:, 0, :], row1[:, :]))
                done(dve.tensor_tensor(weight[:, 1, :], row2[:, :], weight[:, 0, :], ALU.mult))
                for e in range(E):
                    for i in range(2):
                        dve.scalar_tensor_tensor(chosen[:, i, e, :], top_atf[:, i, :], float(e), weight[:, i, :],
                                                 ALU.is_equal, ALU.mult).then_inc(s_r, 1)
                        steps[0] += 1
                dve.wait_ge(s_r, steps[0])
                done(dve.tensor_tensor(share[:, :, :], chosen[:, 0, :, :], chosen[:, 1, :, :], ALU.add))

        with nc.Fori(0, E // E_PAR) as it:
            with nc.Block() as block:
                @block.vector
                def _(dve):
                    def split_weights(par):
                        e = it * E_PAR + par
                        at = split_weights.steps
                        raw1 = w1[:, bass.ds(e, 1), :].rearrange("p o f -> p (o f)")
                        raw2 = w2[:, bass.ds(e, 1), :, :].rearrange("p o c d -> p (o c d)")
                        dve.tensor_copy(w1_hi[par][:, :], raw1).then_inc(split, 1)
                        dve.tensor_copy(w2_hi[par][:, :], raw2).then_inc(split, 1)
                        dve.tensor_copy(b1_e[par][:, :], b1[:, bass.ds(e, 1), :].rearrange("p o c -> p (o c)")).then_inc(split, 1)
                        dve.tensor_copy(b2_e[par][:, :], b2[:, bass.ds(e, 1)]).then_inc(split, 1)
                        dve.tensor_copy(share_e[par][:, :], share[:, bass.ds(e, 1), :].rearrange("p o t -> p (o t)")).then_inc(split, 1)
                        dve.wait_ge(split, at + 5)
                        dve.tensor_tensor(w1_lo[par][:, :], raw1, w1_hi[par][:, :].bitcast(F32), ALU.subtract).then_inc(split, 1)
                        dve.tensor_tensor(w2_lo[par][:, :], raw2, w2_hi[par][:, :].bitcast(F32), ALU.subtract).then_inc(split, 1)
                        split_weights.steps += 7

                    split_weights.steps = 0

                    def add_block(q):
                        par, tb = q // QC, q % QC
                        dve.wait_ge(o_turned, q + 1)
                        if q >= QC:
                            dve.wait_ge(o_added, q - QC + 1)
                        for t in range(QC):
                            n = tb * QC + t
                            last = dve.scalar_tensor_tensor(acc[:, n, :], bank[T_BANKS[q % 2]][:, t * P:(t + 1) * P],
                                                            share_e[par][:, n:n + 1], acc[:, n, :], ALU.mult, ALU.add)
                        last.then_inc(o_added, 1)

                    split_weights(0)
                    for n in range(STEPS):
                        r = n % RING
                        dve.wait_ge(h_kept, n + 1)
                        if n >= RING:
                            dve.wait_ge(h_used, n - RING + 1)
                        dve.tensor_copy(h_hi[:, r, :], hidden[:, r, :]).then_inc(hi_ready, 1)
                        dve.wait_ge(hi_ready, n + 1)
                        dve.tensor_tensor(h_lo[:, r, :], hidden[:, r, :], h_hi[:, r, :].bitcast(F32), ALU.subtract)\
                           .then_inc(lo_ready, 1)
                        if n == FC:
                            for par in range(1, E_PAR):
                                split_weights(par)
                        if n % FC == 2 and n >= 2 * FC:
                            add_block(n // FC - 2)
                    add_block(BLOCKS - 2)
                    add_block(BLOCKS - 1)

                @block.scalar
                def _(act):
                    def keep_out(q):
                        act.wait_ge(h_used, FC * (q + 1))
                        if q >= 2:
                            act.wait_ge(o_turned, q - 1)
                        act.activation(e_out[:, q % 2, :], bank[O_BANKS[q % 2]][:, :], ACT.Identity,
                                       bias=b2_e[q // QC][:, 0:1]).then_inc(o_kept, 1)

                    for n in range(STEPS):
                        act.wait_ge(h_ready, n + 1)
                        if n % (QC * FC) == 0:
                            act.wait_ge(split, 7 * (n // (QC * FC)) + 5)
                        if n >= RING:
                            act.wait_ge(lo_ready, n - RING + 1)
                        act.activation(hidden[:, n % RING, :], bank[H_BANKS[n % 4]][:, :], ACT.Gelu,
                                       bias=b1_e[n // (QC * FC)][:, n % FC:n % FC + 1]).then_inc(h_kept, 1)
                        if n % FC == LEAD + 1 and n > FC:
                            keep_out(n // FC - 1)
                    keep_out(BLOCKS - 1)

                @block.tensor
                def _(pe):
                    def first_product(n):
                        par, tb, c = n // (QC * FC), n // FC % QC, n % FC
                        if n % (QC * FC) == 0:
                            pe.wait_ge(split, 7 * (par + 1))
                        if n >= 4:
                            pe.wait_ge(h_kept, n - 3)
                        dst = bank[H_BANKS[n % 4]][:, :]
                        f, x = slice(c * P, (c + 1) * P), slice(tb * S, (tb + 1) * S)
                        pe.matmul(dst, w1_hi[par][:, f], x_hi[:, x], start=True, stop=False)
                        pe.matmul(dst, w1_hi[par][:, f], x_lo[:, x], start=False, stop=False)
                        pe.matmul(dst, w1_lo[par][:, f], x_hi[:, x], start=False, stop=True).then_inc(h_ready, 1)

                    def second_product(n):
                        par, q, c, r = n // (QC * FC), n // FC, n % FC, n % RING
                        pe.wait_ge(lo_ready, n + 1)
                        if c == 0 and q >= 2:
                            pe.wait_ge(o_kept, q - 1)
                        dst = bank[O_BANKS[q % 2]][:, :]
                        f = slice(c * P, (c + 1) * P)
                        pe.matmul(dst, w2_hi[par][:, f], h_hi[:, r, :], start=c == 0, stop=False)
                        pe.matmul(dst, w2_lo[par][:, f], h_hi[:, r, :], start=False, stop=False)
                        last = pe.matmul(dst, w2_hi[par][:, f], h_lo[:, r, :], start=False, stop=c == FC - 1)
                        last.then_inc(h_used, 1)

                    def turn_out(q):
                        pe.wait_ge(o_kept, q + 1)
                        if q >= 2:
                            pe.wait_ge(o_added, q - 1)
                        for t in range(QC):
                            last = pe.transpose(bank[T_BANKS[q % 2]][:, t * P:(t + 1) * P],
                                                e_out[:, q % 2, t * P:(t + 1) * P], ident[:, :])
                        last.then_inc(o_turned, 1)

                    for n in range(STEPS + LEAD):
                        if n < STEPS:
                            first_product(n)
                        if n >= LEAD:
                            second_product(n - LEAD)
                            if (n - LEAD) % FC == 2 and n - LEAD > FC:
                                turn_out((n - LEAD) // FC - 1)
                    turn_out(BLOCKS - 1)

            nc.all_engine_barrier(sems_to_clear=range(split.num, o_added.num + 1))

        with nc.Block() as block:
            @block.vector
            def _(dve):
                for t in range(T):
                    dve.bn_stats(stats[:, t, :, :].rearrange("p a b -> p (a b)"), acc[:, t, :]).then_inc(s_n, 1)
                dve.wait_ge(s_n, T)
                dve.tensor_tensor(sums[:, :, :], stats[:, :, 0, 1:3], stats[:, :, 1, 1:3], ALU.add).then_inc(s_n, 1)
                dve.tensor_tensor(gap[:, :], stats[:, :, 0, 1], stats[:, :, 1, 1], ALU.subtract).then_inc(s_n, 1)
                dve.wait_ge(s_n, T + 2)
                dve.tensor_tensor(gap2[:, :], gap[:, :], gap[:, :], ALU.mult).then_inc(s_n, 1)
                dve.tensor_scalar(within[:, :], sums[:, :, 1], 1.0 / P, EPS, ALU.mult, ALU.add).then_inc(s_n, 1)
                dve.tensor_scalar(mean[:, :], sums[:, :, 0], 0.5, None, ALU.mult).then_inc(s_n, 1)
                dve.wait_ge(s_n, T + 5)
                dve.scalar_tensor_tensor(var[:, :], gap2[:, :], 0.25, within[:, :], ALU.mult, ALU.add).then_inc(s_n, 1)
                dve.wait_ge(s_rstd, 1)
                for t in range(T):
                    dve.tensor_scalar(z[:, t, :], acc[:, t, :], mean[:, t:t + 1], rstd[:, t:t + 1], ALU.subtract,
                                      ALU.mult).then_inc(s_n, 1)
                for b in range(B):
                    r = slice(b * QC, (b + 1) * QC)
                    g = gamma[:, :].rearrange("p (o d) -> p o d", o=1).to_broadcast([P, QC, P])
                    dve.wait_ge(s_n, T + 6 + (b + 1) * QC)
                    dve.tensor_tensor(z[:, r, :], z[:, r, :], g, ALU.mult).then_inc(s_scaled, 1)
                    dve.wait_ge(s_scaled, b + 1)
                    g = beta[:, :].rearrange("p (o d) -> p o d", o=1).to_broadcast([P, QC, P])
                    dve.tensor_tensor(result[:, r, :], z[:, r, :], g, ALU.add).then_inc(s_result, 1)

            @block.gpsimd
            def _(pool):
                pool.wait_ge(s_n, T + 6)
                pool.tensor_tensor(rstd[:, :], var[:, :], minus_half[:, :], ALU.pow).then_inc(s_rstd, 1)

            @block.sync
            def _(sp):
                for b in range(B):
                    sp.wait_ge(s_result, b + 1)
                    sp.dma_start(out[b].rearrange("(t p) d -> p t d", p=P), result[:, b * QC:(b + 1) * QC, :]).then_inc(s_out, 16)
                sp.wait_ge(s_out, 16 * B)


def build(nc, ins, out):
    xmid = nc.dram_tensor("x_mid", (B, S, P), F32, kind="Internal").ap()
    attention(nc, ins, out if DEBUG else xmid)
    if not DEBUG:
        experts(nc, ins, xmid, out)


DEBUG = False


def kernel(**inputs):
    import concourse.bacc as _bacc
    from concourse.bass_utils import run_bass_kernel_spmd as _run

    nc = _bacc.Bacc("TRN2", target_bir_lowering=False, num_devices=1)
    arrays, ins = {}, {}
    for name, a in inputs.items():
        a = np.ascontiguousarray(a)
        arrays[f"in_{name}"] = a
        ins[name] = nc.dram_tensor(f"in_{name}", a.shape, mybir.dt.from_np(a.dtype), kind="ExternalInput").ap()
    out = nc.dram_tensor("out", (B, S, P), F32, kind="ExternalOutput").ap()
    build(nc, ins, out)
    r = _run(nc, [arrays], core_ids=[0])
    return r.results[0]["out"]
```

```python
import numpy as np
from contextlib import ExitStack

import concourse.bass as bass
from concourse import mybir

F32 = mybir.dt.float32
F32R = mybir.dt.float32r
BF16 = mybir.dt.bfloat16
I32 = mybir.dt.int32
U32 = mybir.dt.uint32
ALU = mybir.AluOpType
ACT = mybir.ActivationFunctionType
AX = mybir.AxisListType

P = 128
B = 4
S = 512
QC = S // P
CTX = 154
H, HD = 16, 8
G = H // 4
E, FF = 8, 512
FC = FF // P
T = B * QC
TAIL = CTX - P
PAD = 32
KCTX = P + PAD
PIECES = 3
STACK = PIECES * PIECES * HD
MASK_ROW = STACK
MAX_ROW = STACK + 1
ROWS_A = STACK + 1
ROWS_B = STACK + 1 + PIECES
LOW = -1.0e38
EPS = 1e-5
SCALE = float(HD) ** -0.5

LAYERS = ("L0", "SELF", "CROSS")
NL = len(LAYERS)
UNITS = NL * B


class Count:

    def __init__(self, sem, per_layer):
        self.sem = sem
        self.before = [0]
        for u in range(UNITS):
            self.before.append(self.before[-1] + per_layer[u // B])

    def index(self, u, k):
        return self.before[u] + k

    def wait(self, eng, u, k):
        eng.wait_ge(self.sem, self.before[u] + k)


def a_items(layer):
    if layer == 1:
        return [[(0, 0, P), (1, P, 2 * P)], [(2, 0, 3 * P)], [(3, 0, 4 * P)]]
    return [[(0, 0, KCTX), (1, 256, KCTX)], [(2, 0, KCTX), (3, 256, KCTX)]]


B_ITEMS = [([(0, 0)], 4 * P), ([(1, 0), (3, 3 * P)], 4 * P), ([(2, 0)], 2 * P)]
P_AT = {0: 0, 1: 4 * P, 3: 7 * P, 2: 8 * P}
P_WIDE = 10 * P


def attention(nc, ins, xmid):
    ctx = ExitStack()
    with ctx:
        def sb(name, shape, dt=F32):
            return ctx.enter_context(nc.sbuf_tensor(name, shape, dt))

        def sem(name):
            return ctx.enter_context(nc.semaphore(name))

        def many(n, name, shape, dt=F32):
            return [sb(f"{name}{c}", shape, dt) for c in range(n)]

        ident = sb("ident", [P, P])
        ident16 = sb("ident16", [P, P], BF16)
        causal_q = sb("causal_q", [P, P], BF16)
        causal_k = sb("causal_k", [P, P], BF16)
        w = sb("w", [P, 4 * NL, P])
        cols = sb("cols", [P, 4 * NL])
        bqs = sb("bqs", [P, NL])
        rows = sb("rows", [P, 4 * NL, P])
        beta_bo = sb("beta_bo", [P, NL - 1, P])
        mask_int = sb("mask_int", [1, B * CTX], I32)
        mask_rows = sb("mask_rows", [1, B + 1, KCTX], BF16)
        zero_row = sb("zero_row", [1, S], BF16)
        one_rows = sb("one_rows", [PIECES, S], BF16)
        minus_half = sb("minus_half", [P, QC])

        x_res = many(B, "x_res", [P, QC, P])
        x_t = many(B, "x_t", [P, S])
        ctx_t = many(B, "ctx_t", [P, P + 4 * PAD])
        pieces = many(2, "pieces", [P, 2, PIECES, S], BF16)
        q_stack = many(2, "q_stack", [P, H, S], BF16)
        k_stack = many(2, "k_stack", [P, H, S], BF16)
        v_aug = many(2, "v_aug", [P, QC + 1, H, PAD])
        neg_max = many(2, "neg_max", [P, QC, H])
        max_pieces = many(2, "max_pieces", [P, QC, 2, PIECES, H // 2], BF16)
        max_t = many(4, "max_t", [PIECES * H // 2, S], BF16)
        qk = sb("qk", [P, 2, S])
        rest = sb("rest", [P, 2, S])
        max_rest = sb("max_rest", [P, QC, H // 2])
        probs = sb("probs", [P, 8, P_WIDE])
        ctx_tok = [probs[:, b, 2 * S:2 * S + 2 * P].rearrange("p (t d) -> p t d", t=2) for b in range(B)]
        o_t = sb("o_t", [P, G, S])
        recip = sb("recip", [P, QC, 4, 1])
        o_tok = sb("o_tok", [P, QC, P])
        o_tt = sb("o_tt", [P, S])
        y = sb("y", [P, QC, P])
        w_raw = y
        z = sb("z", [P, QC, P])
        stats = sb("stats", [P, QC, 2, 3])
        sums = sb("sums", [P, QC, 2])
        gap = sb("gap", [P, QC])
        gap2 = sb("gap2", [P, QC])
        within = sb("within", [P, QC])
        mean = sb("mean", [P, QC])
        var = sb("var", [P, QC])
        rstd = sb("rstd", [P, QC])

        bank = [ctx.enter_context(nc.psum_tensor(f"bank{i}", [P, S], F32)) for i in range(8)]
        A_BANKS, B_BANKS, AV_BANK, JOB_BANKS = (0, 1), (2, 3, 4), 5, (6, 7)

        q_dram = [nc.dram_tensor(f"q_pieces{c}", (H, PIECES, HD, S), BF16, kind="Internal").ap() for c in range(2)]
        k_dram = [nc.dram_tensor(f"k_pieces{c}", (H, PIECES, HD, S), BF16, kind="Internal").ap() for c in range(2)]

        s_const = sem("s_const")
        s_made = sem("s_made")
        s_low = sem("s_low")
        s_beta = sem("s_beta")
        s_wt = sem("s_wt")
        s_w = sem("s_w")
        s_bq = sem("s_bq")
        s_rows = sem("s_rows")
        one = (1, 1, 1)
        n_a = tuple(H * len(a_items(l)) for l in range(NL))
        n_b = tuple(H * len(B_ITEMS) if l == 1 else H + G for l in range(NL))
        a_ready = Count(sem("a_ready"), n_a)
        a_taken = Count(sem("a_taken"), n_a)
        b_ready = Count(sem("b_ready"), n_b)
        p_ready = Count(sem("p_ready"), n_b)
        av_done = Count(sem("av_done"), (G,) * NL)
        o_kept = Count(sem("o_kept"), (G,) * NL)
        t_ready = Count(sem("t_ready"), (G,) * NL)
        t_recip = Count(sem("t_recip"), (G,) * NL)
        t_taken = Count(sem("t_taken"), (G,) * NL)
        m_step = Count(sem("m_step"), (8,) * NL)
        mt_ready = Count(sem("mt_ready"), (2,) * NL)
        mt_kept = Count(sem("mt_kept"), (2,) * NL)
        ot_ready = Count(sem("ot_ready"), one)
        ot_kept = Count(sem("ot_kept"), one)
        y_ready = Count(sem("y_ready"), one)
        y_step = Count(sem("y_step"), one)
        bn_step = Count(sem("bn_step"), (QC + 5,) * NL)
        var_eps = Count(sem("var_eps"), one)
        rstd_ready = Count(sem("rstd_ready"), one)
        z_ready = Count(sem("z_ready"), (QC,) * NL)
        xt_ready = Count(sem("xt_ready"), one)
        xt_kept = Count(sem("xt_kept"), one)
        x_scaled = Count(sem("x_scaled"), one)
        x_new = Count(sem("x_new"), one)
        x_bo = sem("x_bo")
        xl_ready = Count(sem("xl_ready"), (2, 0, 0))
        xl_kept = Count(sem("xl_kept"), (3, 0, 0))
        qk_ready = Count(sem("qk_ready"), (2,) * NL)
        qk_kept = Count(sem("qk_kept"), (4,) * NL)
        rest_step = Count(sem("rest_step"), (6,) * NL)
        v_ready = Count(sem("v_ready"), one)
        v_kept = Count(sem("v_kept"), one)
        v_part = sem("v_part")
        loaded = [sem(f"loaded{b}") for b in range(B)]
        written = [sem(f"written{c}") for c in range(2)]
        stacked = [sem(f"stacked{c}") for c in range(4)]
        max_in = [sem(f"max_in{c}") for c in range(4)]
        stored = sem("stored")
        N_LOAD, N_WRITE, N_STACK = 3, 2 * PIECES, PIECES * PIECES + PIECES + 1
        n_const = 3 * 4 * NL + 1

        def layer(u):
            return u // B

        def batch(u):
            return u % B

        def pair(u):
            return u % 2

        def dma_wait(eng, sems, u, n, half=None):
            at = pair(u) if half is None else 2 * pair(u) + half
            eng.wait_ge(sems[at], 16 * n * (u // 2 + 1))

        def keys(u):
            return S if layer(u) == 1 else KCTX

        taken_by = {"x": (xl_kept, 1), "ctx": (xl_kept, 3), "q": (qk_kept, 2), "k": (qk_kept, 4), "v": (v_kept, 1),
                    "max0": (mt_kept, 1), "max1": (mt_kept, 2), "oT": (ot_kept, 1), "Y": (y_step, 1),
                    "xT": (xt_kept, 1), "T0": (t_taken, 1), "T1": (t_taken, 2), "T2": (t_taken, 3), "T3": (t_taken, 4)}
        SLOTS = UNITS + 2

        STEPS = [[("max1", 1)],
                 [("av3", 2), ("x", -1)],
                 [("ctx", -1), ("T3", 2)],
                 [("q", -1)],
                 [("k", -1), ("cut", -1)],
                 [("av0", 1), ("oT", 2)],
                 [("T0", 1)],
                 [("Y", 2), ("cut max0", 0)],
                 [("max0", 0), ("stats", 2)],
                 [("av1", 1), ("var", 2)],
                 [("T1", 1)],
                 [("z", 2)],
                 [("v", 0)],
                 [("av2", 1), ("xT", 2)],
                 [("T2", 1)],
                 [("cut max1", 0)]]

        def steps(k, h):
            todo = [(name, k - ago) for name, ago in STEPS[h] if 0 <= k - ago < UNITS]
            return [(name, u) for name, u in todo if name not in ("x", "ctx") or layer(u) == 0]

        prologue = [("x", 0), ("ctx", 0), ("q", 0), ("k", 0)]
        all_jobs = prologue + [j for k in range(SLOTS) for h in range(H) for j in steps(k, h) if j[0] in taken_by]
        job_at = {j: i for i, j in enumerate(all_jobs)}

        def job(name, u):
            return bank[JOB_BANKS[job_at[name, u] % 2]]

        def job_bank(pe, name, u):
            i = job_at[name, u]
            if i >= 2:
                before, v = all_jobs[i - 2]
                count, n = taken_by[before]
                count.wait(pe, v, n)
            return job(name, u)

        with nc.Block() as block:
            @block.sync
            def _(sp):
                for b in range(B):
                    sp.dma_start(x_res[b][:, :, :], ins["x"][b].rearrange("(t p) d -> p t d", p=P)).then_inc(loaded[b], 16)
                    sp.dma_start(ctx_tok[b][:, 0, :], ins["ctx_1024"][b, 0:P, :]).then_inc(loaded[b], 16)
                    sp.dma_start(ctx_tok[b][0:TAIL, 1, :], ins["ctx_1024"][b, P:CTX, :]).then_inc(loaded[b], 16)
                names = [("L0_xattn_", ("Wq", "Wk", "Wv", "Wo")), ("L1_xattn_sa_", ("wq", "wk", "wv", "wo")),
                         ("L1_xattn_ca_", ("wq", "wk", "wv", "wo"))]
                norms = [("L0_xattn_ln_gamma", "L0_xattn_ln_beta"), ("L1_xattn_ln1_g", "L1_xattn_ln1_b"),
                         ("L1_xattn_ln2_g", "L1_xattn_ln2_b")]
                for l, (head, ws) in enumerate(names[:NL]):
                    for i, n in enumerate(ws):
                        dst = w_raw[:, i, :] if l == 0 else w[:, 4 * l + i, :]
                        sp.dma_start(dst, ins[head + n]).then_inc(s_const, 16)
                    vectors = [ins[head + "bq"], ins[head + "bk"], ins[norms[l][0]], ins[norms[l][1]]]
                    for i, v in enumerate(vectors):
                        sp.dma_start(cols[:, 4 * l + i:4 * l + i + 1], v.rearrange("(p o) -> p o", o=1)).then_inc(s_const, 16)
                    vectors = [ins[head + "bv"], ins[head + "bo"], ins[norms[l][0]], ins[norms[l][1]]]
                    for i, v in enumerate(vectors):
                        sp.dma_start(rows[:, 4 * l + i, :], v.rearrange("(o d) -> o d", o=1).to_broadcast([P, P])).then_inc(s_const, 16)
                sp.dma_start(mask_int[:, :], ins["mask_BxS2_ik0"].rearrange("(o b) s -> o (b s)", o=1)).then_inc(s_const, 16)
                sp.wait_ge(s_low, 4)
                for c in range(2):
                    src = one_rows[:, :].rearrange("p (o n) -> p o n", o=1)
                    sp.dma_start(q_stack[c][MASK_ROW:MASK_ROW + 1, :, :], src[0:1].to_broadcast([1, H, S])).then_inc(s_rows, 16)
                    sp.dma_start(k_stack[c][MAX_ROW:MAX_ROW + PIECES, :, :], src.to_broadcast([PIECES, H, S])).then_inc(s_rows, 16)

            @block.gpsimd
            def _(pool):
                pool.memset(ident[:, :], 0.0).then_inc(s_made, 1)
                pool.memset(minus_half[:, :], -0.5).then_inc(s_made, 1)
                pool.memset(causal_q[:, :], 0.0).then_inc(s_made, 1)
                pool.memset(causal_k[:, :], 0.0).then_inc(s_made, 1)
                pool.wait_ge(s_made, 4)
                pool.affine_select(out=ident[:, :], in_=ident[:, :], compare_op=ALU.not_equal, fill=1.0, base=0,
                                   pattern=[[-1, P]], channel_multiplier=1).then_inc(s_made, 1)
                pool.affine_select(out=causal_q[:, :], in_=causal_q[:, :], compare_op=ALU.is_ge, fill=LOW, base=0,
                                   pattern=[[-1, P]], channel_multiplier=1).then_inc(s_made, 1)
                pool.affine_select(out=causal_k[:, :], in_=causal_k[:, :], compare_op=ALU.is_ge, fill=LOW, base=0,
                                   pattern=[[1, P]], channel_multiplier=-1).then_inc(s_made, 1)

            @block.vector
            def _(dve):
                dve.memset(one_rows[:, :], 1.0).then_inc(s_low, 1)
                dve.memset(zero_row[:, :], 0.0).then_inc(s_low, 1)
                dve.memset(mask_rows[:, :, :], 0.0).then_inc(s_low, 1)
                dve.wait_ge(s_low, 3)
                dve.memset(mask_rows[:, :, CTX:KCTX], LOW).then_inc(s_low, 1)
                for b in range(B):
                    dve.memset(ctx_t[b][:, :], 0.0).then_inc(s_low, 1)
                for c in range(2):
                    dve.memset(v_aug[c][:, :, :, :], 0.0).then_inc(s_low, 1)
                dve.wait_ge(s_made, 5)
                dve.tensor_copy(ident16[:, :], ident[:, :]).then_inc(s_low, 1)
                dve.wait_ge(s_low, 11)
                for c in range(2):
                    dve.memset(v_aug[c][:, 0:QC, :, HD:HD + 1], 1.0)
                    for j in range(4):
                        dve.memset(v_aug[c][PAD * j:PAD * (j + 1), QC, j:H:4, HD:HD + 1], 1.0)
                dve.wait_ge(s_const, 16 * n_const)
                dve.tensor_scalar(mask_rows[:, 0:B, 0:CTX], mask_int[:, :].rearrange("p (b s) -> p b s", b=B), 0.0, LOW,
                                  ALU.is_equal, ALU.mult).then_inc(s_low, 1)

            @block.scalar
            def _(act):
                act.wait_ge(s_const, 16 * n_const)
                for l in range(NL):
                    act.mul(bqs[:, l:l + 1], cols[:, 4 * l:4 * l + 1], SCALE).then_inc(s_bq, 1)
                act.wait_ge(s_wt, 1)
                act.copy(w[:, 0:4, :], bank[0][:, :].rearrange("p (i d) -> p i d", i=4)).then_inc(s_w, 1)

            @block.tensor
            def _(pe):
                pe.wait_ge(s_made, 5)
                pe.wait_ge(s_const, 16 * n_const)
                for i in range(4):
                    last = pe.transpose(bank[0][:, i * P:(i + 1) * P], w_raw[:, i, :], ident[:, :])
                last.then_inc(s_wt, 1)

        with nc.Block() as block:
            @block.sync
            def _(sp):
                def write(u):
                    c = pair(u)
                    qk_kept.wait(sp, u, 4)
                    rest_step.wait(sp, u, 6)
                    for t, (dram, n) in enumerate(((q_dram[c], S), (k_dram[c], keys(u)))):
                        for i in range(PIECES):
                            sp.dma_start(dram[:, i, :, 0:n], pieces[c][:, t, i, 0:n]).then_inc(written[c], 16)

                def stack(u, half):
                    c, n_k = pair(u), keys(u)
                    hs = slice(half * H // 2, (half + 1) * H // 2)
                    if half == 0:
                        dma_wait(sp, written, u, N_WRITE)
                    if u >= 2:
                        a_ready.wait(sp, u - 2, n_a[layer(u - 2)])
                        b_ready.wait(sp, u - 2, (half + 1) * n_b[layer(u - 2)] // 2)
                    done = stacked[2 * c + half]
                    for i in range(PIECES):
                        at = PIECES * HD * i
                        for j in range(PIECES):
                            sp.dma_start(q_stack[c][at + HD * j:at + HD * (j + 1), hs, :],
                                         q_dram[c][hs, i, :, :].rearrange("h e n -> e h n")).then_inc(done, 16)
                        sp.dma_start(k_stack[c][at:at + PIECES * HD, hs, 0:n_k],
                                     k_dram[c][hs, :, :, 0:n_k].rearrange("h j e n -> (j e) h n")).then_inc(done, 16)
                    src = zero_row[:, :] if layer(u) == 1 else mask_rows[:, batch(u) if layer(u) == 0 else B, :]
                    src = src.rearrange("p (o n) -> p o n", o=1).to_broadcast([1, H // 2, n_k])
                    sp.dma_start(k_stack[c][MASK_ROW:MASK_ROW + 1, hs, 0:n_k], src).then_inc(done, 16)

                def max_rows(u, half):
                    c = 2 * pair(u) + half
                    mt_kept.wait(sp, u, half + 1)
                    sp.dma_start(q_stack[pair(u)][MAX_ROW:MAX_ROW + PIECES, half * H // 2:(half + 1) * H // 2, :],
                                 max_t[c][:, :]).then_inc(max_in[c], 16)

                def store(u):
                    x_new.wait(sp, u, 1)
                    sp.dma_start(xmid[batch(u)].rearrange("(t p) d -> p t d", p=P), x_res[batch(u)][:, :, :]).then_inc(stored, 16)

                sp.wait_ge(s_rows, 16 * 4)
                write(0)
                stack(0, 0)
                stack(0, 1)
                for u in range(UNITS):
                    if u + 1 < UNITS:
                        write(u + 1)
                    max_rows(u, 0)
                    if u + 1 < UNITS:
                        stack(u + 1, 0)
                        stack(u + 1, 1)
                    max_rows(u, 1)
                for u in range(UNITS - B, UNITS):
                    store(u)
                sp.wait_ge(stored, 16 * B)

            @block.gpsimd
            def _(pool):
                def over_tiles(row):
                    return row.to_broadcast([P, QC, P])

                def norm(u):
                    x, l = x_res[batch(u)], layer(u)
                    var_eps.wait(pool, u, 1)
                    pool.tensor_tensor(rstd[:, :], var[:, :], minus_half[:, :], ALU.pow).then_inc(rstd_ready.sem, 1)
                    z_ready.wait(pool, u, QC)
                    pool.tensor_tensor(x[:, :, :], z[:, :, :], over_tiles(rows[:, 4 * l + 2:4 * l + 3, :]), ALU.mult)\
                        .then_inc(x_scaled.sem, 1)
                    x_scaled.wait(pool, u, 1)
                    plus = beta_bo[:, l:l + 1, :] if l + 1 < NL else rows[:, 4 * l + 3:4 * l + 4, :]
                    pool.tensor_tensor(x[:, :, :], x[:, :, :], over_tiles(plus), ALU.add).then_inc(x_new.sem, 1)

                for l in range(NL - 1):
                    pool.tensor_tensor(beta_bo[:, l, :], rows[:, 4 * l + 3, :], rows[:, 4 * l + 5, :], ALU.add).then_inc(s_beta, 1)
                for b in range(B):
                    pool.wait_ge(loaded[b], 16 * N_LOAD)
                    xl_ready.wait(pool, b, 1)
                    pool.tensor_tensor(x_res[b][:, :, :], x_res[b][:, :, :], over_tiles(rows[:, 1:2, :]), ALU.add)\
                        .then_inc(x_bo, 1)
                pool.wait_ge(s_beta, NL - 1)
                for u in range(UNITS):
                    norm(u)

            @block.scalar
            def _(act):
                def inputs(u):
                    b = batch(u)
                    xl_ready.wait(act, u, 1)
                    act.copy(x_t[b][:, :], job("x", u)[:, :]).then_inc(xl_kept.sem, 1)
                    xl_ready.wait(act, u, 2)
                    src = job("ctx", u)
                    act.copy(ctx_t[b][:, 0:P], src[:, 0:P]).then_inc(xl_kept.sem, 1)
                    tail = src[:, P:CTX].rearrange("p (o n) -> p o n", o=1).to_broadcast([P, 4, TAIL])
                    act.copy(ctx_t[b][:, P:P + 4 * PAD].rearrange("p (j n) -> p j n", j=4)[:, :, 0:TAIL], tail)\
                       .then_inc(xl_kept.sem, 1)

                def project(u, t):
                    c, l = pair(u), layer(u)
                    if t == 0:
                        if u >= 1:
                            rest_step.wait(act, u - 1, 6)
                        if u >= 2:
                            dma_wait(act, written, u - 2, N_WRITE)
                    name, n, bias, scale = (("q", S, bqs[:, l:l + 1], SCALE), ("k", keys(u), cols[:, 4 * l + 1:4 * l + 2], 1.0))[t]
                    src = job(name, u)
                    qk_ready.wait(act, u, t + 1)
                    act.activation(qk[:, t, 0:n], src[:, 0:n], ACT.Identity, bias=bias, scale=scale).then_inc(qk_kept.sem, 1)
                    act.activation(pieces[c][:, t, 0, 0:n], src[:, 0:n], ACT.Identity, bias=bias, scale=scale)\
                       .then_inc(qk_kept.sem, 1)

                def exps(u, h, i, n, at):
                    b_ready.wait(act, u, i + 1)
                    if u * G + h // 4 >= 2:
                        act.wait_ge(av_done.sem, u * G + h // 4 - 1)
                    act.activation(probs[:, h % 8, at:at + n], bank[B_BANKS[b_ready.index(u, i) % 3]][:, 0:n], ACT.Exp)\
                       .then_inc(p_ready.sem, 1)

                def head_exps(u, h):
                    if layer(u) == 1:
                        at = 0
                        for n, (_, wide) in enumerate(B_ITEMS):
                            exps(u, h, len(B_ITEMS) * h + n, wide, at)
                            at += wide
                        return
                    i = (h // 4) * 5 + h % 4
                    exps(u, h, i, S, 0)
                    if h % 4 == 3:
                        exps(u, h - 3, i + 1, S, S)

                def keep_o(u, g):
                    av_done.wait(act, u, g + 1)
                    if u >= 1:
                        t_ready.wait(act, u - 1, g + 1)
                    act.copy(o_t[:, g, :], bank[AV_BANK][:, :]).then_inc(o_kept.sem, 1)

                def keep_output(u):
                    ot_ready.wait(act, u, 1)
                    if u >= 1:
                        y_ready.wait(act, u - 1, 1)
                    act.copy(o_tt[:, :], job("oT", u)[:, :]).then_inc(ot_kept.sem, 1)

                def keep_x(u):
                    l = layer(u)
                    xt_ready.wait(act, u, 1)
                    act.activation(x_t[batch(u)][:, :], job("xT", u)[:, :], ACT.Identity, bias=cols[:, 4 * l + 3:4 * l + 4],
                                   scale=cols[:, 4 * l + 2:4 * l + 3]).then_inc(xt_kept.sem, 1)

                inputs(0)
                project(0, 0)
                project(0, 1)
                for k in range(SLOTS):
                    for h in range(H):
                        if 0 <= k - 1 < UNITS:
                            head_exps(k - 1, h)
                        for name, u in steps(k, h):
                            if name == "x":
                                inputs(u)
                            if name in ("q", "k"):
                                project(u, ("q", "k").index(name))
                            if name[:2] == "av":
                                keep_o(u, int(name[2]))
                            if name == "oT":
                                keep_output(u)
                            if name == "xT":
                                keep_x(u)

            @block.vector
            def _(dve):
                parts = [0]

                def cut(u):
                    c = pair(u)
                    for t, n in ((0, S), (1, keys(u))):
                        qk_kept.wait(dve, u, 2 * t + 2)
                        p = pieces[c][:, t, :, 0:n]
                        dve.tensor_tensor(rest[:, t, 0:n], qk[:, t, 0:n], p[:, 0, :], ALU.subtract).then_inc(rest_step.sem, 1)
                        rest_step.wait(dve, u, 3 * t + 1)
                        dve.tensor_copy(p[:, 1, :], rest[:, t, 0:n]).then_inc(rest_step.sem, 1)
                        rest_step.wait(dve, u, 3 * t + 2)
                        dve.tensor_tensor(p[:, 2, :], rest[:, t, 0:n], p[:, 1, :], ALU.subtract).then_inc(rest_step.sem, 1)

                def keep_v(u):
                    c, l = pair(u), layer(u)
                    v_ready.wait(dve, u, 1)
                    if u >= 2:
                        av_done.wait(dve, u - 2, G)
                    v = job("v", u)[:, :].rearrange("p (t h e) -> p t h e", t=QC, h=H)
                    bv = rows[:, 4 * l, :].rearrange("p (h e) -> p h e", h=H)
                    if l != 1:
                        for j in range(4):
                            r = slice(PAD * j, PAD * (j + 1))
                            dve.tensor_tensor(v_aug[c][r, QC, j:H:4, 0:HD], v[r, 1, j:H:4, :], bv[r, j:H:4, :], ALU.add)\
                               .then_inc(v_part, 1)
                            parts[0] += 1
                    for t in range(QC if l == 1 else 1):
                        last = dve.tensor_tensor(v_aug[c][:, t, :, 0:HD], v[:, t, :, :], bv, ALU.add)
                    last.then_inc(v_kept.sem, 1)

                def maxima(u, h):
                    c, l = pair(u), layer(u)
                    items = a_items(l)
                    for n, item in enumerate(items):
                        i = len(items) * h + n
                        src = bank[A_BANKS[a_ready.index(u, i) % 2]]
                        a_ready.wait(dve, u, i + 1)
                        if l == 1:
                            for q, at, n_k in item:
                                last = dve.tensor_reduce(neg_max[c][:, q, h:h + 1], src[:, at:at + n_k], AX.X, ALU.max,
                                                         negate=True)
                        else:
                            q = item[0][0]
                            last = dve.tensor_reduce(neg_max[c][:, q:q + 2, h:h + 1],
                                                     src[:, :].rearrange("p (t n) -> p t n", t=2)[:, :, 0:KCTX],
                                                     AX.X, ALU.max, negate=True)
                        last.then_inc(a_taken.sem, 1)

                def cut_max(u, half):
                    m = neg_max[pair(u)][:, :, half * H // 2:(half + 1) * H // 2]
                    pc = max_pieces[pair(u)][:, :, half, :, :]
                    a_taken.wait(dve, u, (half + 1) * n_a[layer(u)] // 2)
                    dve.tensor_copy(pc[:, :, 0, :], m).then_inc(m_step.sem, 1)
                    m_step.wait(dve, u, 4 * half + 1)
                    dve.tensor_tensor(max_rest[:, :, :], m, pc[:, :, 0, :], ALU.subtract).then_inc(m_step.sem, 1)
                    m_step.wait(dve, u, 4 * half + 2)
                    dve.tensor_copy(pc[:, :, 1, :], max_rest[:, :, :]).then_inc(m_step.sem, 1)
                    m_step.wait(dve, u, 4 * half + 3)
                    dve.tensor_tensor(pc[:, :, 2, :], max_rest[:, :, :], pc[:, :, 1, :], ALU.subtract).then_inc(m_step.sem, 1)

                def keep_max(u, half):
                    mt_ready.wait(dve, u, half + 1)
                    if u >= 2:
                        dma_wait(dve, max_in, u - 2, 1, half)
                    dve.tensor_copy(max_t[2 * pair(u) + half][:, :], job(f"max{half}", u)[0:PIECES * H // 2, :])\
                       .then_inc(mt_kept.sem, 1)

                def normalise(u, g):
                    t = job(f"T{g}", u)[:, :].rearrange("p (t j e) -> p t j e", t=QC, j=4)
                    t_ready.wait(dve, u, g + 1)
                    if u * G + g >= 1:
                        dve.wait_ge(t_taken.sem, u * G + g)
                    dve.reciprocal(recip[:, :, :, :], t[:, :, :, HD:HD + 1]).then_inc(t_recip.sem, 1)
                    t_recip.wait(dve, u, g + 1)
                    if g == 0 and u >= 1:
                        ot_ready.wait(dve, u - 1, 1)
                    out = o_tok[:, :, 4 * HD * g:4 * HD * (g + 1)].rearrange("p t (j e) -> p t j e", j=4)
                    dve.tensor_tensor(out, t[:, :, :, 0:HD], recip[:, :, :, :].to_broadcast([P, QC, 4, HD]), ALU.mult)\
                       .then_inc(t_taken.sem, 1)

                def residual(u):
                    y_ready.wait(dve, u, 1)
                    if layer(u) == 0:
                        dve.wait_ge(x_bo, u + 1)
                    else:
                        x_new.wait(dve, u - B, 1)
                    dve.tensor_tensor(y[:, :, :], job("Y", u)[:, :].rearrange("p (t d) -> p t d", t=QC),
                                      x_res[batch(u)][:, :, :], ALU.add).then_inc(y_step.sem, 1)

                def statistics(u):
                    y_step.wait(dve, u, 1)
                    for t in range(QC):
                        dve.bn_stats(stats[:, t, :, :].rearrange("p a b -> p (a b)"), y[:, t, :]).then_inc(bn_step.sem, 1)

                def variance(u):
                    bn_step.wait(dve, u, QC)
                    dve.tensor_tensor(sums[:, :, :], stats[:, :, 0, 1:3], stats[:, :, 1, 1:3], ALU.add).then_inc(bn_step.sem, 1)
                    dve.tensor_tensor(gap[:, :], stats[:, :, 0, 1], stats[:, :, 1, 1], ALU.subtract).then_inc(bn_step.sem, 1)
                    bn_step.wait(dve, u, QC + 2)
                    dve.tensor_tensor(gap2[:, :], gap[:, :], gap[:, :], ALU.mult).then_inc(bn_step.sem, 1)
                    dve.tensor_scalar(within[:, :], sums[:, :, 1], 1.0 / P, EPS, ALU.mult, ALU.add).then_inc(bn_step.sem, 1)
                    dve.tensor_scalar(mean[:, :], sums[:, :, 0], 0.5, None, ALU.mult).then_inc(bn_step.sem, 1)
                    bn_step.wait(dve, u, QC + 5)
                    if u >= 1:
                        rstd_ready.wait(dve, u - 1, 1)
                    dve.scalar_tensor_tensor(var[:, :], gap2[:, :], 0.25, within[:, :], ALU.mult, ALU.add).then_inc(var_eps.sem, 1)

                def standardise(u):
                    rstd_ready.wait(dve, u, 1)
                    if u >= 1:
                        x_scaled.wait(dve, u - 1, 1)
                        xt_ready.wait(dve, u - 1, 1)
                    for t in range(QC):
                        dve.tensor_scalar(z[:, t, :], y[:, t, :], mean[:, t:t + 1], rstd[:, t:t + 1], ALU.subtract,
                                          ALU.mult).then_inc(z_ready.sem, 1)

                cut(0)
                for k in range(SLOTS):
                    for h in range(H):
                        if k < UNITS:
                            maxima(k, h)
                        for name, u in steps(k, h):
                            if name == "cut":
                                cut(u)
                            if name == "v":
                                keep_v(u)
                            if name[:7] == "cut max":
                                cut_max(u, int(name[7]))
                            if name[:3] == "max":
                                keep_max(u, int(name[3]))
                            if name[0] == "T":
                                normalise(u, int(name[1]))
                            if name == "Y":
                                residual(u)
                            if name == "stats":
                                statistics(u)
                            if name == "var":
                                variance(u)
                            if name == "z":
                                standardise(u)

            @block.tensor
            def _(pe):
                def scores_a(u, h, n):
                    c, l = pair(u), layer(u)
                    if h % (H // 2) == 0 and n == 0:
                        dma_wait(pe, stacked, u, N_STACK, h // (H // 2))
                    items = a_items(l)
                    if n >= len(items):
                        return
                    idx = a_ready.index(u, len(items) * h + n)
                    dst = bank[A_BANKS[idx % 2]]
                    if idx >= 2:
                        pe.wait_ge(a_taken.sem, idx - 1)
                    for q, at, n_k in items[n]:
                        last = pe.matmul(dst[:, at:at + n_k], q_stack[c][0:ROWS_A, h, q * P:(q + 1) * P],
                                         k_stack[c][0:ROWS_A, h, 0:n_k], start=True, stop=l != 1,
                                         skip_group_check=True)
                        if l == 1:
                            last = pe.matmul(dst[:, at + n_k - P:at + n_k], ident16[:, :], causal_q[:, :],
                                             start=False, stop=True, skip_group_check=True)
                    last.then_inc(a_ready.sem, 1)

                def score_bank(u, i):
                    idx = b_ready.index(u, i)
                    if idx >= 3:
                        pe.wait_ge(p_ready.sem, idx - 2)
                    return bank[B_BANKS[idx % 3]]

                def scores_b(u, h, n):
                    c, l = pair(u), layer(u)
                    if h % (H // 2) == 0 and n == 0:
                        dma_wait(pe, max_in, u, 1, h // (H // 2))
                    if l == 1:
                        dst = score_bank(u, len(B_ITEMS) * h + n)
                        for kc, at in B_ITEMS[n][0]:
                            pe.matmul(dst[:, at:at + S - P * kc], k_stack[c][0:ROWS_B, h, kc * P:(kc + 1) * P],
                                      q_stack[c][0:ROWS_B, h, kc * P:S], start=True, stop=False,
                                      skip_group_check=True)
                            last = pe.matmul(dst[:, at:at + P], ident16[:, :], causal_k[:, :], start=False, stop=True,
                                             skip_group_check=True)
                        last.then_inc(b_ready.sem, 1)
                    i = (h // 4) * 5 + h % 4
                    if l != 1 and n == 0:
                        dst = score_bank(u, i)
                        pe.matmul(dst[:, :], k_stack[c][0:ROWS_B, h, 0:P], q_stack[c][0:ROWS_B, h, :], start=True, stop=True)\
                          .then_inc(b_ready.sem, 1)
                    if l != 1 and n == 1 and h % 4 == 3:
                        dst = score_bank(u, i + 1)
                        for j in range(4):
                            last = pe.matmul(dst[PAD * j:PAD * (j + 1), :], k_stack[c][0:ROWS_B, h - 3 + j, P:KCTX],
                                             q_stack[c][0:ROWS_B, h - 3 + j, :], start=True, stop=True)
                        last.then_inc(b_ready.sem, 1)

                def times_v(k, h, n):
                    u, g = (k - 1, h // 4 - 1) if h >= 4 else (k - 2, G - 1)
                    if h % 4 > 1 or not 0 <= u < UNITS:
                        return
                    c, l = pair(u), layer(u)
                    at, chunks = (2, range(QC)) if l == 1 else (4, (0, QC))
                    part = 3 * (h % 4) + n - at
                    if part < 0:
                        return
                    kc = chunks[part]
                    if part == 0:
                        if g == 0:
                            v_kept.wait(pe, u, 1)
                        p_ready.wait(pe, u, (g + 1) * n_b[l] // G)
                        if u * G + g >= 1:
                            pe.wait_ge(o_kept.sem, u * G + g)
                    for j in range(4):
                        head = 4 * g + j
                        q0 = P * kc if l == 1 else 0
                        if kc == QC:
                            rhs = probs[:, (4 * g) % 8, S:2 * S]
                        else:
                            rhs = probs[:, head % 8, P_AT[kc]:P_AT[kc] + S - q0]
                        last = pe.matmul(bank[AV_BANK][PAD * j:PAD * (j + 1), q0:S], v_aug[c][:, kc, head, :], rhs,
                                         start=part == 0, stop=part == len(chunks) - 1, skip_group_check=True)
                    if part == len(chunks) - 1:
                        last.then_inc(av_done.sem, 1)

                def run(name, u):
                    b, l = batch(u), layer(u)
                    dst = job_bank(pe, name, u)
                    src = x_t[b] if l == 1 else ctx_t[b]
                    if name == "x":
                        pe.wait_ge(loaded[b], 16 * N_LOAD)
                        for t in range(QC):
                            last = pe.transpose(dst[:, t * P:(t + 1) * P], x_res[b][:, t, :], ident[:, :])
                        last.then_inc(xl_ready.sem, 1)
                    if name == "ctx":
                        pe.transpose(dst[:, 0:P], ctx_tok[b][:, 0, :], ident[:, :])
                        pe.transpose(dst[:, P:CTX], ctx_tok[b][0:TAIL, 1, :], ident[0:TAIL, 0:TAIL]).then_inc(xl_ready.sem, 1)
                    if name == "q":
                        if l == 0:
                            xl_kept.wait(pe, u, 3)
                        else:
                            xt_kept.wait(pe, u - B, 1)
                        pe.matmul(dst[:, :], w[:, 4 * l, :], x_t[b][:, :], start=True, stop=True).then_inc(qk_ready.sem, 1)
                    if name == "k":
                        n = keys(u)
                        pe.matmul(dst[:, 0:n], w[:, 4 * l + 1, :], src[:, 0:n], start=True, stop=True).then_inc(qk_ready.sem, 1)
                    if name == "v":
                        for t in range(QC if l == 1 else 2):
                            last = pe.matmul(dst[:, t * P:(t + 1) * P], src[:, t * P:(t + 1) * P], w[:, 4 * l + 2, :],
                                             start=True, stop=True)
                        last.then_inc(v_ready.sem, 1)
                    if name[0] == "T":
                        g = int(name[1])
                        o_kept.wait(pe, u, g + 1)
                        for t in range(QC):
                            last = pe.transpose(dst[:, t * P:(t + 1) * P], o_t[:, g, t * P:(t + 1) * P], ident[:, :])
                        last.then_inc(t_ready.sem, 1)
                    if name[:3] == "max":
                        half = int(name[3])
                        m_step.wait(pe, u, 4 * half + 4)
                        for t in range(QC):
                            last = pe.matmul(dst[0:PIECES * H // 2, t * P:(t + 1) * P],
                                             max_pieces[pair(u)][:, t, half, :, :].rearrange("p i h -> p (i h)"),
                                             ident16[:, :], start=True, stop=True)
                        last.then_inc(mt_ready.sem, 1)
                    if name == "oT":
                        t_taken.wait(pe, u, G)
                        for t in range(QC):
                            last = pe.transpose(dst[:, t * P:(t + 1) * P], o_tok[:, t, :], ident[:, :])
                        last.then_inc(ot_ready.sem, 1)
                    if name == "Y":
                        ot_kept.wait(pe, u, 1)
                        for t in range(QC):
                            last = pe.matmul(dst[:, t * P:(t + 1) * P], o_tt[:, t * P:(t + 1) * P], w[:, 4 * l + 3, :],
                                             start=True, stop=True)
                        last.then_inc(y_ready.sem, 1)
                    if name == "xT":
                        z_ready.wait(pe, u, QC)
                        for t in range(QC):
                            last = pe.transpose(dst[:, t * P:(t + 1) * P], z[:, t, :], ident[:, :])
                        last.then_inc(xt_ready.sem, 1)

                for name, u in prologue:
                    run(name, u)
                for k in range(SLOTS):
                    for h in range(H):
                        for n in range(len(B_ITEMS)):
                            if 0 <= k - 1 < UNITS:
                                scores_b(k - 1, h, n)
                            if k < UNITS:
                                scores_a(k, h, n)
                            times_v(k, h, n)
                        for name, u in steps(k, h):
                            if name in taken_by:
                                run(name, u)


E_PAR = 2
RING = 3
LEAD = 2
STEPS = E_PAR * QC * FC
BLOCKS = E_PAR * QC


def experts(nc, ins, xmid, out):
    ctx = ExitStack()
    with ctx:
        def sb(name, shape, dt=F32):
            return ctx.enter_context(nc.sbuf_tensor(name, shape, dt))

        def sem(name):
            return ctx.enter_context(nc.semaphore(name))

        pre = "L1_xattn_"
        ident = sb("ident_e", [P, P])
        acc = sb("acc", [P, T, P])
        x_t = sb("xe_t", [P, T, P])
        x_hi = sb("x_hi", [P, T * P], F32R)
        x_lo = sb("x_lo", [P, T * P], F32R)
        w1 = sb("w1", [P, E, FF])
        w2 = sb("w2", [P, E, FC, P])
        b1 = sb("b1", [P, E, FC])
        b2 = sb("b2", [P, E])
        router_w = sb("router_w", [P, E])
        router_b = sb("router_b", [P, E])
        gamma = sb("gamma", [P, P])
        beta = sb("beta", [P, P])
        w1_hi, w1_lo, w2_hi, w2_lo = ([sb(f"{n}{e}", [P, FF], F32R) for e in range(E_PAR)]
                                      for n in ("w1_hi", "w1_lo", "w2_hi", "w2_lo"))
        b1_e = [sb(f"b1_e{e}", [P, FC]) for e in range(E_PAR)]
        b2_e = [sb(f"b2_e{e}", [P, 1]) for e in range(E_PAR)]
        share_e = [sb(f"share_e{e}", [P, T]) for e in range(E_PAR)]
        hidden = sb("hidden", [P, RING, S])
        h_hi = sb("h_hi", [P, RING, S], F32R)
        h_lo = sb("h_lo", [P, RING, S], F32R)
        e_out = sb("e_out", [P, 2, S])
        logits = sb("logits", [P, T, E])
        top = sb("top", [P, T, 8])
        top_at = sb("top_at", [P, T, 8], U32)
        top_atf = sb("top_atf", [P, 2, T])
        row1 = sb("row1", [P, T])
        row2 = sb("row2", [P, T])
        weight = sb("weight", [P, 2, T])
        chosen = sb("chosen", [P, 2, E, T])
        share = sb("share", [P, E, T])
        minus_half = sb("minus_half_e", [P, T])
        stats = sb("stats_e", [P, T, 2, 3])
        sums = sb("sums_e", [P, T, 2])
        gap = sb("gap_e", [P, T])
        gap2 = sb("gap2_e", [P, T])
        within = sb("within_e", [P, T])
        mean = sb("mean_e", [P, T])
        var = sb("var_e", [P, T])
        rstd = sb("rstd_e", [P, T])
        z = x_t
        result = sb("result", [P, T, P])

        bank = [ctx.enter_context(nc.psum_tensor(f"e_bank{i}", [P, S], F32)) for i in range(8)]
        H_BANKS, O_BANKS, T_BANKS = (0, 1, 2, 3), (4, 5), (6, 7)

        s_x = sem("s_x")
        s_in = sem("s_in")
        s_id = sem("s_id")
        s_xt = sem("s_xt")
        s_xk = sem("s_xk")
        s_hi = sem("s_hi")
        s_log = sem("s_log")
        s_r = sem("s_r")
        s_exp = sem("s_exp")
        s_n = sem("s_n")
        s_rstd = sem("s_rstd")
        s_scaled = sem("s_scaled")
        s_result = sem("s_result")
        s_out = sem("s_out")
        split = sem("split")
        h_ready = sem("h_ready")
        h_kept = sem("h_kept")
        hi_ready = sem("hi_ready")
        lo_ready = sem("lo_ready")
        h_used = sem("h_used")
        o_kept = sem("o_kept_e")
        o_turned = sem("o_turned")
        o_added = sem("o_added")
        INPUTS = 8

        with nc.Block() as block:
            @block.sync
            def _(sp):
                for b in range(B):
                    sp.dma_start(acc[:, b * QC:(b + 1) * QC, :], xmid[b].rearrange("(t p) d -> p t d", p=P)).then_inc(s_x, 16)
                sp.dma_start(router_w[:, :], ins[pre + "router_w"]).then_inc(s_in, 16)
                for dst, n in ((router_b, "router_b"), (gamma, "ln3_g"), (beta, "ln3_b")):
                    v = ins[pre + n]
                    sp.dma_start(dst[:, :], v.rearrange("(o d) -> o d", o=1).to_broadcast([P, v.shape[0]])).then_inc(s_in, 16)
                sp.dma_start(w1[:, :, :], ins[pre + "e_w1"].rearrange("e d f -> d e f")).then_inc(s_in, 16)
                sp.dma_start(w2[:, :, :, :], ins[pre + "e_w2"].rearrange("e (c p) d -> p (e c) d", p=P)).then_inc(s_in, 16)
                with nc.allow_non_contiguous_dma(reason="biases, one per partition: small"):
                    sp.dma_start(b1[:, :, :], ins[pre + "e_b1"].rearrange("e (c p) -> p (e c)", p=P)).then_inc(s_in, 16)
                    sp.dma_start(b2[:, :], ins[pre + "e_b2"].rearrange("e d -> d e")).then_inc(s_in, 16)

            @block.gpsimd
            def _(pool):
                pool.memset(ident[:, :], 0.0).then_inc(s_id, 1)
                pool.memset(minus_half[:, :], -0.5).then_inc(s_id, 1)
                pool.wait_ge(s_id, 2)
                pool.affine_select(out=ident[:, :], in_=ident[:, :], compare_op=ALU.not_equal, fill=1.0, base=0,
                                   pattern=[[-1, P]], channel_multiplier=1).then_inc(s_id, 1)

            @block.tensor
            def _(pe):
                pe.wait_ge(s_id, 3)
                pe.wait_ge(s_x, 16 * B)
                for b in range(B):
                    for t in range(QC):
                        last = pe.transpose(bank[b][:, t * P:(t + 1) * P], acc[:, b * QC + t, :], ident[:, :])
                    last.then_inc(s_xt, 1)
                pe.wait_ge(s_in, 16 * INPUTS)
                pe.wait_ge(s_xk, B)
                for t in range(T):
                    last = pe.matmul(bank[4][:, t * E:(t + 1) * E], x_t[:, t, :], router_w[:, :], start=True, stop=True)
                last.then_inc(s_log, 1)

            @block.scalar
            def _(act):
                for b in range(B):
                    act.wait_ge(s_xt, b + 1)
                    act.copy(x_t[:, b * QC:(b + 1) * QC, :], bank[b][:, :].rearrange("p (t d) -> p t d", t=QC)).then_inc(s_xk, 1)
                act.wait_ge(s_r, 3)
                act.activation(logits[:, :, :], logits[:, :, :], ACT.Exp).then_inc(s_exp, 1)
                act.wait_ge(s_r, 6 + 2 * T + 3)
                act.activation(row2[:, :], row1[:, :], ACT.Exp).then_inc(s_exp, 1)

            @block.vector
            def _(dve):
                steps = [0]

                def done(ins_):
                    steps[0] += 1
                    ins_.then_inc(s_r, 1)
                    dve.wait_ge(s_r, steps[0])

                dve.wait_ge(s_xk, B)
                flat = x_t[:, :, :].rearrange("p t d -> p (t d)")
                dve.tensor_copy(x_hi[:, :], flat).then_inc(s_hi, 1)
                dve.wait_ge(s_hi, 1)
                dve.tensor_tensor(x_lo[:, :], flat, x_hi[:, :].bitcast(F32), ALU.subtract).then_inc(s_hi, 1)
                dve.wait_ge(s_log, 1)
                dve.wait_ge(s_in, 16 * INPUTS)
                done(dve.tensor_tensor(logits[:, :, :], bank[4][:, 0:T * E].rearrange("p (t e) -> p t e", e=E),
                                       router_b[:, :].rearrange("p (o e) -> p o e", o=1).to_broadcast([P, T, E]), ALU.add))
                done(dve.tensor_reduce(row1[:, :], logits[:, :, :], AX.X, ALU.max))
                r1 = row1[:, :].rearrange("p (t o) -> p t o", o=1).to_broadcast([P, T, E])
                done(dve.tensor_tensor(logits[:, :, :], logits[:, :, :], r1, ALU.subtract))
                dve.wait_ge(s_exp, 1)
                done(dve.tensor_reduce(row1[:, :], logits[:, :, :], AX.X, ALU.add))
                done(dve.reciprocal(row1[:, :], row1[:, :]))
                done(dve.tensor_tensor(logits[:, :, :], logits[:, :, :], r1, ALU.mult))
                for t in range(T):
                    dve.max(top[:, t, :], logits[:, t, :]).then_inc(s_r, 1)
                dve.wait_ge(s_r, 6 + T)
                for t in range(T):
                    dve.max_index(top_at[:, t, :], top[:, t, :], logits[:, t, :]).then_inc(s_r, 1)
                dve.wait_ge(s_r, 6 + 2 * T)
                steps[0] = 6 + 2 * T
                for i in range(2):
                    dve.tensor_copy(top_atf[:, i, :], top_at[:, :, i]).then_inc(s_r, 1)
                dve.tensor_tensor(row1[:, :], top[:, :, 1], top[:, :, 0], ALU.subtract).then_inc(s_r, 1)
                steps[0] += 3
                dve.wait_ge(s_exp, 2)
                done(dve.tensor_scalar(row1[:, :], row2[:, :], 1.0, None, ALU.add))
                done(dve.reciprocal(weight[:, 0, :], row1[:, :]))
                done(dve.tensor_tensor(weight[:, 1, :], row2[:, :], weight[:, 0, :], ALU.mult))
                for e in range(E):
                    for i in range(2):
                        dve.scalar_tensor_tensor(chosen[:, i, e, :], top_atf[:, i, :], float(e), weight[:, i, :],
                                                 ALU.is_equal, ALU.mult).then_inc(s_r, 1)
                        steps[0] += 1
                dve.wait_ge(s_r, steps[0])
                done(dve.tensor_tensor(share[:, :, :], chosen[:, 0, :, :], chosen[:, 1, :, :], ALU.add))

        with nc.Fori(0, E // E_PAR) as it:
            with nc.Block() as block:
                @block.vector
                def _(dve):
                    def split_weights(par):
                        e = it * E_PAR + par
                        at = split_weights.steps
                        raw1 = w1[:, bass.ds(e, 1), :].rearrange("p o f -> p (o f)")
                        raw2 = w2[:, bass.ds(e, 1), :, :].rearrange("p o c d -> p (o c d)")
                        dve.tensor_copy(w1_hi[par][:, :], raw1).then_inc(split, 1)
                        dve.tensor_copy(w2_hi[par][:, :], raw2).then_inc(split, 1)
                        dve.tensor_copy(b1_e[par][:, :], b1[:, bass.ds(e, 1), :].rearrange("p o c -> p (o c)")).then_inc(split, 1)
                        dve.tensor_copy(b2_e[par][:, :], b2[:, bass.ds(e, 1)]).then_inc(split, 1)
                        dve.tensor_copy(share_e[par][:, :], share[:, bass.ds(e, 1), :].rearrange("p o t -> p (o t)")).then_inc(split, 1)
                        dve.wait_ge(split, at + 5)
                        dve.tensor_tensor(w1_lo[par][:, :], raw1, w1_hi[par][:, :].bitcast(F32), ALU.subtract).then_inc(split, 1)
                        dve.tensor_tensor(w2_lo[par][:, :], raw2, w2_hi[par][:, :].bitcast(F32), ALU.subtract).then_inc(split, 1)
                        split_weights.steps += 7

                    split_weights.steps = 0

                    def add_block(q):
                        par, tb = q // QC, q % QC
                        dve.wait_ge(o_turned, q + 1)
                        if q >= QC:
                            dve.wait_ge(o_added, q - QC + 1)
                        for t in range(QC):
                            n = tb * QC + t
                            last = dve.scalar_tensor_tensor(acc[:, n, :], bank[T_BANKS[q % 2]][:, t * P:(t + 1) * P],
                                                            share_e[par][:, n:n + 1], acc[:, n, :], ALU.mult, ALU.add)
                        last.then_inc(o_added, 1)

                    split_weights(0)
                    for n in range(STEPS):
                        r = n % RING
                        dve.wait_ge(h_kept, n + 1)
                        if n >= RING:
                            dve.wait_ge(h_used, n - RING + 1)
                        dve.tensor_copy(h_hi[:, r, :], hidden[:, r, :]).then_inc(hi_ready, 1)
                        dve.wait_ge(hi_ready, n + 1)
                        dve.tensor_tensor(h_lo[:, r, :], hidden[:, r, :], h_hi[:, r, :].bitcast(F32), ALU.subtract)\
                           .then_inc(lo_ready, 1)
                        if n == FC:
                            for par in range(1, E_PAR):
                                split_weights(par)
                        if n % FC == 2 and n >= 2 * FC:
                            add_block(n // FC - 2)
                    add_block(BLOCKS - 2)
                    add_block(BLOCKS - 1)

                @block.scalar
                def _(act):
                    def keep_out(q):
                        act.wait_ge(h_used, FC * (q + 1))
                        if q >= 2:
                            act.wait_ge(o_turned, q - 1)
                        act.activation(e_out[:, q % 2, :], bank[O_BANKS[q % 2]][:, :], ACT.Identity,
                                       bias=b2_e[q // QC][:, 0:1]).then_inc(o_kept, 1)

                    for n in range(STEPS):
                        act.wait_ge(h_ready, n + 1)
                        if n % (QC * FC) == 0:
                            act.wait_ge(split, 7 * (n // (QC * FC)) + 5)
                        if n >= RING:
                            act.wait_ge(lo_ready, n - RING + 1)
                        act.activation(hidden[:, n % RING, :], bank[H_BANKS[n % 4]][:, :], ACT.Gelu,
                                       bias=b1_e[n // (QC * FC)][:, n % FC:n % FC + 1]).then_inc(h_kept, 1)
                        if n % FC == LEAD + 1 and n > FC:
                            keep_out(n // FC - 1)
                    keep_out(BLOCKS - 1)

                @block.tensor
                def _(pe):
                    def first_product(n):
                        par, tb, c = n // (QC * FC), n // FC % QC, n % FC
                        if n % (QC * FC) == 0:
                            pe.wait_ge(split, 7 * (par + 1))
                        if n >= 4:
                            pe.wait_ge(h_kept, n - 3)
                        dst = bank[H_BANKS[n % 4]][:, :]
                        f, x = slice(c * P, (c + 1) * P), slice(tb * S, (tb + 1) * S)
                        pe.matmul(dst, w1_hi[par][:, f], x_hi[:, x], start=True, stop=False)
                        pe.matmul(dst, w1_hi[par][:, f], x_lo[:, x], start=False, stop=False)
                        pe.matmul(dst, w1_lo[par][:, f], x_hi[:, x], start=False, stop=True).then_inc(h_ready, 1)

                    def second_product(n):
                        par, q, c, r = n // (QC * FC), n // FC, n % FC, n % RING
                        pe.wait_ge(lo_ready, n + 1)
                        if c == 0 and q >= 2:
                            pe.wait_ge(o_kept, q - 1)
                        dst = bank[O_BANKS[q % 2]][:, :]
                        f = slice(c * P, (c + 1) * P)
                        pe.matmul(dst, w2_hi[par][:, f], h_hi[:, r, :], start=c == 0, stop=False)
                        pe.matmul(dst, w2_lo[par][:, f], h_hi[:, r, :], start=False, stop=False)
                        last = pe.matmul(dst, w2_hi[par][:, f], h_lo[:, r, :], start=False, stop=c == FC - 1)
                        last.then_inc(h_used, 1)

                    def turn_out(q):
                        pe.wait_ge(o_kept, q + 1)
                        if q >= 2:
                            pe.wait_ge(o_added, q - 1)
                        for t in range(QC):
                            last = pe.transpose(bank[T_BANKS[q % 2]][:, t * P:(t + 1) * P],
                                                e_out[:, q % 2, t * P:(t + 1) * P], ident[:, :])
                        last.then_inc(o_turned, 1)

                    for n in range(STEPS + LEAD):
                        if n < STEPS:
                            first_product(n)
                        if n >= LEAD:
                            second_product(n - LEAD)
                            if (n - LEAD) % FC == 2 and n - LEAD > FC:
                                turn_out((n - LEAD) // FC - 1)
                    turn_out(BLOCKS - 1)

            nc.all_engine_barrier(sems_to_clear=range(split.num, o_added.num + 1))

        with nc.Block() as block:
            @block.vector
            def _(dve):
                for t in range(T):
                    dve.bn_stats(stats[:, t, :, :].rearrange("p a b -> p (a b)"), acc[:, t, :]).then_inc(s_n, 1)
                dve.wait_ge(s_n, T)
                dve.tensor_tensor(sums[:, :, :], stats[:, :, 0, 1:3], stats[:, :, 1, 1:3], ALU.add).then_inc(s_n, 1)
                dve.tensor_tensor(gap[:, :], stats[:, :, 0, 1], stats[:, :, 1, 1], ALU.subtract).then_inc(s_n, 1)
                dve.wait_ge(s_n, T + 2)
                dve.tensor_tensor(gap2[:, :], gap[:, :], gap[:, :], ALU.mult).then_inc(s_n, 1)
                dve.tensor_scalar(within[:, :], sums[:, :, 1], 1.0 / P, EPS, ALU.mult, ALU.add).then_inc(s_n, 1)
                dve.tensor_scalar(mean[:, :], sums[:, :, 0], 0.5, None, ALU.mult).then_inc(s_n, 1)
                dve.wait_ge(s_n, T + 5)
                dve.scalar_tensor_tensor(var[:, :], gap2[:, :], 0.25, within[:, :], ALU.mult, ALU.add).then_inc(s_n, 1)
                dve.wait_ge(s_rstd, 1)
                for t in range(T):
                    dve.tensor_scalar(z[:, t, :], acc[:, t, :], mean[:, t:t + 1], rstd[:, t:t + 1], ALU.subtract,
                                      ALU.mult).then_inc(s_n, 1)
                for b in range(B):
                    r = slice(b * QC, (b + 1) * QC)
                    g = gamma[:, :].rearrange("p (o d) -> p o d", o=1).to_broadcast([P, QC, P])
                    dve.wait_ge(s_n, T + 6 + (b + 1) * QC)
                    dve.tensor_tensor(z[:, r, :], z[:, r, :], g, ALU.mult).then_inc(s_scaled, 1)
                    dve.wait_ge(s_scaled, b + 1)
                    g = beta[:, :].rearrange("p (o d) -> p o d", o=1).to_broadcast([P, QC, P])
                    dve.tensor_tensor(result[:, r, :], z[:, r, :], g, ALU.add).then_inc(s_result, 1)

            @block.gpsimd
            def _(pool):
                pool.wait_ge(s_n, T + 6)
                pool.tensor_tensor(rstd[:, :], var[:, :], minus_half[:, :], ALU.pow).then_inc(s_rstd, 1)

            @block.sync
            def _(sp):
                for b in range(B):
                    sp.wait_ge(s_result, b + 1)
                    sp.dma_start(out[b].rearrange("(t p) d -> p t d", p=P), result[:, b * QC:(b + 1) * QC, :]).then_inc(s_out, 16)
                sp.wait_ge(s_out, 16 * B)


def build(nc, ins, out):
    xmid = nc.dram_tensor("x_mid", (B, S, P), F32, kind="Internal").ap()
    attention(nc, ins, out if DEBUG else xmid)
    if not DEBUG:
        experts(nc, ins, xmid, out)


DEBUG = False


def kernel(**inputs):
    import concourse.bacc as _bacc
    from concourse.bass_utils import run_bass_kernel_spmd as _run

    nc = _bacc.Bacc("TRN2", target_bir_lowering=False, num_devices=1)
    arrays, ins = {}, {}
    for name, a in inputs.items():
        a = np.ascontiguousarray(a)
        arrays[f"in_{name}"] = a
        ins[name] = nc.dram_tensor(f"in_{name}", a.shape, mybir.dt.from_np(a.dtype), kind="ExternalInput").ap()
    out = nc.dram_tensor("out", (B, S, P), F32, kind="ExternalOutput").ap()
    build(nc, ins, out)
    r = _run(nc, [arrays], core_ids=[0])
    return r.results[0]["out"]
```

```python
import numpy as np
from contextlib import ExitStack

import concourse.bass as bass
from concourse import mybir

F32 = mybir.dt.float32
F32R = mybir.dt.float32r
BF16 = mybir.dt.bfloat16
I32 = mybir.dt.int32
U32 = mybir.dt.uint32
ALU = mybir.AluOpType
ACT = mybir.ActivationFunctionType
AX = mybir.AxisListType

P = 128
B = 4
S = 512
QC = S // P
CTX = 154
H, HD = 16, 8
G = H // 4
PAIRS = G // 2
V_SHIFT = 16
E, FF = 8, 512
FC = FF // P
T = B * QC
TAIL = CTX - P
PAD = 32
KCTX = P + PAD
PIECES = 3
STACK = PIECES * PIECES * HD
MASK_ROW = STACK
MAX_ROW = STACK + 1
ROWS_A = STACK + 1
ROWS_B = STACK + 1 + PIECES
LOW = -1.0e38
EPS = 1e-5
SCALE = float(HD) ** -0.5

LAYERS = ("L0", "SELF", "CROSS")
NL = len(LAYERS)
UNITS = NL * B


class Count:

    def __init__(self, sem, per_layer):
        self.sem = sem
        self.before = [0]
        for u in range(UNITS):
            self.before.append(self.before[-1] + per_layer[u // B])

    def index(self, u, k):
        return self.before[u] + k

    def wait(self, eng, u, k):
        eng.wait_ge(self.sem, self.before[u] + k)


def a_items(layer):
    if layer == 1:
        return [[(0, 0, P), (1, P, 2 * P)], [(2, 0, 3 * P)], [(3, 0, 4 * P)]]
    return [[(0, 0, KCTX), (1, 256, KCTX)], [(2, 0, KCTX), (3, 256, KCTX)]]


B_ITEMS = [([(0, 0)], 4 * P), ([(1, 0), (3, 3 * P)], 4 * P), ([(2, 0)], 2 * P)]
P_AT = {0: 0, 1: 4 * P, 3: 7 * P, 2: 8 * P}
P_WIDE = 10 * P


class Kept:

    def __init__(self, nc, ctx):
        def sb(name, shape, dt=F32):
            return ctx.enter_context(nc.sbuf_tensor(name, shape, dt))

        self.ident = sb("ident", [P, P])
        self.minus_half = sb("minus_half", [P, T])
        self.x = [sb(f"x{b}", [P, QC, P]) for b in range(B)]
        self.x_t = [sb(f"x_t{b}", [P, S]) for b in range(B)]
        self.w1 = sb("w1", [P, E * FF])
        self.w2 = sb("w2", [P, E * FC * P])
        self.router_w = sb("router_w", [P, E])
        self.router_b = sb("router_b", [P, E])
        self.logits = sb("logits", [P, T, E])
        self.b1 = sb("b1", [P, E, FC])
        self.b2 = sb("b2", [P, E])
        self.gamma = sb("gamma", [P, P])
        self.beta = sb("beta", [P, P])
        self.s_small = ctx.enter_context(nc.semaphore("s_small"))
        self.s_weights = ctx.enter_context(nc.semaphore("s_weights"))


def attention(nc, ins, kept):
    ctx = ExitStack()
    with ctx:
        def sb(name, shape, dt=F32):
            return ctx.enter_context(nc.sbuf_tensor(name, shape, dt))

        def sem(name):
            return ctx.enter_context(nc.semaphore(name))

        def many(n, name, shape, dt=F32):
            return [sb(f"{name}{c}", shape, dt) for c in range(n)]

        ident, minus_half = kept.ident, kept.minus_half
        ident16 = sb("ident16", [P, P], BF16)
        causal_q = sb("causal_q", [P, P], BF16)
        causal_k = sb("causal_k", [P, P], BF16)
        w = sb("w", [P, 4 * NL, P])
        cols = sb("cols", [P, 5 * NL])
        bqs = sb("bqs", [P, NL])
        rows = sb("rows", [P, 3 * NL, P])
        beta_bo = sb("beta_bo", [P, NL - 1, P])
        mask_int = sb("mask_int", [1, B * CTX], I32)
        mask_rows = sb("mask_rows", [1, B + 1, KCTX], BF16)
        zero_row = sb("zero_row", [1, S], BF16)
        one_rows = sb("one_rows", [PIECES, S], BF16)

        x_res = kept.x
        x_t = kept.x_t
        ctx_t = many(B, "ctx_t", [P, P + 4 * PAD])
        pieces = many(2, "pieces", [P, 2, PIECES, S], BF16)
        q_stack = [kept.w1[:, :].bitcast(BF16).rearrange("p (h n) -> p h n", h=H), sb("q_stack", [P, H, S], BF16)]
        k_stack = [kept.w2[:, :].bitcast(BF16).rearrange("p (h n) -> p h n", h=H), sb("k_stack", [P, H, S], BF16)]
        v_aug = many(2, "v_aug", [P, QC + 1, H, PAD])
        neg_max = many(2, "neg_max", [P, QC, H])
        max_pieces = many(2, "max_pieces", [P, QC, 2, PIECES, H // 2], BF16)
        max_t = many(4, "max_t", [PIECES * H // 2, S], BF16)
        qk = sb("qk", [P, 2, S])
        rest = sb("rest", [P, 2, S])
        max_rest = sb("max_rest", [P, QC, H // 2])
        probs = sb("probs", [P, 8, P_WIDE])
        ctx_tok = [probs[:, b, 2 * S:2 * S + 2 * P].rearrange("p (t d) -> p t d", t=2) for b in range(B)]
        o_t = sb("o_t", [P, PAIRS, S])
        recip = sb("recip", [P, QC, 4, 2, 1])
        o_tok = sb("o_tok", [P, QC, P])
        o_tt = sb("o_tt", [P, S])
        y = sb("y", [P, QC, P])
        w_raw = y
        z = sb("z", [P, QC, P])
        stats = sb("stats", [P, QC, 2, 3])
        sums = sb("sums", [P, QC, 2])
        gap = sb("gap", [P, QC])
        gap2 = sb("gap2", [P, QC])
        within = sb("within", [P, QC])
        mean = sb("mean", [P, QC])
        var = sb("var", [P, QC])
        rstd = sb("rstd", [P, QC])

        bank = [ctx.enter_context(nc.psum_tensor(f"bank{i}", [P, S], F32)) for i in range(8)]
        A_BANKS, B_BANKS, AV_BANK, JOB_BANKS = (0, 1, 2), (3, 4, 6), 5, (7,)

        q_dram = [nc.dram_tensor(f"q_pieces{c}", (H, PIECES, HD, S), BF16, kind="Internal").ap() for c in range(2)]
        k_dram = [nc.dram_tensor(f"k_pieces{c}", (H, PIECES, HD, S), BF16, kind="Internal").ap() for c in range(2)]

        s_first = sem("s_first")
        s_bias = sem("s_bias")
        s_mask = sem("s_mask")
        s_rest = sem("s_rest")
        s_late = sem("s_late")
        s_made = sem("s_made")
        s_low = sem("s_low")
        s_beta = sem("s_beta")
        s_wt = sem("s_wt")
        s_w = sem("s_w")
        s_bq = sem("s_bq")
        s_rows = sem("s_rows")
        one = (1, 1, 1)
        n_a = tuple(H * len(a_items(l)) for l in range(NL))
        n_b = tuple(H * len(B_ITEMS) if l == 1 else H + G for l in range(NL))
        a_ready = Count(sem("a_ready"), n_a)
        a_taken = Count(sem("a_taken"), n_a)
        b_ready = Count(sem("b_ready"), n_b)
        p_ready = Count(sem("p_ready"), n_b)
        av_done = Count(sem("av_done"), (G,) * NL)
        o_kept = Count(sem("o_kept"), (PAIRS,) * NL)
        t_ready = Count(sem("t_ready"), (PAIRS,) * NL)
        t_recip = Count(sem("t_recip"), (PAIRS,) * NL)
        t_taken = Count(sem("t_taken"), (PAIRS,) * NL)
        m_step = Count(sem("m_step"), (8,) * NL)
        mt_ready = Count(sem("mt_ready"), (2,) * NL)
        mt_kept = Count(sem("mt_kept"), (2,) * NL)
        ot_ready = Count(sem("ot_ready"), one)
        ot_kept = Count(sem("ot_kept"), one)
        y_ready = Count(sem("y_ready"), one)
        y_step = Count(sem("y_step"), one)
        bn_step = Count(sem("bn_step"), (QC + 5,) * NL)
        var_eps = Count(sem("var_eps"), one)
        rstd_ready = Count(sem("rstd_ready"), one)
        z_ready = Count(sem("z_ready"), (QC,) * NL)
        xt_ready = Count(sem("xt_ready"), one)
        xt_kept = Count(sem("xt_kept"), one)
        x_scaled = Count(sem("x_scaled"), one)
        x_new = Count(sem("x_new"), one)
        r_ready = Count(sem("r_ready"), (0, 0, 1))
        r_taken = Count(sem("r_taken"), (0, 0, 1))
        x_bo = sem("x_bo")
        xl_ready = Count(sem("xl_ready"), (2, 0, 0))
        xl_kept = Count(sem("xl_kept"), (3, 0, 0))
        qk_ready = Count(sem("qk_ready"), (2,) * NL)
        qk_kept = Count(sem("qk_kept"), (4,) * NL)
        rest_step = Count(sem("rest_step"), (6,) * NL)
        v_ready = Count(sem("v_ready"), one)
        v_kept = Count(sem("v_kept"), one)
        loaded = [sem(f"loaded{b}") for b in range(B)]
        written = [sem(f"written{c}") for c in range(2)]
        stacked = [sem(f"stacked{c}") for c in range(4)]
        max_in = [sem(f"max_in{c}") for c in range(4)]
        N_LOAD, N_WRITE, N_STACK = 3, 2 * PIECES, PIECES * PIECES + PIECES + 1
        n_rest, n_late = 5, 3 * 4 * (NL - 1)

        names = [("L0_xattn_", ("Wq", "Wk", "Wv", "Wo"), "ln_gamma", "ln_beta"),
                 ("L1_xattn_", ("sa_wq", "sa_wk", "sa_wv", "sa_wo"), "ln1_g", "ln1_b"),
                 ("L1_xattn_", ("ca_wq", "ca_wk", "ca_wv", "ca_wo"), "ln2_g", "ln2_b")]

        def load_col(eng, l, i):
            pre, ws, gamma, beta = names[l]
            n = (ws[0], ws[1], ws[2], gamma, beta)[i]
            v = ins[pre + (n.replace("w", "b").replace("W", "b") if i < 3 else n)]
            return eng.dma_start(cols[:, 5 * l + i:5 * l + i + 1], v.rearrange("(p o) -> p o", o=1))

        def load_row(eng, l, i):
            pre, ws, gamma, beta = names[l]
            n = (ws[3], gamma, beta)[i]
            v = ins[pre + (n.replace("w", "b").replace("W", "b") if i < 1 else n)]
            return eng.dma_start(rows[:, 3 * l + i, :], v.rearrange("(o d) -> o d", o=1).to_broadcast([P, P]))

        def load_batch(eng, b):
            eng.dma_start(x_res[b][:, :, :], ins["x"][b].rearrange("(t p) d -> p t d", p=P)).then_inc(loaded[b], 16)
            eng.dma_start(ctx_tok[b][:, 0, :], ins["ctx_1024"][b, 0:P, :]).then_inc(loaded[b], 16)
            eng.dma_start(ctx_tok[b][0:TAIL, 1, :], ins["ctx_1024"][b, P:CTX, :]).then_inc(loaded[b], 16)

        def ones_at(g):
            return V_SHIFT * (g % 2) + HD

        def layer(u):
            return u // B

        def batch(u):
            return u % B

        def pair(u):
            return u % 2

        def dma_wait(eng, sems, u, n, half=None):
            at = pair(u) if half is None else 2 * pair(u) + half
            eng.wait_ge(sems[at], 16 * n * (u // 2 + 1))

        def keys(u):
            return S if layer(u) == 1 else KCTX

        taken_by = {"x": (xl_kept, 1), "ctx": (xl_kept, 3), "q": (qk_kept, 2), "k": (qk_kept, 4), "v": (v_kept, 1),
                    "max0": (mt_kept, 1), "max1": (mt_kept, 2), "oT": (ot_kept, 1), "Y": (y_step, 1),
                    "xT": (xt_kept, 1), "logits": (r_taken, 1), "T0": (t_taken, 1), "T1": (t_taken, 2)}
        SLOTS = UNITS + 2

        STEPS = [[("max1", 1)],
                 [("av1", 2), ("x", -1)],
                 [("ctx", -1), ("T1", 2)],
                 [("q", -1)],
                 [("k", -1), ("cut", -1)],
                 [("oT", 2)],
                 [],
                 [("Y", 2), ("cut max0", 0)],
                 [("max0", 0), ("stats", 2)],
                 [("av0", 1), ("var", 2)],
                 [("T0", 1)],
                 [("z", 2)],
                 [("v", 0)],
                 [("xT", 2)],
                 [],
                 [("cut max1", 0), ("logits", 2)]]

        def steps(k, h):
            todo = [(name, k - ago) for name, ago in STEPS[h] if 0 <= k - ago < UNITS]
            only = {"x": 0, "ctx": 0, "logits": NL - 1}
            return [(name, u) for name, u in todo if layer(u) == only.get(name, layer(u))]

        prologue = [("x", 0), ("ctx", 0), ("q", 0), ("k", 0)]
        all_jobs = prologue + [j for k in range(SLOTS) for h in range(H) for j in steps(k, h) if j[0] in taken_by]
        job_at = {j: i for i, j in enumerate(all_jobs)}

        def job(name, u):
            return bank[JOB_BANKS[job_at[name, u] % len(JOB_BANKS)]]

        def job_bank(pe, name, u):
            i = job_at[name, u]
            if i >= len(JOB_BANKS):
                before, v = all_jobs[i - len(JOB_BANKS)]
                count, n = taken_by[before]
                count.wait(pe, v, n)
            return job(name, u)

        with nc.Block() as block:
            @block.sync
            def _(sp):
                for i, n in enumerate(names[0][1]):
                    sp.dma_start(w_raw[:, i, :], ins[names[0][0] + n]).then_inc(s_first, 16)
                for i in range(3):
                    load_col(sp, 0, i).then_inc(s_bias, 16)
                sp.dma_start(mask_int[:, :], ins["mask_BxS2_ik0"].rearrange("(o b) s -> o (b s)", o=1)).then_inc(s_mask, 16)
                load_batch(sp, 0)
                sp.wait_ge(s_low, 4)
                for c in range(2):
                    src = one_rows[:, :].rearrange("p (o n) -> p o n", o=1)
                    sp.dma_start(q_stack[c][MASK_ROW:MASK_ROW + 1, :, :], src[0:1].to_broadcast([1, H, S])).then_inc(s_rows, 16)
                    sp.dma_start(k_stack[c][MAX_ROW:MAX_ROW + PIECES, :, :], src.to_broadcast([PIECES, H, S])).then_inc(s_rows, 16)

            @block.gpsimd
            def _(pool):
                pool.memset(ident[:, :], 0.0).then_inc(s_made, 1)
                pool.memset(minus_half[:, :], -0.5).then_inc(s_made, 1)
                pool.memset(causal_q[:, :], 0.0).then_inc(s_made, 1)
                pool.memset(causal_k[:, :], 0.0).then_inc(s_made, 1)
                pool.wait_ge(s_made, 4)
                pool.affine_select(out=ident[:, :], in_=ident[:, :], compare_op=ALU.not_equal, fill=1.0, base=0,
                                   pattern=[[-1, P]], channel_multiplier=1).then_inc(s_made, 1)
                pool.affine_select(out=causal_q[:, :], in_=causal_q[:, :], compare_op=ALU.is_ge, fill=LOW, base=0,
                                   pattern=[[-1, P]], channel_multiplier=1).then_inc(s_made, 1)
                pool.affine_select(out=causal_k[:, :], in_=causal_k[:, :], compare_op=ALU.is_ge, fill=LOW, base=0,
                                   pattern=[[1, P]], channel_multiplier=-1).then_inc(s_made, 1)

            @block.vector
            def _(dve):
                dve.memset(one_rows[:, :], 1.0).then_inc(s_low, 1)
                dve.memset(zero_row[:, :], 0.0).then_inc(s_low, 1)
                dve.memset(mask_rows[:, :, :], 0.0).then_inc(s_low, 1)
                dve.wait_ge(s_low, 3)
                dve.memset(mask_rows[:, :, CTX:KCTX], LOW).then_inc(s_low, 1)
                for b in range(B):
                    dve.memset(ctx_t[b][:, :], 0.0).then_inc(s_low, 1)
                for c in range(2):
                    dve.memset(v_aug[c][:, :, :, :], 0.0).then_inc(s_low, 1)
                dve.wait_ge(s_made, 5)
                dve.tensor_copy(ident16[:, :], ident[:, :]).then_inc(s_low, 1)
                dve.wait_ge(s_low, 11)
                for c in range(2):
                    for g in range(G):
                        dve.memset(v_aug[c][:, 0:QC, 4 * g:4 * (g + 1), ones_at(g):ones_at(g) + 1], 1.0)
                    for j in range(4):
                        for g in range(2):
                            dve.memset(v_aug[c][PAD * j:PAD * (j + 1), QC, 4 * g + j:H:8, ones_at(g):ones_at(g) + 1], 1.0)
                dve.wait_ge(s_mask, 16)
                dve.tensor_scalar(mask_rows[:, 0:B, 0:CTX], mask_int[:, :].rearrange("p (b s) -> p b s", b=B), 0.0, LOW,
                                  ALU.is_equal, ALU.mult).then_inc(s_low, 1)

            @block.scalar
            def _(act):
                act.wait_ge(s_bias, 16 * 3)
                act.mul(bqs[:, 0:1], cols[:, 0:1], SCALE).then_inc(s_bq, 1)
                act.wait_ge(s_wt, 1)
                act.copy(w[:, 0:4, :], bank[0][:, :].rearrange("p (i d) -> p i d", i=4)).then_inc(s_w, 1)

            @block.tensor
            def _(pe):
                pe.wait_ge(s_made, 5)
                pe.wait_ge(s_first, 16 * 4)
                for i in range(4):
                    last = pe.transpose(bank[0][:, i * P:(i + 1) * P], w_raw[:, i, :], ident[:, :])
                last.then_inc(s_wt, 1)

        with nc.Block() as block:
            @block.sync
            def _(sp):
                def write(u):
                    c = pair(u)
                    qk_kept.wait(sp, u, 4)
                    rest_step.wait(sp, u, 6)
                    for t, (dram, n) in enumerate(((q_dram[c], S), (k_dram[c], keys(u)))):
                        for i in range(PIECES):
                            sp.dma_start(dram[:, i, :, 0:n], pieces[c][:, t, i, 0:n]).then_inc(written[c], 16)

                def stack(u, half):
                    c, n_k = pair(u), keys(u)
                    hs = slice(half * H // 2, (half + 1) * H // 2)
                    if half == 0:
                        dma_wait(sp, written, u, N_WRITE)
                    if u >= 2:
                        a_ready.wait(sp, u - 2, n_a[layer(u - 2)])
                        b_ready.wait(sp, u - 2, (half + 1) * n_b[layer(u - 2)] // 2)
                    done = stacked[2 * c + half]
                    for i in range(PIECES):
                        at = PIECES * HD * i
                        for j in range(PIECES):
                            sp.dma_start(q_stack[c][at + HD * j:at + HD * (j + 1), hs, :],
                                         q_dram[c][hs, i, :, :].rearrange("h e n -> e h n")).then_inc(done, 16)
                        sp.dma_start(k_stack[c][at:at + PIECES * HD, hs, 0:n_k],
                                     k_dram[c][hs, :, :, 0:n_k].rearrange("h j e n -> (j e) h n")).then_inc(done, 16)
                    src = zero_row[:, :] if layer(u) == 1 else mask_rows[:, batch(u) if layer(u) == 0 else B, :]
                    src = src.rearrange("p (o n) -> p o n", o=1).to_broadcast([1, H // 2, n_k])
                    sp.dma_start(k_stack[c][MASK_ROW:MASK_ROW + 1, hs, 0:n_k], src).then_inc(done, 16)

                def max_rows(u, half):
                    c = 2 * pair(u) + half
                    mt_kept.wait(sp, u, half + 1)
                    sp.dma_start(q_stack[pair(u)][MAX_ROW:MAX_ROW + PIECES, half * H // 2:(half + 1) * H // 2, :],
                                 max_t[c][:, :]).then_inc(max_in[c], 16)

                sp.wait_ge(s_rows, 16 * 4)
                load_batch(sp, 1)
                write(0)
                for i in range(3):
                    load_row(sp, 0, i).then_inc(s_rest, 16)
                stack(0, 0)
                stack(0, 1)
                for i in (3, 4):
                    load_col(sp, 0, i).then_inc(s_rest, 16)
                for b in range(2, B):
                    load_batch(sp, b)
                pre = "L1_xattn_"
                sp.dma_start(kept.router_w[:, :], ins[pre + "router_w"]).then_inc(kept.s_small, 16)
                for dst, n in ((kept.router_b, "router_b"), (kept.gamma, "ln3_g"), (kept.beta, "ln3_b")):
                    v = ins[pre + n]
                    sp.dma_start(dst[:, :], v.rearrange("(o d) -> o d", o=1).to_broadcast([P, v.shape[0]])).then_inc(kept.s_small, 16)
                with nc.allow_non_contiguous_dma(reason="biases, one per partition: small"):
                    sp.dma_start(kept.b1[:, :, :], ins[pre + "e_b1"].rearrange("e (c p) -> p (e c)", p=P)).then_inc(kept.s_small, 16)
                    sp.dma_start(kept.b2[:, :], ins[pre + "e_b2"].rearrange("e d -> d e")).then_inc(kept.s_small, 16)
                for u in range(UNITS):
                    if u + 1 < UNITS:
                        write(u + 1)
                    max_rows(u, 0)
                    if u + 1 < UNITS:
                        stack(u + 1, 0)
                        stack(u + 1, 1)
                    max_rows(u, 1)
                a_ready.wait(sp, UNITS - 2, n_a[NL - 1])
                b_ready.wait(sp, UNITS - 2, n_b[NL - 1])
                sp.dma_start(kept.w1[:, :].rearrange("d (e f) -> d e f", e=E), ins[pre + "e_w1"].rearrange("e d f -> d e f"))\
                  .then_inc(kept.s_weights, 16)
                sp.dma_start(kept.w2[:, :].rearrange("p (c d) -> p c d", d=P), ins[pre + "e_w2"].rearrange("e (c p) d -> p (e c) d", p=P))\
                  .then_inc(kept.s_weights, 16)

            @block.gpsimd
            def _(pool):
                def over_tiles(row):
                    return row.to_broadcast([P, QC, P])

                def norm(u):
                    x, l = x_res[batch(u)], layer(u)
                    var_eps.wait(pool, u, 1)
                    pool.tensor_tensor(rstd[:, :], var[:, :], minus_half[:, 0:QC], ALU.pow).then_inc(rstd_ready.sem, 1)
                    z_ready.wait(pool, u, QC)
                    pool.tensor_tensor(x[:, :, :], z[:, :, :], over_tiles(rows[:, 3 * l + 1:3 * l + 2, :]), ALU.mult)\
                        .then_inc(x_scaled.sem, 1)
                    x_scaled.wait(pool, u, 1)
                    plus = beta_bo[:, l:l + 1, :] if l + 1 < NL else rows[:, 3 * l + 2:3 * l + 3, :]
                    pool.tensor_tensor(x[:, :, :], x[:, :, :], over_tiles(plus), ALU.add).then_inc(x_new.sem, 1)

                for l in range(1, NL):
                    for i, n in enumerate(names[l][1]):
                        pool.dma_start(w[:, 4 * l + i, :], ins[names[l][0] + n]).then_inc(s_late, 16)
                    for i in range(5):
                        load_col(pool, l, i).then_inc(s_late, 16)
                    for i in range(3):
                        load_row(pool, l, i).then_inc(s_late, 16)
                pool.wait_ge(s_rest, 16 * n_rest)
                for b in range(B):
                    pool.wait_ge(loaded[b], 16 * N_LOAD)
                    xl_ready.wait(pool, b, 1)
                    pool.tensor_tensor(x_res[b][:, :, :], x_res[b][:, :, :], over_tiles(rows[:, 0:1, :]), ALU.add)\
                        .then_inc(x_bo, 1)
                pool.wait_ge(s_late, 16 * n_late)
                for l in range(NL - 1):
                    pool.tensor_tensor(beta_bo[:, l, :], rows[:, 3 * l + 2, :], rows[:, 3 * l + 3, :], ALU.add).then_inc(s_beta, 1)
                pool.wait_ge(s_beta, NL - 1)
                for u in range(UNITS):
                    norm(u)

            @block.scalar
            def _(act):
                def inputs(u):
                    b = batch(u)
                    xl_ready.wait(act, u, 1)
                    act.copy(x_t[b][:, :], job("x", u)[:, :]).then_inc(xl_kept.sem, 1)
                    xl_ready.wait(act, u, 2)
                    src = job("ctx", u)
                    act.copy(ctx_t[b][:, 0:P], src[:, 0:P]).then_inc(xl_kept.sem, 1)
                    tail = src[:, P:CTX].rearrange("p (o n) -> p o n", o=1).to_broadcast([P, 4, TAIL])
                    act.copy(ctx_t[b][:, P:P + 4 * PAD].rearrange("p (j n) -> p j n", j=4)[:, :, 0:TAIL], tail)\
                       .then_inc(xl_kept.sem, 1)

                def project(u, t):
                    c, l = pair(u), layer(u)
                    if u == B and t == 0:
                        act.wait_ge(s_late, 16 * n_late)
                        for later in range(1, NL):
                            act.mul(bqs[:, later:later + 1], cols[:, 5 * later:5 * later + 1], SCALE).then_inc(s_bq, 1)
                        act.wait_ge(s_bq, NL)
                    if t == 0:
                        if u >= 1:
                            rest_step.wait(act, u - 1, 6)
                        if u >= 2:
                            dma_wait(act, written, u - 2, N_WRITE)
                    name, n, bias, scale = (("q", S, bqs[:, l:l + 1], SCALE), ("k", keys(u), cols[:, 5 * l + 1:5 * l + 2], 1.0))[t]
                    src = job(name, u)
                    qk_ready.wait(act, u, t + 1)
                    act.activation(qk[:, t, 0:n], src[:, 0:n], ACT.Identity, bias=bias, scale=scale).then_inc(qk_kept.sem, 1)
                    act.activation(pieces[c][:, t, 0, 0:n], src[:, 0:n], ACT.Identity, bias=bias, scale=scale)\
                       .then_inc(qk_kept.sem, 1)

                def exps(u, h, i, n, at):
                    b_ready.wait(act, u, i + 1)
                    if u * G + h // 4 >= 2:
                        act.wait_ge(av_done.sem, u * G + h // 4 - 1)
                    act.activation(probs[:, h % 8, at:at + n], bank[B_BANKS[b_ready.index(u, i) % len(B_BANKS)]][:, 0:n], ACT.Exp)\
                       .then_inc(p_ready.sem, 1)

                def head_exps(u, h):
                    if layer(u) == 1:
                        at = 0
                        for n, (_, wide) in enumerate(B_ITEMS):
                            exps(u, h, len(B_ITEMS) * h + n, wide, at)
                            at += wide
                        return
                    i = (h // 4) * 5 + h % 4
                    exps(u, h, i, S, 0)
                    if h % 4 == 3:
                        exps(u, h - 3, i + 1, S, S)

                def keep_o(u, m):
                    av_done.wait(act, u, 2 * (m + 1))
                    if u >= 1:
                        t_ready.wait(act, u - 1, m + 1)
                    act.copy(o_t[:, m, :], bank[AV_BANK][:, :]).then_inc(o_kept.sem, 1)

                def keep_output(u):
                    ot_ready.wait(act, u, 1)
                    if u >= 1:
                        y_ready.wait(act, u - 1, 1)
                    l = layer(u)
                    act.activation(o_tt[:, :], job("oT", u)[:, :], ACT.Identity, bias=cols[:, 5 * l + 2:5 * l + 3])\
                       .then_inc(ot_kept.sem, 1)

                def keep_v(u):
                    c, l = pair(u), layer(u)
                    v_ready.wait(act, u, 1)
                    if u >= 2:
                        av_done.wait(act, u - 2, G)
                    v = job("v", u)[:, :].rearrange("p (t h e) -> p t h e", t=QC, h=H)
                    for g in range(2):
                        at = slice(V_SHIFT * g, V_SHIFT * g + HD)
                        if l != 1:
                            for j in range(4):
                                r = slice(PAD * j, PAD * (j + 1))
                                act.copy(v_aug[c][r, QC, 4 * g + j:H:8, at], v[r, 1, 4 * g + j:H:8, :])
                        n_t = QC if l == 1 else 1
                        src = job("v", u)[:, 0:n_t * P].rearrange("p (m g j e) -> p m g j e", g=2, j=4, e=HD)[:, :, g, :, :]
                        dst = v_aug[c][:, 0:n_t, :, at].rearrange("p t (m g j) e -> p (t m) g j e", g=2, j=4)[:, :, g, :, :]
                        last = act.copy(dst, src)
                    last.then_inc(v_kept.sem, 1)

                def keep_x(u):
                    l = layer(u)
                    if u == 0:
                        act.wait_ge(s_rest, 16 * n_rest)
                    xt_ready.wait(act, u, 1)
                    act.activation(x_t[batch(u)][:, :], job("xT", u)[:, :], ACT.Identity, bias=cols[:, 5 * l + 4:5 * l + 5],
                                   scale=cols[:, 5 * l + 3:5 * l + 4]).then_inc(xt_kept.sem, 1)

                inputs(0)
                project(0, 0)
                project(0, 1)
                for k in range(SLOTS):
                    for h in range(H):
                        if 0 <= k - 1 < UNITS:
                            head_exps(k - 1, h)
                        for name, u in steps(k, h):
                            if name == "x":
                                inputs(u)
                            if name in ("q", "k"):
                                project(u, ("q", "k").index(name))
                            if name[:2] == "av":
                                keep_o(u, int(name[2]))
                            if name == "oT":
                                keep_output(u)
                            if name == "v":
                                keep_v(u)
                            if name == "xT":
                                keep_x(u)

            @block.vector
            def _(dve):
                def cut(u):
                    c = pair(u)
                    for t, n in ((0, S), (1, keys(u))):
                        qk_kept.wait(dve, u, 2 * t + 2)
                        p = pieces[c][:, t, :, 0:n]
                        dve.tensor_tensor(rest[:, t, 0:n], qk[:, t, 0:n], p[:, 0, :], ALU.subtract).then_inc(rest_step.sem, 1)
                        rest_step.wait(dve, u, 3 * t + 1)
                        dve.tensor_copy(p[:, 1, :], rest[:, t, 0:n]).then_inc(rest_step.sem, 1)
                        rest_step.wait(dve, u, 3 * t + 2)
                        dve.tensor_tensor(p[:, 2, :], rest[:, t, 0:n], p[:, 1, :], ALU.subtract).then_inc(rest_step.sem, 1)

                def maxima(u, h):
                    c, l = pair(u), layer(u)
                    items = a_items(l)
                    for n, item in enumerate(items):
                        i = len(items) * h + n
                        src = bank[A_BANKS[a_ready.index(u, i) % len(A_BANKS)]]
                        a_ready.wait(dve, u, i + 1)
                        if l == 1:
                            for q, at, n_k in item:
                                last = dve.tensor_reduce(neg_max[c][:, q, h:h + 1], src[:, at:at + n_k], AX.X, ALU.max,
                                                         negate=True)
                        else:
                            q = item[0][0]
                            last = dve.tensor_reduce(neg_max[c][:, q:q + 2, h:h + 1],
                                                     src[:, :].rearrange("p (t n) -> p t n", t=2)[:, :, 0:KCTX],
                                                     AX.X, ALU.max, negate=True)
                        last.then_inc(a_taken.sem, 1)

                def cut_max(u, half):
                    m = neg_max[pair(u)][:, :, half * H // 2:(half + 1) * H // 2]
                    pc = max_pieces[pair(u)][:, :, half, :, :]
                    a_taken.wait(dve, u, (half + 1) * n_a[layer(u)] // 2)
                    dve.tensor_copy(pc[:, :, 0, :], m).then_inc(m_step.sem, 1)
                    m_step.wait(dve, u, 4 * half + 1)
                    dve.tensor_tensor(max_rest[:, :, :], m, pc[:, :, 0, :], ALU.subtract).then_inc(m_step.sem, 1)
                    m_step.wait(dve, u, 4 * half + 2)
                    dve.tensor_copy(pc[:, :, 1, :], max_rest[:, :, :]).then_inc(m_step.sem, 1)
                    m_step.wait(dve, u, 4 * half + 3)
                    dve.tensor_tensor(pc[:, :, 2, :], max_rest[:, :, :], pc[:, :, 1, :], ALU.subtract).then_inc(m_step.sem, 1)

                def keep_max(u, half):
                    mt_ready.wait(dve, u, half + 1)
                    if u >= 2:
                        dma_wait(dve, max_in, u - 2, 1, half)
                    dve.tensor_copy(max_t[2 * pair(u) + half][:, :], job(f"max{half}", u)[0:PIECES * H // 2, :])\
                       .then_inc(mt_kept.sem, 1)

                def normalise(u, m):
                    t = job(f"T{m}", u)[:, :].rearrange("p (t j g e) -> p t j g e", t=QC, j=4, g=2)
                    t_ready.wait(dve, u, m + 1)
                    if u * PAIRS + m >= 1:
                        dve.wait_ge(t_taken.sem, u * PAIRS + m)
                    dve.reciprocal(recip[:, :, :, :, :].rearrange("p t j g o -> p (t j g) o"),
                                   t.rearrange("p t j g e -> p (t j g) e")[:, :, HD:HD + 1]).then_inc(t_recip.sem, 1)
                    t_recip.wait(dve, u, m + 1)
                    if m == 0 and u >= 1:
                        ot_ready.wait(dve, u - 1, 1)
                    for g in range(2):
                        h = 8 * m + 4 * g
                        out = o_tok[:, :, HD * h:HD * (h + 4)].rearrange("p t (j e) -> p t j e", j=4)
                        last = dve.tensor_tensor(out, t[:, :, :, g, 0:HD],
                                                 recip[:, :, :, g, :].to_broadcast([P, QC, 4, HD]), ALU.mult)
                    last.then_inc(t_taken.sem, 1)

                def residual(u):
                    y_ready.wait(dve, u, 1)
                    if layer(u) == 0:
                        dve.wait_ge(x_bo, u + 1)
                    else:
                        x_new.wait(dve, u - B, 1)
                    dve.tensor_tensor(y[:, :, :], job("Y", u)[:, :].rearrange("p (t d) -> p t d", t=QC),
                                      x_res[batch(u)][:, :, :], ALU.add).then_inc(y_step.sem, 1)

                def statistics(u):
                    y_step.wait(dve, u, 1)
                    for t in range(QC):
                        dve.bn_stats(stats[:, t, :, :].rearrange("p a b -> p (a b)"), y[:, t, :]).then_inc(bn_step.sem, 1)

                def variance(u):
                    bn_step.wait(dve, u, QC)
                    dve.tensor_tensor(sums[:, :, :], stats[:, :, 0, 1:3], stats[:, :, 1, 1:3], ALU.add).then_inc(bn_step.sem, 1)
                    dve.tensor_tensor(gap[:, :], stats[:, :, 0, 1], stats[:, :, 1, 1], ALU.subtract).then_inc(bn_step.sem, 1)
                    bn_step.wait(dve, u, QC + 2)
                    dve.tensor_tensor(gap2[:, :], gap[:, :], gap[:, :], ALU.mult).then_inc(bn_step.sem, 1)
                    dve.tensor_scalar(within[:, :], sums[:, :, 1], 1.0 / P, EPS, ALU.mult, ALU.add).then_inc(bn_step.sem, 1)
                    dve.tensor_scalar(mean[:, :], sums[:, :, 0], 0.5, None, ALU.mult).then_inc(bn_step.sem, 1)
                    bn_step.wait(dve, u, QC + 5)
                    if u >= 1:
                        rstd_ready.wait(dve, u - 1, 1)
                    dve.scalar_tensor_tensor(var[:, :], gap2[:, :], 0.25, within[:, :], ALU.mult, ALU.add).then_inc(var_eps.sem, 1)

                def standardise(u):
                    rstd_ready.wait(dve, u, 1)
                    if u >= 1:
                        x_scaled.wait(dve, u - 1, 1)
                        xt_ready.wait(dve, u - 1, 1)
                    for t in range(QC):
                        dve.tensor_scalar(z[:, t, :], y[:, t, :], mean[:, t:t + 1], rstd[:, t:t + 1], ALU.subtract,
                                          ALU.mult).then_inc(z_ready.sem, 1)

                def keep_logits(u):
                    if u == UNITS - B:
                        dve.wait_ge(kept.s_small, 16 * 6)
                    r_ready.wait(dve, u, 1)
                    bias = kept.router_b[:, :].rearrange("p (o e) -> p o e", o=1).to_broadcast([P, QC, E])
                    dve.tensor_tensor(kept.logits[:, QC * batch(u):QC * (batch(u) + 1), :],
                                      job("logits", u)[:, 0:QC * E].rearrange("p (t e) -> p t e", t=QC), bias, ALU.add)\
                       .then_inc(r_taken.sem, 1)

                cut(0)
                for k in range(SLOTS):
                    for h in range(H):
                        if k < UNITS:
                            maxima(k, h)
                        for name, u in steps(k, h):
                            if name == "cut":
                                cut(u)
                            if name[:7] == "cut max":
                                cut_max(u, int(name[7]))
                            if name[:3] == "max":
                                keep_max(u, int(name[3]))
                            if name[0] == "T":
                                normalise(u, int(name[1]))
                            if name == "Y":
                                residual(u)
                            if name == "stats":
                                statistics(u)
                            if name == "var":
                                variance(u)
                            if name == "z":
                                standardise(u)
                            if name == "logits":
                                keep_logits(u)

            @block.tensor
            def _(pe):
                def scores_a(u, h, n):
                    c, l = pair(u), layer(u)
                    if h % (H // 2) == 0 and n == 0:
                        dma_wait(pe, stacked, u, N_STACK, h // (H // 2))
                    items = a_items(l)
                    if n >= len(items):
                        return
                    idx = a_ready.index(u, len(items) * h + n)
                    dst = bank[A_BANKS[idx % len(A_BANKS)]]
                    if idx >= len(A_BANKS):
                        pe.wait_ge(a_taken.sem, idx - len(A_BANKS) + 1)
                    for q, at, n_k in items[n]:
                        last = pe.matmul(dst[:, at:at + n_k], q_stack[c][0:ROWS_A, h, q * P:(q + 1) * P],
                                         k_stack[c][0:ROWS_A, h, 0:n_k], start=True, stop=l != 1,
                                         skip_group_check=True)
                        if l == 1:
                            last = pe.matmul(dst[:, at + n_k - P:at + n_k], ident16[:, :], causal_q[:, :],
                                             start=False, stop=True, skip_group_check=True)
                    last.then_inc(a_ready.sem, 1)

                def score_bank(u, i):
                    idx = b_ready.index(u, i)
                    if idx >= len(B_BANKS):
                        pe.wait_ge(p_ready.sem, idx - len(B_BANKS) + 1)
                    return bank[B_BANKS[idx % len(B_BANKS)]]

                def scores_b(u, h, n):
                    c, l = pair(u), layer(u)
                    if h % (H // 2) == 0 and n == 0:
                        dma_wait(pe, max_in, u, 1, h // (H // 2))
                    if l == 1:
                        dst = score_bank(u, len(B_ITEMS) * h + n)
                        for kc, at in B_ITEMS[n][0]:
                            pe.matmul(dst[:, at:at + S - P * kc], k_stack[c][0:ROWS_B, h, kc * P:(kc + 1) * P],
                                      q_stack[c][0:ROWS_B, h, kc * P:S], start=True, stop=False,
                                      skip_group_check=True)
                            last = pe.matmul(dst[:, at:at + P], ident16[:, :], causal_k[:, :], start=False, stop=True,
                                             skip_group_check=True)
                        last.then_inc(b_ready.sem, 1)
                    i = (h // 4) * 5 + h % 4
                    if l != 1 and n == 0:
                        dst = score_bank(u, i)
                        pe.matmul(dst[:, :], k_stack[c][0:ROWS_B, h, 0:P], q_stack[c][0:ROWS_B, h, :], start=True, stop=True)\
                          .then_inc(b_ready.sem, 1)
                    if l != 1 and n == 1 and h % 4 == 3:
                        dst = score_bank(u, i + 1)
                        for j in range(4):
                            last = pe.matmul(dst[PAD * j:PAD * (j + 1), :], k_stack[c][0:ROWS_B, h - 3 + j, P:KCTX],
                                             q_stack[c][0:ROWS_B, h - 3 + j, :], start=True, stop=True)
                        last.then_inc(b_ready.sem, 1)

                def times_v(k, h, n):
                    u, g = (k - 1, h // 4 - 1) if h >= 4 else (k - 2, G - 1)
                    if h % 4 > 1 or not 0 <= u < UNITS:
                        return
                    c, l = pair(u), layer(u)
                    places, chunks = ((2, 3, 4, 5), range(QC)) if l == 1 else ((2, 4), (0, QC))
                    if 3 * (h % 4) + n not in places:
                        return
                    part = places.index(3 * (h % 4) + n)
                    kc = chunks[part]
                    if part == 0:
                        if g == 0:
                            v_kept.wait(pe, u, 1)
                        p_ready.wait(pe, u, (g + 1) * n_b[l] // G)
                        if g % 2 == 0 and u + g >= 1:
                            pe.wait_ge(o_kept.sem, u * PAIRS + g // 2)
                    for j in range(4):
                        head = 4 * g + j
                        q0 = P * kc if l == 1 else 0
                        if kc == QC:
                            rhs = probs[:, (4 * g) % 8, S:2 * S]
                        else:
                            rhs = probs[:, head % 8, P_AT[kc]:P_AT[kc] + S - q0]
                        last = pe.matmul(bank[AV_BANK][PAD * j:PAD * (j + 1), q0:S], v_aug[c][:, kc, head, :], rhs,
                                         start=part == 0 and g % 2 == 0,
                                         stop=part == len(chunks) - 1 and g % 2 == 1, skip_group_check=True)
                    if part == len(chunks) - 1:
                        last.then_inc(av_done.sem, 1)

                def run(name, u):
                    b, l = batch(u), layer(u)
                    dst = job_bank(pe, name, u)
                    src = x_t[b] if l == 1 else ctx_t[b]
                    if name == "x":
                        pe.wait_ge(loaded[b], 16 * N_LOAD)
                        for t in range(QC):
                            last = pe.transpose(dst[:, t * P:(t + 1) * P], x_res[b][:, t, :], ident[:, :])
                        last.then_inc(xl_ready.sem, 1)
                    if name == "ctx":
                        pe.transpose(dst[:, 0:P], ctx_tok[b][:, 0, :], ident[:, :])
                        pe.transpose(dst[:, P:CTX], ctx_tok[b][0:TAIL, 1, :], ident[0:TAIL, 0:TAIL]).then_inc(xl_ready.sem, 1)
                    if name == "q":
                        if l == 0:
                            xl_kept.wait(pe, u, 3)
                        else:
                            xt_kept.wait(pe, u - B, 1)
                            if u == B:
                                pe.wait_ge(s_late, 16 * n_late)
                        pe.matmul(dst[:, :], w[:, 4 * l, :], x_t[b][:, :], start=True, stop=True).then_inc(qk_ready.sem, 1)
                    if name == "k":
                        n = keys(u)
                        pe.matmul(dst[:, 0:n], w[:, 4 * l + 1, :], src[:, 0:n], start=True, stop=True).then_inc(qk_ready.sem, 1)
                    if name == "v":
                        for t in range(QC if l == 1 else 2):
                            last = pe.matmul(dst[:, t * P:(t + 1) * P], src[:, t * P:(t + 1) * P], w[:, 4 * l + 2, :],
                                             start=True, stop=True)
                        last.then_inc(v_ready.sem, 1)
                    if name[0] == "T":
                        m = int(name[1])
                        o_kept.wait(pe, u, m + 1)
                        for t in range(QC):
                            last = pe.transpose(dst[:, t * P:(t + 1) * P], o_t[:, m, t * P:(t + 1) * P], ident[:, :])
                        last.then_inc(t_ready.sem, 1)
                    if name[:3] == "max":
                        half = int(name[3])
                        m_step.wait(pe, u, 4 * half + 4)
                        for t in range(QC):
                            last = pe.matmul(dst[0:PIECES * H // 2, t * P:(t + 1) * P],
                                             max_pieces[pair(u)][:, t, half, :, :].rearrange("p i h -> p (i h)"),
                                             ident16[:, :], start=True, stop=True)
                        last.then_inc(mt_ready.sem, 1)
                    if name == "oT":
                        t_taken.wait(pe, u, PAIRS)
                        for t in range(QC):
                            last = pe.transpose(dst[:, t * P:(t + 1) * P], o_tok[:, t, :], ident[:, :])
                        last.then_inc(ot_ready.sem, 1)
                    if name == "Y":
                        ot_kept.wait(pe, u, 1)
                        for t in range(QC):
                            last = pe.matmul(dst[:, t * P:(t + 1) * P], o_tt[:, t * P:(t + 1) * P], w[:, 4 * l + 3, :],
                                             start=True, stop=True)
                        last.then_inc(y_ready.sem, 1)
                    if name == "xT":
                        z_ready.wait(pe, u, QC)
                        for t in range(QC):
                            last = pe.transpose(dst[:, t * P:(t + 1) * P], z[:, t, :], ident[:, :])
                        last.then_inc(xt_ready.sem, 1)

                    if name == "logits":
                        if u == UNITS - B:
                            pe.wait_ge(kept.s_small, 16 * 6)
                        xt_kept.wait(pe, u, 1)
                        for t in range(QC):
                            last = pe.matmul(dst[:, t * E:(t + 1) * E], x_t[b][:, t * P:(t + 1) * P], kept.router_w[:, :],
                                             start=True, stop=True)
                        last.then_inc(r_ready.sem, 1)

                for name, u in prologue:
                    run(name, u)
                for k in range(SLOTS):
                    for h in range(H):
                        for n in range(len(B_ITEMS)):
                            if 0 <= k - 1 < UNITS:
                                scores_b(k - 1, h, n)
                            if k < UNITS:
                                scores_a(k, h, n)
                            times_v(k, h, n)
                        for name, u in steps(k, h):
                            if name in taken_by:
                                run(name, u)


E_PAR = 4
RING = 4
LEAD = 3
STEPS = E_PAR * QC * FC
BLOCKS = E_PAR * QC


def experts(nc, ins, kept, out):
    ctx = ExitStack()
    with ctx:
        def sb(name, shape, dt=F32):
            return ctx.enter_context(nc.sbuf_tensor(name, shape, dt))

        def sem(name):
            return ctx.enter_context(nc.semaphore(name))

        ident, minus_half = kept.ident, kept.minus_half
        x, x_t = kept.x, kept.x_t
        x_hi = sb("x_hi", [P, T * P], F32R)
        x_lo = sb("x_lo", [P, T * P], F32R)
        w1 = kept.w1[:, :].rearrange("p (e f) -> p e f", e=E)
        w2 = kept.w2[:, :].rearrange("p (e f) -> p e f", e=E)
        b1, b2, gamma, beta, logits = kept.b1, kept.b2, kept.gamma, kept.beta, kept.logits
        w1_hi, w1_lo, w2_hi, w2_lo = ([sb(f"{n}{e}", [P, FF], F32R) for e in range(E_PAR)]
                                      for n in ("w1_hi", "w1_lo", "w2_hi", "w2_lo"))
        b1_e = [sb(f"b1_e{e}", [P, FC]) for e in range(E_PAR)]
        b2_e = [sb(f"b2_e{e}", [P, 1]) for e in range(E_PAR)]
        share_e = [sb(f"share_e{e}", [P, T]) for e in range(E_PAR)]
        hidden = sb("hidden", [P, RING, S])
        h_hi = sb("h_hi", [P, RING, S], F32R)
        h_lo = sb("h_lo", [P, RING, S], F32R)
        e_out = sb("e_out", [P, 2, S])
        top = sb("top", [P, T, 8])
        top_at = sb("top_at", [P, T, 8], U32)
        top_atf = sb("top_atf", [P, 2, T])
        row1 = sb("row1", [P, T])
        row2 = sb("row2", [P, T])
        weight = sb("weight", [P, 2, T])
        chosen = sb("chosen", [P, 2, E, T])
        share = sb("share", [P, E, T])
        stats = sb("stats_e", [P, T, 2, 3])
        sums = sb("sums_e", [P, T, 2])
        gap = sb("gap_e", [P, T])
        gap2 = sb("gap2_e", [P, T])
        within = sb("within_e", [P, T])
        mean = sb("mean_e", [P, T])
        var = sb("var_e", [P, T])
        rstd = sb("rstd_e", [P, T])
        result = [sb(f"result{b}", [P, QC, P]) for b in range(B)]

        bank = [ctx.enter_context(nc.psum_tensor(f"e_bank{i}", [P, S], F32)) for i in range(8)]
        H_BANKS, O_BANKS, T_BANKS = (0, 1, 2, 3), (4, 5), (6, 7)

        s_hi = sem("s_hi")
        s_lo = sem("s_lo")
        s_r = sem("s_r")
        s_exp = sem("s_exp")
        s_n = sem("s_n")
        s_rstd = sem("s_rstd")
        s_scaled = sem("s_scaled")
        s_result = sem("s_result")
        s_out = sem("s_out")
        split = sem("split")
        h_ready = sem("h_ready")
        hi_ready = sem("hi_ready")
        lo_ready = sem("lo_ready")
        h_used = sem("h_used")
        o_kept = sem("o_kept_e")
        o_turned = sem("o_turned")
        o_added = sem("o_added")

        with nc.Block() as block:
            @block.scalar
            def _(act):
                for b in range(B):
                    act.copy(x_hi[:, b * S:(b + 1) * S], x_t[b][:, :]).then_inc(s_hi, 1)
                act.wait_ge(s_r, 2)
                act.activation(logits[:, :, :], logits[:, :, :], ACT.Exp).then_inc(s_exp, 1)
                act.wait_ge(s_r, 5 + 2 * T + 3)
                act.activation(row2[:, :], row1[:, :], ACT.Exp).then_inc(s_exp, 1)

            @block.vector
            def _(dve):
                steps = [0]

                def done(ins_):
                    steps[0] += 1
                    ins_.then_inc(s_r, 1)
                    dve.wait_ge(s_r, steps[0])

                for b in range(B):
                    dve.wait_ge(s_hi, b + 1)
                    at = slice(b * S, (b + 1) * S)
                    dve.tensor_tensor(x_lo[:, at], x_t[b][:, :], x_hi[:, at].bitcast(F32), ALU.subtract).then_inc(s_lo, 1)
                done(dve.tensor_reduce(row1[:, :], logits[:, :, :], AX.X, ALU.max))
                r1 = row1[:, :].rearrange("p (t o) -> p t o", o=1).to_broadcast([P, T, E])
                done(dve.tensor_tensor(logits[:, :, :], logits[:, :, :], r1, ALU.subtract))
                dve.wait_ge(s_exp, 1)
                done(dve.tensor_reduce(row1[:, :], logits[:, :, :], AX.X, ALU.add))
                done(dve.reciprocal(row1[:, :], row1[:, :]))
                done(dve.tensor_tensor(logits[:, :, :], logits[:, :, :], r1, ALU.mult))
                for t in range(T):
                    dve.max(top[:, t, :], logits[:, t, :]).then_inc(s_r, 1)
                dve.wait_ge(s_r, 5 + T)
                for t in range(T):
                    dve.max_index(top_at[:, t, :], top[:, t, :], logits[:, t, :]).then_inc(s_r, 1)
                dve.wait_ge(s_r, 5 + 2 * T)
                steps[0] = 5 + 2 * T
                for i in range(2):
                    dve.tensor_copy(top_atf[:, i, :], top_at[:, :, i]).then_inc(s_r, 1)
                dve.tensor_tensor(row1[:, :], top[:, :, 1], top[:, :, 0], ALU.subtract).then_inc(s_r, 1)
                steps[0] += 3
                dve.wait_ge(s_exp, 2)
                done(dve.tensor_scalar(row1[:, :], row2[:, :], 1.0, None, ALU.add))
                done(dve.reciprocal(weight[:, 0, :], row1[:, :]))
                done(dve.tensor_tensor(weight[:, 1, :], row2[:, :], weight[:, 0, :], ALU.mult))
                for e in range(E):
                    for i in range(2):
                        dve.scalar_tensor_tensor(chosen[:, i, e, :], top_atf[:, i, :], float(e), weight[:, i, :],
                                                 ALU.is_equal, ALU.mult).then_inc(s_r, 1)
                        steps[0] += 1
                dve.wait_ge(s_r, steps[0])
                done(dve.tensor_tensor(share[:, :, :], chosen[:, 0, :, :], chosen[:, 1, :, :], ALU.add))

        with nc.Fori(0, E // E_PAR) as it:
            with nc.Block() as block:
                @block.vector
                def _(dve):
                    def split_weights(par):
                        e = it * E_PAR + par
                        at = 7 * par
                        raw1 = w1[:, bass.ds(e, 1), :].rearrange("p o f -> p (o f)")
                        raw2 = w2[:, bass.ds(e, 1), :].rearrange("p o f -> p (o f)")
                        dve.tensor_copy(w1_hi[par][:, :], raw1).then_inc(split, 1)
                        dve.tensor_copy(w2_hi[par][:, :], raw2).then_inc(split, 1)
                        dve.tensor_copy(b1_e[par][:, :], b1[:, bass.ds(e, 1), :].rearrange("p o c -> p (o c)")).then_inc(split, 1)
                        dve.tensor_copy(b2_e[par][:, :], b2[:, bass.ds(e, 1)]).then_inc(split, 1)
                        dve.tensor_copy(share_e[par][:, :], share[:, bass.ds(e, 1), :].rearrange("p o t -> p (o t)")).then_inc(split, 1)
                        dve.wait_ge(split, at + 5)
                        dve.tensor_tensor(w1_lo[par][:, :], raw1, w1_hi[par][:, :].bitcast(F32), ALU.subtract).then_inc(split, 1)
                        dve.tensor_tensor(w2_lo[par][:, :], raw2, w2_hi[par][:, :].bitcast(F32), ALU.subtract).then_inc(split, 1)

                    dve.wait_ge(kept.s_weights, 16 * 2)

                    def add_block(q):
                        par, tb = q // QC, q % QC
                        dve.wait_ge(o_turned, q + 1)
                        if q >= QC:
                            dve.wait_ge(o_added, q - QC + 1)
                        for t in range(QC):
                            n = tb * QC + t
                            last = dve.scalar_tensor_tensor(x[tb][:, t, :], bank[T_BANKS[q % 2]][:, t * P:(t + 1) * P],
                                                            share_e[par][:, n:n + 1], x[tb][:, t, :], ALU.mult, ALU.add)
                        last.then_inc(o_added, 1)

                    split_weights(0)
                    for n in range(STEPS):
                        r = n % RING
                        dve.wait_ge(hi_ready, 2 * (n + 1))
                        if n >= RING:
                            dve.wait_ge(h_used, n - RING + 1)
                        dve.tensor_tensor(h_lo[:, r, :], hidden[:, r, :], h_hi[:, r, :].bitcast(F32), ALU.subtract)\
                           .then_inc(lo_ready, 1)
                        if n % (QC * FC) == FC and n // (QC * FC) + 1 < E_PAR:
                            split_weights(n // (QC * FC) + 1)
                        if n % FC == 2 and n >= 2 * FC:
                            add_block(n // FC - 2)
                    add_block(BLOCKS - 2)
                    add_block(BLOCKS - 1)

                @block.scalar
                def _(act):
                    def keep_out(q):
                        act.wait_ge(h_used, FC * (q + 1))
                        if q >= 2:
                            act.wait_ge(o_turned, q - 1)
                        act.activation(e_out[:, q % 2, :], bank[O_BANKS[q % 2]][:, :], ACT.Identity,
                                       bias=b2_e[q // QC][:, 0:1]).then_inc(o_kept, 1)

                    for n in range(STEPS):
                        act.wait_ge(h_ready, n + 1)
                        if n % (QC * FC) == 0:
                            act.wait_ge(split, 7 * (n // (QC * FC)) + 5)
                        if n >= RING:
                            act.wait_ge(lo_ready, n - RING + 1)
                            act.wait_ge(h_used, n - RING + 1)
                        hid, bias = bank[H_BANKS[n % 4]][:, :], b1_e[n // (QC * FC)][:, n % FC:n % FC + 1]
                        act.activation(hidden[:, n % RING, :], hid, ACT.Gelu, bias=bias).then_inc(hi_ready, 1)
                        act.activation(h_hi[:, n % RING, :], hid, ACT.Gelu, bias=bias).then_inc(hi_ready, 1)
                        if n % FC == FC - 1 and n > FC:
                            keep_out(n // FC - 1)
                    keep_out(BLOCKS - 1)

                @block.tensor
                def _(pe):
                    def first_product(n):
                        par, tb, c = n // (QC * FC), n // FC % QC, n % FC
                        if n % (QC * FC) == 0:
                            pe.wait_ge(split, 7 * (par + 1))
                        if n >= 4:
                            pe.wait_ge(hi_ready, 2 * (n - 3))
                        dst = bank[H_BANKS[n % 4]][:, :]
                        f, x = slice(c * P, (c + 1) * P), slice(tb * S, (tb + 1) * S)
                        pe.matmul(dst, w1_hi[par][:, f], x_hi[:, x], start=True, stop=False)
                        pe.matmul(dst, w1_hi[par][:, f], x_lo[:, x], start=False, stop=False)
                        pe.matmul(dst, w1_lo[par][:, f], x_hi[:, x], start=False, stop=True).then_inc(h_ready, 1)

                    def second_product(n):
                        par, q, c, r = n // (QC * FC), n // FC, n % FC, n % RING
                        pe.wait_ge(lo_ready, n + 1)
                        if c == 0 and q >= 2:
                            pe.wait_ge(o_kept, q - 1)
                        dst = bank[O_BANKS[q % 2]][:, :]
                        f = slice(c * P, (c + 1) * P)
                        pe.matmul(dst, w2_hi[par][:, f], h_hi[:, r, :], start=c == 0, stop=False)
                        pe.matmul(dst, w2_lo[par][:, f], h_hi[:, r, :], start=False, stop=False)
                        last = pe.matmul(dst, w2_hi[par][:, f], h_lo[:, r, :], start=False, stop=c == FC - 1)
                        last.then_inc(h_used, 1)

                    def turn_out(q):
                        pe.wait_ge(o_kept, q + 1)
                        if q >= 2:
                            pe.wait_ge(o_added, q - 1)
                        for t in range(QC):
                            last = pe.transpose(bank[T_BANKS[q % 2]][:, t * P:(t + 1) * P],
                                                e_out[:, q % 2, t * P:(t + 1) * P], ident[:, :])
                        last.then_inc(o_turned, 1)

                    for n in range(STEPS + LEAD):
                        if n < STEPS:
                            first_product(n)
                        if n >= LEAD:
                            second_product(n - LEAD)
                            if (n - LEAD) % FC == 2 and n - LEAD > FC:
                                turn_out((n - LEAD) // FC - 1)
                    turn_out(BLOCKS - 1)

            nc.all_engine_barrier(sems_to_clear=range(split.num, o_added.num + 1))

        with nc.Block() as block:
            @block.vector
            def _(dve):
                for t in range(T):
                    dve.bn_stats(stats[:, t, :, :].rearrange("p a b -> p (a b)"), x[t // QC][:, t % QC, :]).then_inc(s_n, 1)
                dve.wait_ge(s_n, T)
                dve.tensor_tensor(sums[:, :, :], stats[:, :, 0, 1:3], stats[:, :, 1, 1:3], ALU.add).then_inc(s_n, 1)
                dve.tensor_tensor(gap[:, :], stats[:, :, 0, 1], stats[:, :, 1, 1], ALU.subtract).then_inc(s_n, 1)
                dve.wait_ge(s_n, T + 2)
                dve.tensor_tensor(gap2[:, :], gap[:, :], gap[:, :], ALU.mult).then_inc(s_n, 1)
                dve.tensor_scalar(within[:, :], sums[:, :, 1], 1.0 / P, EPS, ALU.mult, ALU.add).then_inc(s_n, 1)
                dve.tensor_scalar(mean[:, :], sums[:, :, 0], 0.5, None, ALU.mult).then_inc(s_n, 1)
                dve.wait_ge(s_n, T + 5)
                dve.scalar_tensor_tensor(var[:, :], gap2[:, :], 0.25, within[:, :], ALU.mult, ALU.add).then_inc(s_n, 1)
                dve.wait_ge(s_rstd, 1)
                for t in range(T):
                    dve.tensor_scalar(x[t // QC][:, t % QC, :], x[t // QC][:, t % QC, :], mean[:, t:t + 1], rstd[:, t:t + 1], ALU.subtract,
                                      ALU.mult).then_inc(s_n, 1)
                for b in range(B):
                    g = gamma[:, :].rearrange("p (o d) -> p o d", o=1).to_broadcast([P, QC, P])
                    dve.wait_ge(s_n, T + 6 + (b + 1) * QC)
                    dve.tensor_tensor(x[b][:, :, :], x[b][:, :, :], g, ALU.mult).then_inc(s_scaled, 1)
                    dve.wait_ge(s_scaled, b + 1)
                    g = beta[:, :].rearrange("p (o d) -> p o d", o=1).to_broadcast([P, QC, P])
                    dve.tensor_tensor(result[b][:, :, :], x[b][:, :, :], g, ALU.add).then_inc(s_result, 1)

            @block.gpsimd
            def _(pool):
                pool.wait_ge(s_n, T + 6)
                pool.tensor_tensor(rstd[:, :], var[:, :], minus_half[:, :], ALU.pow).then_inc(s_rstd, 1)

            @block.sync
            def _(sp):
                for b in range(B):
                    sp.wait_ge(s_result, b + 1)
                    sp.dma_start(out[b].rearrange("(t p) d -> p t d", p=P), result[b][:, :, :]).then_inc(s_out, 16)
                sp.wait_ge(s_out, 16 * B)


def build(nc, ins, out):
    with ExitStack() as ctx:
        kept = Kept(nc, ctx)
        attention(nc, ins, kept)
        experts(nc, ins, kept, out)


def kernel(**inputs):
    import concourse.bacc as _bacc
    from concourse.bass_utils import run_bass_kernel_spmd as _run

    nc = _bacc.Bacc("TRN2", target_bir_lowering=False, num_devices=1)
    arrays, ins = {}, {}
    for name, a in inputs.items():
        a = np.ascontiguousarray(a)
        arrays[f"in_{name}"] = a
        ins[name] = nc.dram_tensor(f"in_{name}", a.shape, mybir.dt.from_np(a.dtype), kind="ExternalInput").ap()
    out = nc.dram_tensor("out", (B, S, P), F32, kind="ExternalOutput").ap()
    build(nc, ins, out)
    r = _run(nc, [arrays], core_ids=[0])
    return r.results[0]["out"]
```
